# Optimizing a Trainium2 kernel written in Bass

```python
import numpy as np
import jax
import jax.numpy as jnp

def _softmax(x, axis=-1):
    return jax.nn.softmax(x, axis=axis)

def _gelu(x):
    return jax.nn.gelu(x, approximate=True)

def _silu(x):
    return jax.nn.silu(x)

def _sigmoid(x):
    return jax.nn.sigmoid(x)

def _layernorm(x, axis=-1, eps=1e-05):
    m = jnp.mean(x, axis=axis, keepdims=True)
    v = jnp.var(x, axis=axis, keepdims=True)
    return (x - m) / jnp.sqrt(v + eps)

def _scatter_add(tgt, idx, src, axis=0):
    return tgt.at[idx].add(src)

def _segment_sum(src, seg, n):
    return jax.ops.segment_sum(src, seg, n)
kernel_name = 'mk_adj_ffn_d2_adj_r2_0356c4'

def setup_inputs(seed: int=0):
    np.random.seed(seed)
    _w = jnp.asarray

    def _rec_inputs():
        import jax
        import jax.numpy as jnp
        _gk = jax.random.key(seed)
        x = -0.0002928 + 1 * jax.random.normal(jax.random.fold_in(_gk, 1), (32, 256, 128), jnp.float32)
        _a = jax.random.bernoulli(jax.random.fold_in(_gk, 2), 0.0078125, (32, 256, 256))
        _a = jnp.logical_or(_a, jnp.swapaxes(_a, -1, -2))
        _a = jnp.logical_or(_a, jnp.eye(256, dtype=bool))
        _af = _a.astype(jnp.float32)
        _af = _af * jax.random.uniform(jax.random.fold_in(_gk, 3), (32, 256, 256), jnp.float32, 0.05, 1)
        adj = _af
        return (x, adj)
    x, adj = _rec_inputs()

    def _L0_gnn_setup():
        import jax, jax.numpy as jnp
        import numpy as np
        B, N, D, H = (8, 1024, 128, 512)
        RMS_EPS = 1e-06

        def _rmsnorm(h, w, eps=RMS_EPS):
            var = jnp.mean(jnp.square(h), axis=-1, keepdims=True)
            return h * jax.lax.rsqrt(var + eps) * w
        key = jax.random.key(seed)
        ks = jax.random.split(key, 5)
        x = jax.random.normal(ks[0], (B, N, D), dtype=jnp.float32)
        adjacency = jax.random.uniform(ks[1], (B, N, N), dtype=jnp.float32)
        epsilon = jnp.zeros((), dtype=jnp.float32)
        W1 = jax.random.normal(ks[2], (D, H), dtype=jnp.float32) * (1.0 / np.sqrt(D))
        b1 = jnp.zeros((H,), dtype=jnp.float32)
        rms_weight = jnp.ones((H,), dtype=jnp.float32)
        W2 = jax.random.normal(ks[3], (H, D), dtype=jnp.float32) * (1.0 / np.sqrt(H))
        b2 = jnp.zeros((D,), dtype=jnp.float32)
        return {'x': x, 'adjacency': adjacency, 'epsilon': epsilon, 'W1': W1, 'b1': b1, 'rms_weight': rms_weight, 'W2': W2, 'b2': b2}
    _L0_gnn_all = _L0_gnn_setup()
    _L0_gnn_in = {k: v for k, v in _L0_gnn_all.items() if k in ('epsilon', 'W1', 'b1', 'rms_weight', 'W2', 'b2')}
    del _L0_gnn_all

    def _L0_ffn_setup():
        import jax, jax.numpy as jnp
        import numpy as np
        B, T, IN_DIM = (64, 128, 128)
        HID, OUT_DIM = (256, 128)
        N_LAYERS, N_EXPERTS, N_SHARED = (2, 16, 1)
        key = jax.random.key(seed)
        ks = jax.random.split(key, 10)
        s = 0.02
        x = jax.random.normal(ks[0], (B, T, IN_DIM), dtype=jnp.float32)
        route_id = jax.random.randint(ks[1], (B,), 0, N_EXPERTS)
        Wi = jax.random.normal(ks[2], (HID, IN_DIM), dtype=jnp.float32) * s
        bi = jnp.zeros((HID,), dtype=jnp.float32)
        Wr = jax.random.normal(ks[3], (N_LAYERS, N_EXPERTS, HID, HID), dtype=jnp.float32) * s
        br = jax.random.normal(ks[4], (N_LAYERS, N_EXPERTS, HID), dtype=jnp.float32) * s
        Ws = jax.random.normal(ks[5], (N_LAYERS, N_SHARED, HID, HID), dtype=jnp.float32) * s
        bs = jax.random.normal(ks[6], (N_LAYERS, N_SHARED, HID), dtype=jnp.float32) * s
        Wo = jax.random.normal(ks[7], (OUT_DIM, HID), dtype=jnp.float32) * s
        bo = jnp.zeros((OUT_DIM,), dtype=jnp.float32)
        return {'x': x, 'route_id': route_id, 'Wi': Wi, 'bi': bi, 'Wr': Wr, 'br': br, 'Ws': Ws, 'bs': bs, 'Wo': Wo, 'bo': bo}
    _L0_ffn_all = _L0_ffn_setup()
    _L0_ffn_in = {k: v for k, v in _L0_ffn_all.items() if k in ('route_id', 'Wi', 'bi', 'Wr', 'br', 'Ws', 'bs', 'Wo', 'bo')}
    del _L0_ffn_all

    def _L1_gnn_setup():
        import jax, jax.numpy as jnp
        import numpy as np
        DIM = 128
        HEADS = 8
        BS = 8
        N = 512
        NEG = -1000000000.0
        key = jax.random.key(seed)
        ks = jax.random.split(key, 8)
        feats = jax.random.normal(ks[0], (BS, N, DIM), dtype=jnp.float32)
        adj_mat = (jax.random.uniform(ks[1], (BS, N, N)) < 0.1).astype(jnp.float32)
        s = 1.0 / np.sqrt(DIM)
        fc_w = jax.random.normal(ks[2], (DIM, DIM * HEADS), dtype=jnp.float32) * s
        fc_b = jnp.zeros((DIM * HEADS,), dtype=jnp.float32)
        q_w = jax.random.normal(ks[3], (DIM, 1), dtype=jnp.float32) * s
        q_b = jnp.zeros((1,), dtype=jnp.float32)
        k_w = jax.random.normal(ks[4], (DIM, 1), dtype=jnp.float32) * s
        k_b = jnp.zeros((1,), dtype=jnp.float32)
        fp_w = jax.random.normal(ks[5], (DIM * HEADS, DIM), dtype=jnp.float32) * (1.0 / np.sqrt(DIM * HEADS))
        fp_b = jnp.zeros((DIM,), dtype=jnp.float32)
        return {'feats': feats, 'adj_mat': adj_mat, 'fc_w': fc_w, 'fc_b': fc_b, 'q_w': q_w, 'q_b': q_b, 'k_w': k_w, 'k_b': k_b, 'fp_w': fp_w, 'fp_b': fp_b}
    _L1_gnn_all = _L1_gnn_setup()
    _L1_gnn_in = {k: v for k, v in _L1_gnn_all.items() if k in ('fc_w', 'fc_b', 'q_w', 'q_b', 'k_w', 'k_b', 'fp_w', 'fp_b')}
    del _L1_gnn_all

    def _L1_ffn_setup():
        import jax, jax.numpy as jnp
        import numpy as np
        B, S, D, F, E, K = (8, 1024, 128, 512, 8, 2)
        key = jax.random.key(seed)
        ks = jax.random.split(key, 10)
        s = 0.02
        return {'x': jax.random.normal(ks[0], (B, S, D), dtype=jnp.float32), 'Wr': jax.random.normal(ks[1], (D, E), dtype=jnp.float32) * s, 'W1s': jax.random.normal(ks[2], (D, F), dtype=jnp.float32) * s, 'b1s': jnp.zeros((F,), dtype=jnp.float32), 'W2s': jax.random.normal(ks[3], (F, D), dtype=jnp.float32) * s, 'b2s': jnp.zeros((D,), dtype=jnp.float32), 'W1p': jax.random.normal(ks[4], (E, D, F), dtype=jnp.float32) * s, 'b1p': jnp.zeros((E, F), dtype=jnp.float32), 'W2p': jax.random.normal(ks[5], (E, F, D), dtype=jnp.float32) * s, 'b2p': jnp.zeros((E, D), dtype=jnp.float32)}
    _L1_ffn_all = _L1_ffn_setup()
    _L1_ffn_in = {k: v for k, v in _L1_ffn_all.items() if k in ('Wr', 'W1s', 'b1s', 'W2s', 'b2s', 'W1p', 'b1p', 'W2p', 'b2p')}
    del _L1_ffn_all
    return {'x': x, 'adj': adj, 'L0_gnn_epsilon': _L0_gnn_in['epsilon'], 'L0_gnn_W1': _L0_gnn_in['W1'], 'L0_gnn_b1': _L0_gnn_in['b1'], 'L0_gnn_rms_weight': _L0_gnn_in['rms_weight'], 'L0_gnn_W2': _L0_gnn_in['W2'], 'L0_gnn_b2': _L0_gnn_in['b2'], 'L0_ffn_route_id': _L0_ffn_in['route_id'], 'L0_ffn_Wi': _L0_ffn_in['Wi'], 'L0_ffn_bi': _L0_ffn_in['bi'], 'L0_ffn_Wr': _L0_ffn_in['Wr'], 'L0_ffn_br': _L0_ffn_in['br'], 'L0_ffn_Ws': _L0_ffn_in['Ws'], 'L0_ffn_bs': _L0_ffn_in['bs'], 'L0_ffn_Wo': _L0_ffn_in['Wo'], 'L0_ffn_bo': _L0_ffn_in['bo'], 'L1_gnn_fc_w': _L1_gnn_in['fc_w'], 'L1_gnn_fc_b': _L1_gnn_in['fc_b'], 'L1_gnn_q_w': _L1_gnn_in['q_w'], 'L1_gnn_q_b': _L1_gnn_in['q_b'], 'L1_gnn_k_w': _L1_gnn_in['k_w'], 'L1_gnn_k_b': _L1_gnn_in['k_b'], 'L1_gnn_fp_w': _L1_gnn_in['fp_w'], 'L1_gnn_fp_b': _L1_gnn_in['fp_b'], 'L1_ffn_Wr': _L1_ffn_in['Wr'], 'L1_ffn_W1s': _L1_ffn_in['W1s'], 'L1_ffn_b1s': _L1_ffn_in['b1s'], 'L1_ffn_W2s': _L1_ffn_in['W2s'], 'L1_ffn_b2s': _L1_ffn_in['b2s'], 'L1_ffn_W1p': _L1_ffn_in['W1p'], 'L1_ffn_b1p': _L1_ffn_in['b1p'], 'L1_ffn_W2p': _L1_ffn_in['W2p'], 'L1_ffn_b2p': _L1_ffn_in['b2p']}

def reference(x, adj, L0_gnn_epsilon, L0_gnn_W1, L0_gnn_b1, L0_gnn_rms_weight, L0_gnn_W2, L0_gnn_b2, L0_ffn_route_id, L0_ffn_Wi, L0_ffn_bi, L0_ffn_Wr, L0_ffn_br, L0_ffn_Ws, L0_ffn_bs, L0_ffn_Wo, L0_ffn_bo, L1_gnn_fc_w, L1_gnn_fc_b, L1_gnn_q_w, L1_gnn_q_b, L1_gnn_k_w, L1_gnn_k_b, L1_gnn_fp_w, L1_gnn_fp_b, L1_ffn_Wr, L1_ffn_W1s, L1_ffn_b1s, L1_ffn_W2s, L1_ffn_b2s, L1_ffn_W1p, L1_ffn_b1p, L1_ffn_W2p, L1_ffn_b2p):
    import jax
    import jax.numpy as jnp

    def _L0_gnn_ref(x, adjacency, epsilon, W1, b1, rms_weight, W2, b2):
        import jax, jax.numpy as jnp
        import numpy as np
        B, N, D, H = (8, 1024, 128, 512)
        RMS_EPS = 1e-06

        def _rmsnorm(h, w, eps=RMS_EPS):
            var = jnp.mean(jnp.square(h), axis=-1, keepdims=True)
            return h * jax.lax.rsqrt(var + eps) * w
        neighbor_sum = jnp.einsum('bnm,bmd->bnd', adjacency, x)
        agg = epsilon * x + neighbor_sum
        h = jnp.einsum('bnd,dh->bnh', agg, W1) + b1
        h = jax.nn.silu(_rmsnorm(h, rms_weight))
        out = jnp.einsum('bnh,hd->bnd', h, W2) + b2
        return out

    def _L0_ffn_ref(x, route_id, Wi, bi, Wr, br, Ws, bs, Wo, bo):
        import jax, jax.numpy as jnp
        import numpy as np
        B, T, IN_DIM = (64, 128, 128)
        HID, OUT_DIM = (256, 128)
        N_LAYERS, N_EXPERTS, N_SHARED = (2, 16, 1)
        flat = x.reshape(-1, x.shape[-1])
        n_tok = flat.shape[0]
        route = jnp.repeat(route_id, n_tok // route_id.shape[0])
        h = jax.nn.relu(flat @ Wi.T + bi)
        n_layers, n_experts = (Wr.shape[0], Wr.shape[1])
        for l in range(n_layers):
            shared = (jnp.einsum('nd,shd->snh', h, Ws[l]) + bs[l][:, None, :]).mean(axis=0)
            routed = jnp.zeros_like(h)
            for e in range(n_experts):
                ye = h @ Wr[l, e].T + br[l, e]
                routed = routed + jnp.where((route == e)[:, None], ye, 0.0)
            h = jax.nn.relu(shared + routed + h)
        out = h @ Wo.T + bo
        return out.reshape(*x.shape[:-1], out.shape[-1])

    def _L1_gnn_ref(feats, adj_mat, fc_w, fc_b, q_w, q_b, k_w, k_b, fp_w, fp_b):
        import jax, jax.numpy as jnp
        import numpy as np
        DIM = 128
        HEADS = 8
        BS = 8
        N = 512
        NEG = -1000000000.0
        bs, n, dim = feats.shape
        feat_proj = (feats @ fc_w + fc_b).reshape(bs, n, HEADS, dim).transpose(0, 2, 1, 3)
        q = feat_proj @ q_w + q_b
        k = feat_proj @ k_w + k_b
        logits = q + jnp.swapaxes(k, -1, -2)
        masked = logits + (1.0 - adj_mat[:, None]) * NEG
        masked = jax.nn.leaky_relu(masked, negative_slope=0.01)
        attn = jax.nn.softmax(masked, axis=-1)
        out = attn @ feat_proj
        out = out.transpose(0, 2, 1, 3).reshape(bs, n, HEADS * dim)
        out = out @ fp_w + fp_b + feats
        return jax.nn.sigmoid(out)

    def _L1_ffn_ref(x, Wr, W1s, b1s, W2s, b2s, W1p, b1p, W2p, b2p):
        import jax, jax.numpy as jnp
        import numpy as np
        B, S, D, F, E, K = (8, 1024, 128, 512, 8, 2)
        gelu = lambda t: jax.nn.gelu(t, approximate=False)
        shared = gelu(x @ W1s + b1s) @ W2s + b2s
        rw = jax.nn.softmax(x @ Wr, axis=-1)
        topw, topi = jax.lax.top_k(rw, K)
        topw = topw / jnp.sum(topw, axis=-1, keepdims=True)
        mask = jnp.sum(jax.nn.one_hot(topi, E, dtype=topw.dtype) * topw[..., None], axis=-2)
        h = gelu(jnp.einsum('bsd,edf->bsef', x, W1p) + b1p)
        priv = jnp.einsum('bsef,efd->bsed', h, W2p) + b2p
        routed = jnp.einsum('bsed,bse->bsd', priv, mask)
        return shared + routed
    x = x + _L0_gnn_ref(_layernorm(x, axis=-1), adj, L0_gnn_epsilon, L0_gnn_W1, L0_gnn_b1, L0_gnn_rms_weight, L0_gnn_W2, L0_gnn_b2)
    x = x + _L0_ffn_ref(_layernorm(x, axis=-1), L0_ffn_route_id, L0_ffn_Wi, L0_ffn_bi, L0_ffn_Wr, L0_ffn_br, L0_ffn_Ws, L0_ffn_bs, L0_ffn_Wo, L0_ffn_bo)
    x = x + _L1_gnn_ref(_layernorm(x, axis=-1), adj, L1_gnn_fc_w, L1_gnn_fc_b, L1_gnn_q_w, L1_gnn_q_b, L1_gnn_k_w, L1_gnn_k_b, L1_gnn_fp_w, L1_gnn_fp_b)
    x = x + _L1_ffn_ref(_layernorm(x, axis=-1), L1_ffn_Wr, L1_ffn_W1s, L1_ffn_b1s, L1_ffn_W2s, L1_ffn_b2s, L1_ffn_W1p, L1_ffn_b1p, L1_ffn_W2p, L1_ffn_b2p)
    return x

_drawn_inputs = setup_inputs


def setup_inputs(seed=0):
    import zlib

    import numpy as np

    out = dict(_drawn_inputs(seed))
    spreads = {'L0_gnn_b1': (0.0, 0.1),
     'L0_gnn_rms_weight': (1.0, 0.2),
     'L0_gnn_b2': (0.0, 0.1),
     'L0_ffn_bi': (0.0, 0.407),
     'L0_ffn_bo': (0.0, 0.1),
     'L1_gnn_fc_b': (0.0, 0.55),
     'L1_gnn_fp_b': (0.0, 0.591),
     'L1_ffn_b1s': (0.0, 0.515),
     'L1_ffn_b2s': (0.0, 0.1),
     'L1_ffn_b1p': (0.0, 0.696),
     'L1_ffn_b2p': (0.0, 0.1)}
    factors = {'L0_ffn_Wr': 3.204, 'L0_ffn_br': 7.861, 'L0_ffn_Ws': 3.229, 'L0_ffn_bs': 7.973}
    for name, (base, spread) in spreads.items():
        noise = np.random.default_rng([zlib.crc32(name.encode()), seed]).standard_normal(out[name].shape)
        drawn = base * np.exp(spread * noise) if base else spread * noise
        out[name] = jnp.asarray(drawn.astype(out[name].dtype))
    for name, factor in factors.items():
        out[name] = (out[name] * factor).astype(out[name].dtype)
    return out
```

```python
from contextlib import ExitStack

import concourse.bass as bass
from concourse import mybir

F32 = mybir.dt.float32
I32 = mybir.dt.int32
ALU = mybir.AluOpType
ACT = mybir.ActivationFunctionType
AX = mybir.AxisListType

P = 128
GRAPHS = 32
TILES = 2
D = 128
NODES = P * TILES
LN_EPS = 1e-5
RMS_EPS = 1e-6


def pair(g):
    return g[0]


def par(g):
    return g[1]


def number(g):
    return 2 * g[0] + g[1]


def graph(i):
    return i // 2, i % 2


def count(g, each, k=None, back=0):
    n = each * (number(g) - back) + (each if k is None else k)
    return 0 if isinstance(n, int) and number(g) < back else n


def loads(g, back=0):
    return 16 * (pair(g) - back) + 16


def sweep(eng, depth, body, units=GRAPHS):
    first = (depth + 3) // 2 * 2

    def peeled(i):
        return lambda lag: graph(i - lag) if 0 <= i - lag < units else None

    for i in range(first):
        body(peeled(i))
    with eng.Fori(first // 2, units // 2) as j:
        for q in (0, 1):
            body(lambda lag: (j + (q - lag) // 2, (q - lag) % 2))
    for i in range(units, units + depth):
        body(peeled(i))


def one(ap):
    return ap.rearrange("p a d -> p (a d)")


def graph_rows(X, g):
    return one(X[:, bass.ds(pair(g), 1), par(g), :])


def transpose(nc, out, in_, ident):
    return nc.tensor.transpose(out, in_, ident)


def gnn0(nc, outer, X, ident, mhalf, lneps, rmseps, epsi, WC, WS, d):
    with ExitStack() as ctx:
        def sb(name, shape, dt=F32):
            return ctx.enter_context(nc.sbuf_tensor(name, shape, dt))

        def two(name, shape, dt=F32):
            return [sb(name + "0", shape, dt), sb(name + "1", shape, dt)]

        def bank(name):
            return ctx.enter_context(nc.psum_tensor(name, [P, 512], F32))

        def sem(name):
            return outer.enter_context(nc.semaphore(name))

        W1 = sb("a_W1", [P, 512])
        W2 = sb("a_W2", [P, 4, D])
        b1 = sb("a_b1", [P, 512])
        rmsw = sb("a_rmsw", [P, 512])
        b2 = sb("a_b2", [P, 2, D])
        AT = two("a_AT", [P, TILES, NODES])
        st = two("a_st", [P, TILES, 6])
        mv = two("a_mv", [P, TILES, 2])
        ve = two("a_ve", [P, TILES])
        rstd = two("a_rstd", [P, TILES])
        xln = two("a_xln", [P, TILES, D])
        aggT = two("a_aggT", [P, NODES])
        hb = two("a_hb", [P, TILES, 512])
        hn = two("a_hn", [P, TILES, 512])
        junk = two("a_junk", [P, TILES, 512])
        ssq = two("a_ssq", [P, TILES])
        ms = two("a_ms", [P, TILES])
        rr = two("a_rr", [P, TILES])
        hT = two("a_hT", [P, TILES, 4, P])
        tmp = two("a_tmp", [P, NODES])
        p_agg = bank("a_pagg")
        p_h = [bank("a_ph0"), bank("a_ph1")]
        p_t = [bank("a_pt0"), bank("a_pt1")]
        p_out = bank("a_pout")

        weights_in = sem("a_weights_in")
        rms_weight = sem("a_rms_weight")
        adj_in = [sem("a_adj_in0"), sem("a_adj_in1")]
        wr_in = [sem("a_wr_in0"), sem("a_wr_in1")]
        stats = sem("a_stats")
        scale = sem("a_scale")
        normed = sem("a_normed")
        self_loop = sem("a_self_loop")
        wr_sum = sem("a_wr_sum")
        agg = sem("a_agg")
        agg_sb = sem("a_agg_sb")
        hidden = sem("a_hidden")
        biased = sem("a_biased")
        squares = sem("a_squares")
        rms = sem("a_rms")
        scaled = sem("a_scaled")
        silu = sem("a_silu")
        turned = sem("a_turned")
        turned_sb = sem("a_turned_sb")
        product = sem("a_product")
        added = sem("a_added")

        adjT = d["adjT"].rearrange("(j b) p c n -> j b p c n", b=2)
        wr = d["WrT"].rearrange("p l e n -> l p e n")
        weight_dmas = 5

        with nc.Block() as block:
            @block.sync
            def _(sp):
                sp.dma_start(W1[:, :], d["a_W1"]).then_inc(weights_in, 16)
                sp.dma_start(W2[:, :, :], d["a_W2"].rearrange("(f p) n -> p f n", p=P)).then_inc(weights_in, 16)
                sp.dma_start(b1[:, :], d["a_b1"].partition_broadcast(P)).then_inc(weights_in, 16)
                sp.dma_start(rmsw[:, :], d["a_rmsw"].partition_broadcast(P)).then_inc(weights_in, 16)
                sp.dma_start(b2[:, :, :], d["a_b2x2"].partition_broadcast(P)).then_inc(weights_in, 16)

                def body(at):
                    if g := at(0):
                        sp.wait_ge(agg, count(g, 1, back=2))
                        sp.wait_ge(self_loop, count(g, 2, back=2))
                        sp.dma_start(AT[par(g)][:, :, :], adjT[bass.ds(pair(g), 1), par(g)].rearrange("a p c n -> (a p) c n")).then_inc(adj_in[par(g)], 16)
                        sp.wait_ge(wr_sum, count(g, 1, back=2))
                        sp.dma_start(WC[:, par(g), bass.ds(pair(g), 1), :], wr[par(g), :, bass.ds(pair(g), 1), :]).then_inc(wr_in[par(g)], 16)

                sweep(sp, 0, body)

            @block.vector
            def _(dve):
                dve.wait_ge(weights_in, 16 * weight_dmas)
                dve.tensor_scalar(rmsw[:, :], rmsw[:, :], 512 ** 0.5, None, ALU.mult).then_inc(rms_weight, 1)
                dve.wait_ge(rms_weight, 1)

                def body(at):
                    if g := at(0):
                        x = graph_rows(X, g)
                        for t in range(TILES):
                            dve.bn_stats(st[par(g)][:, t, :], x[:, t * D:(t + 1) * D]).then_inc(stats, 1)
                        dve.wait_ge(stats, count(g, 4, TILES))
                    if g := at(1):
                        x = graph_rows(X, g)
                        dve.wait_ge(scale, count(g, 2))
                        dve.wait_ge(agg, count(g, 1, back=2))
                        for t in range(TILES):
                            dve.tensor_scalar(xln[par(g)][:, t, :], x[:, t * D:(t + 1) * D], mv[par(g)][:, t, 0:1],
                                                        rstd[par(g)][:, t:t + 1], ALU.subtract, ALU.mult).then_inc(normed, 1)
                    if g := at(0):
                        for t in range(TILES):
                            dve.bn_aggr(mv[par(g)][:, t, :], st[par(g)][:, t, :]).then_inc(stats, 1)
                    if g := at(2):
                        dve.wait_ge(squares, count(g, 2, back=2))
                        for t in range(TILES):
                            dve.wait_ge(hidden, count(g, 2, t + 1))
                            dve.tensor_tensor(hb[par(g)][:, t, :], p_h[t][:, :], b1[:, :], ALU.add).then_inc(biased, 1)
                    if g := at(3):
                        dve.wait_ge(rms, count(g, 2))
                        dve.wait_ge(biased, count(g, 2))
                        dve.wait_ge(turned, count(g, 2, back=2))
                        for t in range(TILES):
                            dve.scalar_tensor_tensor(out=hn[par(g)][:, t, :], in0=hb[par(g)][:, t, :],
                                                               scalar=rr[par(g)][:, t:t + 1], in1=rmsw[:, :],
                                                               op0=ALU.mult, op1=ALU.mult).then_inc(scaled, 1)
                    if g := at(5):
                        x = graph_rows(X, g)
                        dve.wait_ge(product, count(g, 1))
                        dve.tensor_tensor(tmp[par(g)][:, :], p_out[:, 0:NODES], b2[:, :, :].rearrange("p a d -> p (a d)"), ALU.add).then_inc(added, 1)
                        dve.wait_ge(added, count(g, 2, 1))
                        dve.tensor_tensor(x, x, tmp[par(g)][:, :], ALU.add).then_inc(added, 1)

                sweep(dve, 5, body)

            @block.gpsimd
            def _(pool):
                def body(at):
                    if g := at(0):
                        pool.wait_ge(stats, count(g, 4))
                        pool.tensor_tensor(ve[par(g)][:, :], mv[par(g)][:, :, 1], lneps[:, 0:TILES], ALU.add).then_inc(scale, 1)
                        pool.wait_ge(scale, count(g, 2, 1))
                        pool.wait_ge(normed, count(g, 2, back=2))
                        pool.tensor_tensor(rstd[par(g)][:, :], ve[par(g)][:, :], mhalf[:, 0:TILES], ALU.pow).then_inc(scale, 1)
                        pool.wait_ge(adj_in[par(g)], loads(g))
                        for t in range(TILES):
                            a = AT[par(g)][:, t, t * P:(t + 1) * P]
                            pool.tensor_tensor(a, a, epsi[:, :], ALU.add).then_inc(self_loop, 1)
                        pool.wait_ge(wr_in[par(g)], loads(g))
                        w = one(WC[:, par(g), bass.ds(pair(g), 1), :])
                        pool.tensor_tensor(w, w, WS[:, par(g), :], ALU.add).then_inc(wr_sum, 1)
                    if g := at(2):
                        pool.wait_ge(squares, count(g, 2))
                        pool.tensor_tensor(ms[par(g)][:, :], ssq[par(g)][:, :], rmseps[:, 0:TILES], ALU.add).then_inc(rms, 1)
                        pool.wait_ge(rms, count(g, 2, 1))
                        pool.wait_ge(scaled, count(g, 2, back=2))
                        pool.tensor_tensor(rr[par(g)][:, :], ms[par(g)][:, :], mhalf[:, 0:TILES], ALU.pow).then_inc(rms, 1)

                sweep(pool, 2, body)

            @block.scalar
            def _(act):
                def body(at):
                    if g := at(1):
                        act.wait_ge(agg, count(g, 1))
                        act.wait_ge(hidden, count(g, 2, back=2))
                        act.copy(aggT[par(g)][:, :], p_agg[:, 0:NODES]).then_inc(agg_sb, 1)
                    if g := at(2):
                        for t in range(TILES):
                            act.wait_ge(biased, count(g, 2, t + 1))
                            act.wait_ge(rms, count(g, 2, back=2))
                            act.activation(junk[par(g)][:, t, :], hb[par(g)][:, t, :], ACT.Square, accum_out=ssq[par(g)][:, t:t + 1]).then_inc(squares, 1)
                    if g := at(3):
                        for t in range(TILES):
                            act.wait_ge(scaled, count(g, 2, t + 1))
                            act.activation(hn[par(g)][:, t, :], hn[par(g)][:, t, :], ACT.Silu).then_inc(silu, 1)
                    if g := at(4):
                        act.wait_ge(product, count(g, 1, back=2))
                        for t in range(TILES):
                            act.wait_ge(turned, count(g, 2, t + 1))
                            act.copy(hT[par(g)][:, t, :, :].rearrange("p f n -> p (f n)"), p_t[t][:, :]).then_inc(turned_sb, 1)

                sweep(act, 4, body)

            @block.tensor
            def _(pe):
                pe.wait_ge(weights_in, 16 * weight_dmas)

                def body(at):
                    if g := at(1):
                        pe.wait_ge(normed, count(g, 2))
                        pe.wait_ge(self_loop, count(g, 2))
                        pe.wait_ge(agg_sb, count(g, 1, back=1))
                        for t in range(TILES):
                            mm = nc.tensor.matmul(p_agg[:, 0:NODES], xln[par(g)][:, t, :], AT[par(g)][:, t, :],
                                                  start=(t == 0), stop=(t == TILES - 1))
                        mm.then_inc(agg, 1)
                    if g := at(2):
                        pe.wait_ge(agg_sb, count(g, 1))
                        for t in range(TILES):
                            pe.wait_ge(biased, count(g, 2, t + 1, back=1))
                            nc.tensor.matmul(p_h[t][:, :], aggT[par(g)][:, t * P:(t + 1) * P], W1[:, :], start=True, stop=True).then_inc(hidden, 1)
                    if g := at(4):
                        for t in range(TILES):
                            pe.wait_ge(silu, count(g, 2, t + 1))
                            pe.wait_ge(turned_sb, count(g, 2, t + 1, back=1))
                            for f in range(4):
                                mm = transpose(nc, p_t[t][:, f * P:(f + 1) * P], hn[par(g)][:, t, f * P:(f + 1) * P], ident[:, :])
                            mm.then_inc(turned, 1)
                    if g := at(5):
                        pe.wait_ge(turned_sb, count(g, 2))
                        pe.wait_ge(added, count(g, 2, 1, back=1))
                        for t in range(TILES):
                            for f in range(4):
                                mm = nc.tensor.matmul(p_out[:, t * D:(t + 1) * D], hT[par(g)][:, t, f, :], W2[:, f, :],
                                                      start=(f == 0), stop=(f == 3))
                        mm.then_inc(product, 1)

                sweep(pe, 5, body)


EXPERTS0 = 16
HID = 256


def ffn0(nc, outer, X, ident, mhalf, lneps, WC, biases, ids, d):
    with ExitStack() as ctx:
        def sb(name, shape, dt=F32):
            return ctx.enter_context(nc.sbuf_tensor(name, shape, dt))

        def two(name, shape, dt=F32):
            return [sb(name + "0", shape, dt), sb(name + "1", shape, dt)]

        def bank(name):
            return ctx.enter_context(nc.psum_tensor(name, [P, 512], F32))

        def sem(name):
            return outer.enter_context(nc.semaphore(name))

        Wi = sb("b_Wi", [P, HID])
        bi = sb("b_bi", [P, 2])
        Wo = sb("b_Wo", [P, 2, D])
        bo = sb("b_bo", [P, 2, D])
        st = two("b_st", [P, TILES, 6])
        mv = two("b_mv", [P, TILES, 2])
        ve = two("b_ve", [P, TILES])
        rstd = two("b_rstd", [P, TILES])
        xln = two("b_xln", [P, TILES, D])
        xT = two("b_xT", [P, NODES])
        hT = [two(f"b_hT{l}", [P, 2, NODES]) for l in range(3)]
        y = [two(f"b_y{l}", [P, TILES, HID]) for l in range(2)]
        tmp = two("b_tmp", [P, NODES])
        p_x = bank("b_px")
        p_h = bank("b_ph")
        p_y = [bank("b_py0"), bank("b_py1")]
        p_t = [bank("b_pt0"), bank("b_pt1")]
        p_out = bank("b_pout")

        weights_in = sem("b_weights_in")
        stats = sem("b_stats")
        scale = sem("b_scale")
        normed = sem("b_normed")
        x_turned = sem("b_x_turned")
        x_sb = sem("b_x_sb")
        first = sem("b_first")
        layer = [sem(f"b_layer{l}") for l in range(2)]
        layer_sb = [sem(f"b_layer_sb{l}") for l in range(2)]
        turned = [sem(f"b_turned{l}") for l in range(2)]
        relu = [sem(f"b_relu{l}") for l in range(3)]
        product = sem("b_product")
        added = sem("b_added")

        with nc.Block() as block:
            @block.sync
            def _(sp):
                sp.dma_start(Wi[:, :], d["b_WiT"]).then_inc(weights_in, 16)
                sp.dma_start(bi[:, :], d["b_bi"]).then_inc(weights_in, 16)
                sp.dma_start(Wo[:, :, :], d["b_WoT"].rearrange("(k p) n -> p k n", p=P)).then_inc(weights_in, 16)
                sp.dma_start(bo[:, :, :], d["b_box2"].partition_broadcast(P)).then_inc(weights_in, 16)

            @block.vector
            def _(dve):
                dve.wait_ge(weights_in, 64)

                def body(at):
                    if g := at(0):
                        x = graph_rows(X, g)
                        for t in range(TILES):
                            dve.bn_stats(st[par(g)][:, t, :], x[:, t * D:(t + 1) * D]).then_inc(stats, 1)
                        dve.wait_ge(stats, count(g, 4, TILES))
                    if g := at(1):
                        x = graph_rows(X, g)
                        dve.wait_ge(scale, count(g, 2))
                        dve.wait_ge(x_turned, count(g, 1, back=2))
                        for t in range(TILES):
                            dve.tensor_scalar(xln[par(g)][:, t, :], x[:, t * D:(t + 1) * D], mv[par(g)][:, t, 0:1],
                                                        rstd[par(g)][:, t:t + 1], ALU.subtract, ALU.mult).then_inc(normed, 1)
                    if g := at(0):
                        for t in range(TILES):
                            dve.bn_aggr(mv[par(g)][:, t, :], st[par(g)][:, t, :]).then_inc(stats, 1)
                    for l in range(2):
                        if g := at(4 + 2 * l):
                            dve.wait_ge(layer[l], count(g, 1))
                            dve.wait_ge(turned[l], count(g, 1, back=2))
                            dve.tensor_copy(y[l][par(g)][:, :, :].rearrange("p t n -> p (t n)"), p_y[l][:, :]).then_inc(layer_sb[l], 1)
                    if g := at(8):
                        x = graph_rows(X, g)
                        dve.wait_ge(product, count(g, 1))
                        dve.tensor_tensor(tmp[par(g)][:, :], p_out[:, 0:NODES], bo[:, :, :].rearrange("p a d -> p (a d)"), ALU.add).then_inc(added, 1)
                        dve.wait_ge(added, count(g, 2, 1))
                        dve.tensor_tensor(x, x, tmp[par(g)][:, :], ALU.add).then_inc(added, 1)

                sweep(dve, 8, body)

            @block.gpsimd
            def _(pool):
                def body(at):
                    if g := at(0):
                        pool.wait_ge(stats, count(g, 4))
                        pool.tensor_tensor(ve[par(g)][:, :], mv[par(g)][:, :, 1], lneps[:, 0:TILES], ALU.add).then_inc(scale, 1)
                        pool.wait_ge(scale, count(g, 2, 1))
                        pool.wait_ge(normed, count(g, 2, back=2))
                        pool.tensor_tensor(rstd[par(g)][:, :], ve[par(g)][:, :], mhalf[:, 0:TILES], ALU.pow).then_inc(scale, 1)

                sweep(pool, 0, body)

            @block.scalar
            def _(act):
                act.wait_ge(weights_in, 64)

                def body(at):
                    if g := at(2):
                        act.wait_ge(x_turned, count(g, 1))
                        act.wait_ge(first, count(g, 1, back=2))
                        act.copy(xT[par(g)][:, :], p_x[:, 0:NODES]).then_inc(x_sb, 1)
                    if g := at(3):
                        act.wait_ge(first, count(g, 1))
                        act.wait_ge(layer[0], count(g, 1, back=2))
                        for k in range(2):
                            act.activation(hT[0][par(g)][:, k, :], p_h[:, k * NODES:(k + 1) * NODES], ACT.Relu, bias=bi[:, k:k + 1]).then_inc(relu[0], 1)
                    for l in range(2):
                        if g := at(5 + 2 * l):
                            act.wait_ge(turned[l], count(g, 1))
                            act.wait_ge((product if l else layer[1]), count(g, 1, back=2))
                            for t in range(TILES):
                                e = act.value_load(ids[0:1, bass.ds(pair(g), 1), par(g) * 2 + t], min_val=0, max_val=EXPERTS0)
                                for k in range(2):
                                    act.activation(hT[l + 1][par(g)][:, k, t * P:(t + 1) * P],
                                                                  p_t[l][:, (2 * k + t) * P:(2 * k + t + 1) * P], ACT.Relu,
                                                                  bias=biases[:, bass.ds(e, 1), 2 * l + k]).then_inc(relu[l + 1], 1)

                sweep(act, 7, body)

            @block.tensor
            def _(pe):
                pe.wait_ge(weights_in, 64)

                def body(at):
                    if g := at(2):
                        pe.wait_ge(normed, count(g, 2))
                        pe.wait_ge(x_sb, count(g, 1, back=1))
                        for t in range(TILES):
                            mm = transpose(nc, p_x[:, t * P:(t + 1) * P], xln[par(g)][:, t, :], ident[:, :])
                        mm.then_inc(x_turned, 1)
                    if g := at(3):
                        pe.wait_ge(x_sb, count(g, 1))
                        pe.wait_ge(relu[0], count(g, 2, back=1))
                        for k in range(2):
                            mm = nc.tensor.matmul(p_h[:, k * NODES:(k + 1) * NODES], Wi[:, k * P:(k + 1) * P], xT[par(g)][:, :], start=True, stop=True)
                        mm.then_inc(first, 1)
                    for l in range(2):
                        if g := at(4 + 2 * l):
                            pe.wait_ge(relu[l], count(g, (4 if l else 2)))
                            pe.wait_ge(layer_sb[l], count(g, 1, back=1))
                            for t in range(TILES):
                                e = pe.value_load(ids[0:1, bass.ds(pair(g), 1), par(g) * 2 + t], min_val=0, max_val=EXPERTS0)
                                for k in range(2):
                                    mm = nc.tensor.matmul(p_y[l][:, t * HID:(t + 1) * HID], hT[l][par(g)][:, k, t * P:(t + 1) * P],
                                                          one(WC[:, l, bass.ds(e, 1), k * HID:(k + 1) * HID]), start=(k == 0), stop=(k == 1))
                            mm.then_inc(layer[l], 1)
                        if g := at(5 + 2 * l):
                            pe.wait_ge(layer_sb[l], count(g, 1))
                            pe.wait_ge(relu[l + 1], count(g, 4, back=1))
                            for t in range(TILES):
                                for k in range(2):
                                    mm = transpose(nc, p_t[l][:, (2 * k + t) * P:(2 * k + t + 1) * P], y[l][par(g)][:, t, k * P:(k + 1) * P], ident[:, :])
                            mm.then_inc(turned[l], 1)
                    if g := at(8):
                        pe.wait_ge(relu[2], count(g, 4))
                        pe.wait_ge(added, count(g, 2, 1, back=1))
                        for t in range(TILES):
                            for k in range(2):
                                mm = nc.tensor.matmul(p_out[:, t * D:(t + 1) * D], hT[2][par(g)][:, k, t * P:(t + 1) * P], Wo[:, k, :],
                                                      start=(k == 0), stop=(k == 1))
                        mm.then_inc(product, 1)

                sweep(pe, 8, body)


HEADS = 8
NEG = -1e9
LEAK = 0.01


def gnn1(nc, outer, X, ident, mhalf, lneps, d):
    with ExitStack() as ctx:
        def sb(name, shape, dt=F32):
            return ctx.enter_context(nc.sbuf_tensor(name, shape, dt))

        def two(name, shape, dt=F32):
            return [sb(name + "0", shape, dt), sb(name + "1", shape, dt)]

        def bank(name):
            return ctx.enter_context(nc.psum_tensor(name, [P, 512], F32))

        def sem(name):
            return outer.enter_context(nc.semaphore(name))

        values_w = sb("c_values_w", [P, HEADS * D])
        query_w = sb("c_query_w", [P, HEADS])
        key_w = sb("c_key_w", [P, P])
        query_c = sb("c_query_c", [P, TILES, HEADS])
        key_c = sb("c_key_c", [P, 1])
        out_c = sb("c_out_c", [P, TILES, D])
        pick = sb("c_pick", [P, HEADS, P])
        gnn1_weights(nc, outer, values_w, query_w, key_w, query_c, key_c, out_c, pick, d)

        AN = two("c_AN", [P, TILES, NODES])
        mask = two("c_mask", [P, TILES, NODES])
        st = two("c_st", [P, TILES, 6])
        mv = two("c_mv", [P, TILES, 2])
        ve = two("c_ve", [P, TILES])
        rstd = two("c_rstd", [P, TILES])
        f = two("c_f", [P, TILES * D])
        residual = sb("c_residual", [P, GRAPHS // 2, 2, TILES * D])
        fT = two("c_fT", [P, NODES])
        fT_late = two("c_fT_late", [P, NODES])
        q = two("c_q", [P, TILES * HEADS])
        kT = two("c_kT", [P, NODES])
        top = two("c_top", [P, TILES * HEADS])
        neg = two("c_neg", [P, TILES * HEADS])
        shift = two("c_shift", [P, TILES * HEADS])
        L = two("c_L", [P, TILES, HEADS, NODES])
        E = two("c_E", [P, TILES, HEADS, NODES])
        total = two("c_total", [P, TILES * HEADS])
        inv = two("c_inv", [P, TILES * HEADS])
        V = two("c_V", [P, TILES, HEADS * D])
        ET = two("c_ET", [P, 512])
        z = two("c_z", [P, NODES])
        th = two("c_th", [P, NODES])
        sg = two("c_sg", [P, NODES])
        p_x = bank("c_px")
        p_qk = bank("c_pqk")
        p_k = [bank("c_pk0"), bank("c_pk1")]
        p_v = bank("c_pv")
        p_e = [bank("c_pe0"), bank("c_pe1")]
        p_out = bank("c_pout")

        adj_in = [sem("c_adj_in0"), sem("c_adj_in1")]
        stats = sem("c_stats")
        scale = sem("c_scale")
        masked = sem("c_masked")
        normed = sem("c_normed")
        kept = sem("c_kept")
        x_turned = sem("c_x_turned")
        x_sb = sem("c_x_sb")
        x_late = sem("c_x_late")
        qk = sem("c_qk")
        qk_sb = sem("c_qk_sb")
        keys = sem("c_keys")
        summed = sem("c_summed")
        shifted = sem("c_shifted")
        leaky = sem("c_leaky")
        shift_ready = sem("c_shift_ready")
        exped = sem("c_exped")
        inverse = sem("c_inverse")
        weighted = sem("c_weighted")
        values = sem("c_values")
        values_sb = sem("c_values_sb")
        e_turned = sem("c_e_turned")
        e_sb = sem("c_e_sb")
        attended = sem("c_attended")
        z_ready = sem("c_z_ready")
        tanh = sem("c_tanh")
        added = sem("c_added")

        adj = d["adj"].rearrange("(j b) (t p) m -> j b p t m", b=2, p=P)

        with nc.Block() as block:
            @block.sync
            def _(sp):
                def body(at):
                    if g := at(0):
                        sp.wait_ge(masked, count(g, 1, back=2))
                        sp.dma_start(AN[par(g)][:, :, :], adj[bass.ds(pair(g), 1), par(g)].rearrange("a p t m -> (a p) t m")).then_inc(adj_in[par(g)], 16)

                sweep(sp, 0, body)

            @block.vector
            def _(dve):
                def body(at):
                    g0, g4, g5 = at(0), at(4), at(5)
                    if g := at(7):
                        dve.wait_ge(attended, count(g, 8))
                        dve.wait_ge(kept, count(g, 1))
                        dve.wait_ge(tanh, count(g, 1, back=2))
                        dve.tensor_tensor(z[par(g)][:, :], p_out[:, 0:NODES], graph_rows(residual, g), ALU.add).then_inc(z_ready, 1)
                    if g := g0:
                        x = graph_rows(X, g)
                        for t in range(TILES):
                            dve.bn_stats(st[par(g)][:, t, :], x[:, t * D:(t + 1) * D]).then_inc(stats, 1)
                        dve.wait_ge(stats, count(g, 4, TILES))
                    if g := at(1):
                        x = graph_rows(X, g)
                        dve.wait_ge(scale, count(g, 2))
                        dve.wait_ge(x_turned, count(g, 1, back=2))
                        dve.wait_ge(kept, count(g, 1, back=2))
                        for t in range(TILES):
                            dve.tensor_scalar(f[par(g)][:, t * D:(t + 1) * D], x[:, t * D:(t + 1) * D], mv[par(g)][:, t, 0:1],
                                                        rstd[par(g)][:, t:t + 1], ALU.subtract, ALU.mult).then_inc(normed, 1)
                    if g := g0:
                        for t in range(TILES):
                            dve.bn_aggr(mv[par(g)][:, t, :], st[par(g)][:, t, :]).then_inc(stats, 1)
                    if g := at(3):
                        dve.wait_ge(qk, count(g, 1))
                        dve.wait_ge(keys, count(g, 4, back=2))
                        dve.tensor_tensor(q[par(g)][:, :], p_qk[:, 0:TILES * HEADS], query_c[:, :, :].rearrange("p t h -> p (t h)"), ALU.add).then_inc(qk_sb, 1)
                        dve.tensor_scalar(kT[par(g)][:, :], p_qk[:, 256:512], key_c[:, 0:1], None, ALU.add).then_inc(qk_sb, 1)
                    if g := g4:
                        dve.wait_ge(adj_in[par(g)], loads(g))
                        dve.tensor_scalar(mask[par(g)][:, :, :].rearrange("p t m -> p (t m)"), AN[par(g)][:, :, :].rearrange("p t m -> p (t m)"),
                                                    1.0, -NEG, ALU.subtract, ALU.mult).then_inc(masked, 1)
                        dve.wait_ge(keys, count(g, 4, 1))
                        dve.wait_ge(x_sb, count(g, 1))
                        dve.wait_ge(values, count(g, 4, back=2))
                        dve.wait_ge(exped, count(g, 16, back=2))
                        dve.wait_ge(masked, count(g, 1))
                        dve.tensor_copy(fT_late[par(g)][:, :], fT[par(g)][:, :]).then_inc(x_late, 1)
                    for u in range(5):
                        if (g := g4) and u:
                            if u < 4:
                                dve.wait_ge(keys, count(g, 4, u + 1))
                            dve.wait_ge(summed, count(g, 16, 4 * u))
                            for h in (2 * u - 2, 2 * u - 1):
                                for t in range(TILES):
                                    e = L[par(g)][:, t, h, :]
                                    dve.tensor_scalar(e, e, q[par(g)][:, t * HEADS + h:t * HEADS + h + 1], None, ALU.add).then_inc(shifted, 1)
                        if (g := g4) and u < 4:
                            for h in (2 * u, 2 * u + 1):
                                for t in range(TILES):
                                    n = t * HEADS + h
                                    dve.tensor_tensor_reduce(L[par(g)][:, t, h, :], p_k[u % 2][:, (h % 2) * NODES:(h % 2 + 1) * NODES],
                                                                       mask[par(g)][:, t, :], 1.0, -3.4e38, ALU.add, ALU.max, top[par(g)][:, n:n + 1]).then_inc(summed, 1)
                        if (g := g4) and u:
                            dve.wait_ge(shifted, count(g, 16, 4 * u))
                            for t in range(TILES):
                                e = L[par(g)][:, t, 2 * u - 2:2 * u, :].rearrange("p h m -> p (h m)")
                                dve.scalar_tensor_tensor(out=e, in0=e, scalar=LEAK, in1=e, op0=ALU.mult, op1=ALU.max).then_inc(leaky, 1)
                        if (g := g5) and u == 3:
                            dve.wait_ge(exped, count(g, 16, HEADS))
                            dve.wait_ge(weighted, count(g, 2, 1, back=2))
                            dve.reciprocal(inv[par(g)][:, 0:HEADS], total[par(g)][:, 0:HEADS]).then_inc(inverse, 1)
                    if g := g4:
                        dve.scalar_tensor_tensor(out=neg[par(g)][:, :], in0=top[par(g)][:, :], scalar=-1.0, in1=q[par(g)][:, :],
                                                                op0=ALU.mult, op1=ALU.subtract).then_inc(shift_ready, 1)
                        dve.wait_ge(shift_ready, count(g, 2, 1))
                        dve.scalar_tensor_tensor(out=shift[par(g)][:, :], in0=neg[par(g)][:, :], scalar=LEAK, in1=neg[par(g)][:, :],
                                                                op0=ALU.mult, op1=ALU.min).then_inc(shift_ready, 1)
                    if g := at(8):
                        x = graph_rows(X, g)
                        dve.wait_ge(tanh, count(g, 1))
                        dve.tensor_scalar(sg[par(g)][:, :], th[par(g)][:, :], 0.5, 0.5, ALU.mult, ALU.add).then_inc(added, 1)
                        dve.wait_ge(added, count(g, 2, 1))
                        dve.tensor_tensor(x, x, sg[par(g)][:, :], ALU.add).then_inc(added, 1)
                    if g := g5:
                        dve.wait_ge(exped, count(g, 16))
                        dve.wait_ge(weighted, count(g, 2, back=2))
                        dve.reciprocal(inv[par(g)][:, HEADS:], total[par(g)][:, HEADS:]).then_inc(inverse, 1)

                sweep(dve, 8, body)

            @block.gpsimd
            def _(pool):
                def body(at):
                    if g := at(0):
                        pool.wait_ge(stats, count(g, 4))
                        pool.tensor_tensor(ve[par(g)][:, :], mv[par(g)][:, :, 1], lneps[:, 0:TILES], ALU.add).then_inc(scale, 1)
                        pool.wait_ge(scale, count(g, 2, 1))
                        pool.wait_ge(normed, count(g, 2, back=2))
                        pool.tensor_tensor(rstd[par(g)][:, :], ve[par(g)][:, :], mhalf[:, 0:TILES], ALU.pow).then_inc(scale, 1)
                    if g := at(1):
                        pool.wait_ge(normed, count(g, 2))
                        pool.tensor_tensor(graph_rows(residual, g), f[par(g)][:, :], out_c[:, :, :].rearrange("p t d -> p (t d)"), ALU.add).then_inc(kept, 1)
                    if g := at(5):
                        for t in range(TILES):
                            pool.wait_ge(inverse, count(g, 2, t + 1))
                            e = E[par(g)][:, t, :, :]
                            w = inv[par(g)][:, t * HEADS:(t + 1) * HEADS].unsqueeze(2).to_broadcast([P, HEADS, NODES])
                            pool.tensor_tensor(e, e, w, ALU.mult).then_inc(weighted, 1)

                sweep(pool, 5, body)

            @block.scalar
            def _(act):
                def body(at):
                    if g := at(2):
                        act.wait_ge(x_turned, count(g, 1))
                        act.wait_ge(x_late, count(g, 1, back=2))
                        act.wait_ge(qk, count(g, 1, back=2))
                        act.copy(fT[par(g)][:, :], p_x[:, 0:NODES]).then_inc(x_sb, 1)
                    g5, g6 = at(5), at(6)
                    for u in range(4):
                        if g := g5:
                            act.wait_ge(values, count(g, 4, u + 1))
                            act.wait_ge(attended, count(g, 8, back=2))
                            act.copy(V[par(g)][:, u // 2, (u % 2) * 512:(u % 2 + 1) * 512], p_v[:, :]).then_inc(values_sb, 1)
                        if g := g6:
                            for w in (2 * u, 2 * u + 1):
                                act.wait_ge(e_turned, count(g, 8, w + 1))
                                if w < 2:
                                    act.wait_ge(attended, count(g, 8, w + 7, back=1))
                                else:
                                    act.wait_ge(attended, count(g, 8, w - 1))
                                act.copy(ET[w % 2][:, :], p_e[w % 2][:, :]).then_inc(e_sb, 1)
                        if g := g5:
                            if u == 0:
                                act.wait_ge(shift_ready, count(g, 2))
                                act.wait_ge(leaky, count(g, 8))
                                act.wait_ge(e_turned, count(g, 8, back=2))
                                act.wait_ge(inverse, count(g, 2, back=2))
                            for h in range(4 * (u % 2), 4 * (u % 2) + 4):
                                t = u // 2
                                n = t * HEADS + h
                                act.activation(E[par(g)][:, t, h, :], L[par(g)][:, t, h, :], ACT.Exp, bias=shift[par(g)][:, n:n + 1],
                                                        accum_out=total[par(g)][:, n:n + 1]).then_inc(exped, 1)
                    if g := at(7):
                        act.wait_ge(z_ready, count(g, 1))
                        act.wait_ge(added, count(g, 2, back=2))
                        act.activation(th[par(g)][:, :], z[par(g)][:, :], ACT.Tanh, scale=0.5).then_inc(tanh, 1)

                sweep(act, 7, body)

            @block.tensor
            def _(pe):
                def body(at):
                    g4, g5, g6 = at(4), at(5), at(6)

                    def key_rows(u):
                        if g := g4:
                            if u < 2:
                                pe.wait_ge(summed, count(g, 16, 4 * u + 12, back=1))
                            else:
                                pe.wait_ge(summed, count(g, 16, 4 * u - 4))
                            for h in (2 * u, 2 * u + 1):
                                mm = nc.tensor.matmul(p_k[u % 2][:, (h % 2) * NODES:(h % 2 + 1) * NODES], pick[:, h, :], kT[par(g)][:, :],
                                                      start=True, stop=True)
                            mm.then_inc(keys, 1)

                    def value_rows(u):
                        if g := g5:
                            if u:
                                pe.wait_ge(values_sb, count(g, 4, u))
                            else:
                                pe.wait_ge(values_sb, count(g, 4, back=1))
                            nc.tensor.matmul(p_v[:, :], fT_late[par(g)][:, (u // 2) * P:(u // 2 + 1) * P],
                                                       values_w[:, (u % 2) * 512:(u % 2 + 1) * 512], start=True, stop=True).then_inc(values, 1)

                    def turn(w):
                        if g := g6:
                            t, u = w // 4, w % 4
                            pe.wait_ge(weighted, count(g, 2, t + 1))
                            if w < 2:
                                pe.wait_ge(e_sb, count(g, 8, w + 7, back=1))
                            else:
                                pe.wait_ge(e_sb, count(g, 8, w - 1))
                            for k in range(2):
                                for m in range(2):
                                    mm = transpose(nc, p_e[w % 2][:, (2 * k + m) * P:(2 * k + m + 1) * P], E[par(g)][:, t, 2 * u + k, m * P:(m + 1) * P], ident[:, :])
                            mm.then_inc(e_turned, 1)

                    def attend(w):
                        if g := g6:
                            t, u = w // 4, w % 4
                            if w == 0:
                                pe.wait_ge(z_ready, count(g, 1, back=1))
                                pe.wait_ge(values_sb, count(g, 4))
                            pe.wait_ge(e_sb, count(g, 8, w + 1))
                            for k in range(2):
                                for m in range(2):
                                    mm = nc.tensor.matmul(p_out[:, t * D:(t + 1) * D], ET[w % 2][:, (2 * k + m) * P:(2 * k + m + 1) * P],
                                                          V[par(g)][:, m, (2 * u + k) * D:(2 * u + k + 1) * D],
                                                          start=(w == 0 and k == 0 and m == 0), stop=(w == 7 and k == 1 and m == 1),
                                                          skip_group_check=True)
                            mm.then_inc(attended, 1)

                    if g := at(2):
                        pe.wait_ge(normed, count(g, 2))
                        pe.wait_ge(x_sb, count(g, 1, back=1))
                        for t in range(TILES):
                            mm = transpose(nc, p_x[:, t * P:(t + 1) * P], f[par(g)][:, t * D:(t + 1) * D], ident[:, :])
                        mm.then_inc(x_turned, 1)
                    if g := at(3):
                        pe.wait_ge(x_sb, count(g, 1))
                        pe.wait_ge(qk_sb, count(g, 2, back=1))
                        for t in range(TILES):
                            nc.tensor.matmul(p_qk[:, t * HEADS:(t + 1) * HEADS], fT[par(g)][:, t * P:(t + 1) * P], query_w[:, :], start=True, stop=True)
                        nc.tensor.matmul(p_qk[:, 256:512], key_w[:, :], fT[par(g)][:, :], start=True, stop=True).then_inc(qk, 1)
                    if g := g4:
                        pe.wait_ge(qk_sb, count(g, 2))
                    if g := g5:
                        pe.wait_ge(x_late, count(g, 1))
                    key_rows(0)
                    key_rows(1)
                    value_rows(0)
                    turn(0)
                    key_rows(2)
                    turn(1)
                    attend(0)
                    value_rows(1)
                    key_rows(3)
                    for w in range(2, 8):
                        turn(w)
                        attend(w - 1)
                        if w in (4, 6):
                            value_rows(w // 2)
                    attend(7)

                sweep(pe, 6, body)


def gnn1_weights(nc, outer, values_w, query_w, key_w, query_c, key_c, out_c, pick, d):
    with ExitStack() as ctx:
        def sb(name, shape, dt=F32):
            return ctx.enter_context(nc.sbuf_tensor(name, shape, dt))

        def two(name, shape, dt=F32):
            return [sb(name + "0", shape, dt), sb(name + "1", shape, dt)]

        def bank(name):
            return ctx.enter_context(nc.psum_tensor(name, [P, 512], F32))

        def sem(name):
            return outer.enter_context(nc.semaphore(name))

        fc_w = sb("w_fc_w", [P, HEADS, D])
        fp_w = sb("w_fp_w", [P, HEADS, D])
        fc_b = sb("w_fc_b", [P, HEADS])
        qk_w = sb("w_qk_w", [P, 2])
        q_b = sb("w_q_b", [P, 1])
        k_b = sb("w_k_b", [HEADS, 1])
        fp_b = sb("w_fp_b", [P, TILES, D])
        fc_b_wide = sb("w_fc_b_wide", [P, HEADS, P])
        q_wide = sb("w_q_wide", [P, P])
        p_w = [bank("w_pw0"), bank("w_pw1")]
        p_qk = bank("w_pqk")
        p_c = bank("w_pc")
        weights_in, picks, wide, products, steps = (sem(n) for n in ("w_in", "w_picks", "w_wide", "w_products", "w_steps"))

        with nc.Block() as block:
            @block.sync
            def _(sp):
                for to, of in ((fc_w[:, :, :], d["c_fc_wT"]), (fp_w[:, :, :], d["c_fp_w"].rearrange("(h p) n -> p h n", p=P)),
                               (fc_b[:, :], d["c_fc_bT"]), (qk_w[:, :], d["c_qk_w"]), (q_b[:, :], d["c_q_b"].partition_broadcast(P)),
                               (k_b[:, :], d["c_k_b"].partition_broadcast(HEADS)), (fp_b[:, :, :], d["c_fp_bx2"].partition_broadcast(P))):
                    sp.dma_start(to, of).then_inc(weights_in, 16)

            @block.gpsimd
            def _(pool):
                pool.memset(pick[:, :, :], 0.0).then_inc(picks, 1)
                pool.wait_ge(picks, 1)
                pool.affine_select(out=pick[:, :, :], in_=pick[:, :, :], compare_op=ALU.not_equal, fill=1.0, base=0,
                                   pattern=[[-1, HEADS], [0, P]], channel_multiplier=1).then_inc(picks, 1)

            @block.vector
            def _(dve):
                dve.wait_ge(weights_in, 16 * 7)
                dve.tensor_copy(fc_b_wide[:, :, :], fc_b[:, :].unsqueeze(2).to_broadcast([P, HEADS, P])).then_inc(wide, 1)
                dve.tensor_copy(q_wide[:, :], qk_w[:, 0:1].to_broadcast([P, P])).then_inc(wide, 1)
                dve.memset(key_w[:, :], 0.0).then_inc(steps, 1)
                dve.memset(key_c[:, :], 0.0).then_inc(steps, 1)
                dve.wait_ge(products, 1)
                dve.wait_ge(steps, 2)
                for k in range(2):
                    dve.tensor_copy(values_w[:, k * 512:(k + 1) * 512], p_w[k][:, :])
                qk = p_qk[:, 0:2 * HEADS].rearrange("p (h w) -> p h w", w=2)
                dve.tensor_copy(query_w[:, :], qk[:, :, 0])
                dve.tensor_copy(key_w[:, 0:HEADS], qk[:, :, 1])
                for t in range(TILES):
                    dve.tensor_scalar(query_c[:, t, :], p_qk[:, 32:32 + HEADS], q_b[:, 0:1], None, ALU.add)
                    dve.tensor_tensor(out_c[:, t, :], p_c[:, 0:D], fp_b[:, t, :], ALU.add)
                dve.tensor_tensor(key_c[0:HEADS, :], p_qk[0:HEADS, 64:65], k_b[:, :], ALU.add)

            @block.tensor
            def _(pe):
                pe.wait_ge(weights_in, 16 * 7)
                pe.wait_ge(wide, 2)
                for h in range(HEADS):
                    nc.tensor.matmul(p_w[h // 4][:, (h % 4) * D:(h % 4 + 1) * D], fc_w[:, h, :], fp_w[:, h, :], start=True, stop=True)
                    nc.tensor.matmul(p_qk[:, 2 * h:2 * h + 2], fc_w[:, h, :], qk_w[:, :], start=True, stop=True)
                nc.tensor.matmul(p_qk[:, 32:32 + HEADS], q_wide[:, :], fc_b[:, :], start=True, stop=True)
                nc.tensor.matmul(p_qk[0:HEADS, 64:65], fc_b[:, :], qk_w[:, 1:2], start=True, stop=True)
                for h in range(HEADS):
                    mm = nc.tensor.matmul(p_c[:, 0:D], fc_b_wide[:, h, :], fp_w[:, h, :], start=(h == 0), stop=(h == HEADS - 1))
                mm.then_inc(products, 1)


EXPERTS = 8
CHOICES = 2
FF = 512
TOKENS = GRAPHS * NODES
REGION = TOKENS + P
SLOT_TILES = TOKENS * CHOICES // P + EXPERTS
SPARE_TILES = EXPERTS
ROWS = EXPERTS * REGION + SPARE_TILES * P
PAD_TILES = EXPERTS + SPARE_TILES
ROW = D + 1


def route(nc, outer, X, ident, mhalf, lneps, weights, slot_e, slot_row, rows_in, d):
    with ExitStack() as ctx:
        def sb(name, shape, dt=F32):
            return ctx.enter_context(nc.sbuf_tensor(name, shape, dt))

        def two(name, shape, dt=F32):
            return [sb(name + "0", shape, dt), sb(name + "1", shape, dt)]

        def bank(name):
            return ctx.enter_context(nc.psum_tensor(name, [P, 512], F32))

        def sem(name):
            return outer.enter_context(nc.semaphore(name))

        router = sb("d_router", [P, EXPERTS])
        W1 = sb("d_W1", [P, FF])
        b1 = sb("d_b1", [P, 4])
        W2 = sb("d_W2", [P, 4, D])
        b2 = sb("d_b2", [P, TILES, D])
        upper = sb("d_upper", [P, P])
        ones = sb("d_ones", [P, P])
        iota8 = sb("d_iota8", [P, EXPERTS])
        start8 = sb("d_start8", [P, TILES, EXPERTS])
        target = sb("d_target", [P, GRAPHS // 2, 2, CHOICES * TILES], I32)
        padding = sb("d_padding", [P, PAD_TILES, ROW])
        dump = sb("d_dump", [P, PAD_TILES], I32)
        lane = sb("d_lane", [P, 1])
        lastf = sb("d_lastf", [P, EXPERTS])
        last = sb("d_last", [P, EXPERTS], I32)
        st = two("d_st", [P, TILES, 6])
        mv = two("d_mv", [P, TILES, 2])
        ve = two("d_ve", [P, TILES])
        rstd = two("d_rstd", [P, TILES])
        xn = two("d_xn", [P, TILES, D])
        xT = two("d_xT", [P, NODES])
        hT = two("d_hT", [P, 4, NODES])
        tmp = two("d_tmp", [P, NODES])
        pay = [two(f"d_pay{k}", [P, TILES, ROW]) for k in range(CHOICES)]
        best = two("d_best", [P, TILES, 8])
        besti = two("d_besti", [P, TILES, 8], mybir.dt.uint32)
        gap = two("d_gap", [P, TILES])
        th = two("d_th", [P, TILES])
        bestf = two("d_bestf", [P, TILES, CHOICES])
        hot = two("d_hot", [P, TILES, CHOICES, EXPERTS])
        both = two("d_both", [P, TILES, EXPERTS])
        carry = two("d_carry", [P, EXPERTS])
        carry1 = two("d_carry1", [P, EXPERTS])
        rank = two("d_rank", [P, TILES, EXPERTS])
        chosen = two("d_chosen", [P, TILES, CHOICES, EXPERTS])
        rowf = two("d_rowf", [P, TILES * CHOICES])
        row = two("d_row", [P, TILES * CHOICES], I32)
        waited = two("d_waited", [P, 1])
        steps64 = sb("d_steps64", [1, EXPERTS, 64])
        over = sb("d_over", [1, EXPERTS, 64])
        tiles = sb("d_tiles", [1, EXPERTS])
        end = sb("d_end", [1, EXPERTS])
        skip = sb("d_skip", [1, EXPERTS])
        slot = sb("d_slot", [1, SLOT_TILES])
        slotf = sb("d_slotf", [1, SLOT_TILES])
        past = sb("d_past", [1, SLOT_TILES])
        rowsf = sb("d_rowsf", [1, SLOT_TILES])
        p_x = bank("d_px")
        p_h = [bank("d_ph0"), bank("d_ph1")]
        p_y = bank("d_py")
        p_r = bank("d_pr")
        p_c = bank("d_pc")

        weights_in, consts, table, padded = (sem(n) for n in ("d_in", "d_consts", "d_table", "d_padded"))
        scattered = [sem("d_scattered0"), sem("d_scattered1")]
        relay = sem("d_relay")
        stats = sem("d_stats")
        scale = sem("d_scale")
        normed = sem("d_normed")
        x_turned = sem("d_x_turned")
        x_sb = sem("d_x_sb")
        logits = sem("d_logits")
        hidden = sem("d_hidden")
        gelu = sem("d_gelu")
        product = sem("d_product")
        added = sem("d_added")
        packed = sem("d_packed")
        picked = sem("d_picked")
        tanh = sem("d_tanh")
        counted = sem("d_counted")
        placed = sem("d_placed")
        weighed = sem("d_weighed")

        with nc.Block() as block:
            @block.sync
            def _(sp):
                for to, of in ((router[:, :], d["d_router"]), (W1[:, :], d["d_W1s"]), (b1[:, :], d["d_b1sT"]),
                               (W2[:, :, :], d["d_W2s"].rearrange("(f p) n -> p f n", p=P)), (b2[:, :, :], d["d_b2sx2"].partition_broadcast(P))):
                    sp.dma_start(to, of).then_inc(weights_in, 16)

            @block.gpsimd
            def _(pool):
                n = 0

                def made(ins):
                    nonlocal n
                    n += 1
                    ins.then_inc(consts, 1)

                made(pool.memset(ones[:, :], 1.0))
                pool.wait_ge(consts, 1)
                made(pool.affine_select(out=upper[:, :], in_=ones[:, :], compare_op=ALU.is_ge, fill=0.0, base=-1,
                                        pattern=[[1, P]], channel_multiplier=-1))
                made(pool.iota(iota8[:, :], [[1, EXPERTS]], base=0, channel_multiplier=0, allow_small_or_imprecise_dtypes=True))
                made(pool.iota(start8[:, :, :], [[0, TILES], [REGION, EXPERTS]], base=0, channel_multiplier=0, allow_small_or_imprecise_dtypes=True))
                for k in range(CHOICES):
                    made(pool.iota(target[:, :, :, k * TILES:(k + 1) * TILES], [[NODES, GRAPHS], [P, TILES]], base=k * TOKENS, channel_multiplier=1))
                made(pool.iota(dump[:, :], [[P, PAD_TILES]], base=CHOICES * TOKENS, channel_multiplier=1))
                made(pool.iota(lane[:, :], [[0, 1]], base=0, channel_multiplier=1, allow_small_or_imprecise_dtypes=True))
                made(pool.memset(padding[:, :, 0:D], 0.0))
                made(pool.iota(steps64[:, :, :], [[0, EXPERTS], [P, 64]], base=0, channel_multiplier=0, allow_small_or_imprecise_dtypes=True))
                made(pool.iota(slot[:, :], [[1, SLOT_TILES]], base=0, channel_multiplier=0, allow_small_or_imprecise_dtypes=True))
                made(pool.memset(carry[0][:, :], 0.0))
                assert n == 12

                def body(at):
                    if g := at(0):
                        pool.wait_ge(stats, count(g, 4))
                        pool.tensor_tensor(ve[par(g)][:, :], mv[par(g)][:, :, 1], lneps[:, 0:TILES], ALU.add).then_inc(scale, 1)
                        pool.wait_ge(scale, count(g, 2, 1))
                        pool.wait_ge(normed, count(g, 2, back=2))
                        pool.tensor_tensor(rstd[par(g)][:, :], ve[par(g)][:, :], mhalf[:, 0:TILES], ALU.pow).then_inc(scale, 1)
                    if g := at(4):
                        pool.wait_ge(packed, count(g, 6))
                        pool.wait_ge(placed, count(g, 8))
                        pool.wait_ge(relay, count(g, 1, back=2))
                        pool.tensor_tensor(waited[par(g)][:, :], ident[:, 0:1], ident[:, 0:1], ALU.mult).then_inc(relay, 1)
                        for t in range(TILES):
                            for k in range(CHOICES):
                                n = t * CHOICES + k
                                pool.indirect_dma_start(
                                    out=rows_in, out_offset=bass.IndirectOffsetOnAxis(ap=row[par(g)][:, n:n + 1], axis=0),
                                    in_=pay[k][par(g)][:, t, :], in_offset=None).then_inc(scattered[par(g)], 16)

                sweep(pool, 4, body)
                pool.wait_ge(table, 3)
                for e in range(EXPERTS):
                    pool.indirect_dma_start(out=rows_in, out_offset=bass.IndirectOffsetOnAxis(ap=last[:, e:e + 1], axis=0),
                                            in_=padding[:, e, :], in_offset=None).then_inc(padded, 16)
                for k in range(SPARE_TILES):
                    r = EXPERTS * REGION + k * P
                    pool.dma_start(rows_in[r:r + P, :], padding[:, EXPERTS + k, :]).then_inc(padded, 16)
                pool.wait_ge(padded, 16 * (EXPERTS + SPARE_TILES))
                for b in range(2):
                    pool.wait_ge(scattered[b], 16 * 4 * (GRAPHS // 2))

            @block.vector
            def _(dve):
                dve.wait_ge(weights_in, 16 * 5)
                dve.wait_ge(consts, 12)
                dve.tensor_copy(padding[:, :, D:ROW].bitcast(I32), dump[:, :].unsqueeze(2)).then_inc(table, 1)

                def body(at):
                    if g := at(0):
                        x = graph_rows(X, g)
                        for t in range(TILES):
                            dve.bn_stats(st[par(g)][:, t, :], x[:, t * D:(t + 1) * D]).then_inc(stats, 1)
                        dve.wait_ge(stats, count(g, 4, TILES))
                    if g := at(3):
                        dve.wait_ge(scattered[par(g)], 16 * 4 * pair(g))
                        dve.tensor_copy(pay[0][par(g)][:, :, 0:D], xn[par(g)][:, :, :]).then_inc(packed, 1)
                        dve.tensor_copy(pay[1][par(g)][:, :, 0:D], xn[par(g)][:, :, :]).then_inc(packed, 1)
                    if g := at(1):
                        x = graph_rows(X, g)
                        dve.wait_ge(scale, count(g, 2))
                        dve.wait_ge(x_turned, count(g, 1, back=2))
                        dve.wait_ge(packed, count(g, 6, 2, back=2))
                        for t in range(TILES):
                            dve.tensor_scalar(xn[par(g)][:, t, :], x[:, t * D:(t + 1) * D], mv[par(g)][:, t, 0:1],
                                                        rstd[par(g)][:, t:t + 1], ALU.subtract, ALU.mult).then_inc(normed, 1)
                    if g := at(0):
                        for t in range(TILES):
                            dve.bn_aggr(mv[par(g)][:, t, :], st[par(g)][:, t, :]).then_inc(stats, 1)
                    if g := at(4):
                        a, b = par(g), 1 - par(g)
                        dve.wait_ge(counted, count(g, 1))
                        dve.tensor_tensor(carry1[a][:, :], carry[a][:, :], p_c[:, 64:64 + EXPERTS], ALU.add).then_inc(placed, 1)
                        dve.wait_ge(placed, count(g, 8, 1))
                        dve.tensor_tensor(carry[b][:, :], carry1[a][:, :], p_c[:, 64 + EXPERTS:64 + 2 * EXPERTS], ALU.add).then_inc(placed, 1)
                        dve.tensor_tensor(rank[a][:, :, :].rearrange("p t e -> p (t e)"), p_c[:, 0:TILES * EXPERTS],
                                               start8[:, :, :].rearrange("p t e -> p (t e)"), ALU.add).then_inc(placed, 1)
                        dve.wait_ge(placed, count(g, 8, 3))
                        dve.tensor_tensor(rank[a][:, 0, :], rank[a][:, 0, :], carry[a][:, :], ALU.add).then_inc(placed, 1)
                        dve.tensor_tensor(rank[a][:, 1, :], rank[a][:, 1, :], carry1[a][:, :], ALU.add).then_inc(placed, 1)
                        dve.wait_ge(placed, count(g, 8, 5))
                        dve.tensor_tensor(chosen[a][:, :, :, :], hot[a][:, :, :, :],
                                               rank[a][:, :, :].unsqueeze(2).to_broadcast([P, TILES, CHOICES, EXPERTS]), ALU.mult).then_inc(placed, 1)
                        dve.wait_ge(placed, count(g, 8, 6))
                        dve.tensor_reduce(rowf[a][:, :], chosen[a][:, :, :, :].rearrange("p t k e -> p (t k) e"), AX.X, ALU.add).then_inc(placed, 1)
                        dve.wait_ge(placed, count(g, 8, 7))
                        dve.tensor_copy(row[a][:, :], rowf[a][:, :]).then_inc(placed, 1)
                        dve.wait_ge(tanh, count(g, 1))
                        for k, sign in ((0, 0.5), (1, -0.5)):
                            dve.tensor_scalar(one_of(weights, g, slice(k * TILES, k * TILES + TILES)), th[a][:, :], sign, 0.5, ALU.mult, ALU.add).then_inc(weighed, 1)
                    if g := at(3):
                        for k in range(CHOICES):
                            for t in range(TILES):
                                n = k * TILES + t
                                if n == 0:
                                    dve.wait_ge(logits, count(g, 1))
                                dve.tensor_copy(pay[k][par(g)][:, t, D:ROW].bitcast(I32), one_of(target, g, n)).then_inc(packed, 1)
                        for t in range(TILES):
                            dve.max(best[par(g)][:, t, :], p_r[:, t * EXPERTS:(t + 1) * EXPERTS]).then_inc(picked, 1)
                        dve.wait_ge(picked, count(g, 8, 2))
                        dve.tensor_tensor(gap[par(g)][:, :], best[par(g)][:, :, 0], best[par(g)][:, :, 1], ALU.subtract).then_inc(picked, 1)
                        for t in range(TILES):
                            dve.max_index(besti[par(g)][:, t, :], best[par(g)][:, t, :], p_r[:, t * EXPERTS:(t + 1) * EXPERTS]).then_inc(picked, 1)
                        dve.wait_ge(picked, count(g, 8, 5))
                        dve.tensor_copy(bestf[par(g)][:, :, :], besti[par(g)][:, :, 0:CHOICES]).then_inc(picked, 1)
                        dve.wait_ge(picked, count(g, 8, 6))
                        dve.wait_ge(placed, count(g, 8, back=2))
                        dve.tensor_tensor(hot[par(g)][:, :, :, :].rearrange("p t k e -> p (t k) e"),
                                               iota8[:, :].unsqueeze(1).to_broadcast([P, TILES * CHOICES, EXPERTS]),
                                               bestf[par(g)][:, :, :].rearrange("p t k -> p (t k)").unsqueeze(2).to_broadcast([P, TILES * CHOICES, EXPERTS]),
                                               ALU.is_equal).then_inc(picked, 1)
                        dve.wait_ge(picked, count(g, 8, 7))
                        dve.wait_ge(counted, count(g, 1, back=2))
                        dve.tensor_tensor(both[par(g)][:, :, :], hot[par(g)][:, :, 0, :], hot[par(g)][:, :, 1, :], ALU.add).then_inc(picked, 1)
                    if g := at(4):
                        x = graph_rows(X, g)
                        dve.wait_ge(product, count(g, 1))
                        dve.tensor_tensor(tmp[par(g)][:, :], p_y[:, 0:NODES], b2[:, :, :].rearrange("p t d -> p (t d)"), ALU.add).then_inc(added, 1)
                        dve.wait_ge(added, count(g, 2, 1))
                        dve.tensor_tensor(x, x, tmp[par(g)][:, :], ALU.add).then_inc(added, 1)

                sweep(dve, 4, body)

                n = 1

                def step(ins):
                    nonlocal n
                    ins.then_inc(table, 1)
                    n += 1
                    dve.wait_ge(table, n)

                taken = carry[0]
                dve.wait_ge(placed, count(graph(GRAPHS - 1), 8))
                step(dve.scalar_tensor_tensor(out=lastf[:, :], in0=taken[:, :], scalar=lane[:, 0:1], in1=start8[:, 0, :], op0=ALU.add, op1=ALU.add))
                step(dve.tensor_copy(last[:, :], lastf[:, :]))
                step(dve.tensor_tensor(over[:, :, :], taken[0:1, :].unsqueeze(2).to_broadcast([1, EXPERTS, 64]), steps64[:, :, :], ALU.is_gt))
                step(dve.tensor_reduce(tiles[:, :], over[:, :, :], AX.X, ALU.add))
                step(dve.tensor_copy(end[:, :], tiles[:, :]))
                for e in range(1, EXPERTS):
                    step(dve.tensor_tensor(end[:, e:e + 1], end[:, e - 1:e], tiles[:, e:e + 1], ALU.add))
                step(dve.tensor_scalar(skip[:, :], tiles[:, :], -float(P), float(REGION), ALU.mult, ALU.add))
                step(dve.tensor_scalar(rowsf[:, :], slot[:, :], float(P), None, ALU.mult))
                step(dve.memset(slotf[:, :], 0.0))
                for e in range(EXPERTS):
                    step(dve.tensor_scalar(past[:, :], slot[:, :], end[:, e:e + 1], None, ALU.is_ge))
                    step(dve.scalar_tensor_tensor(out=rowsf[:, :], in0=past[:, :], scalar=skip[:, e:e + 1], in1=rowsf[:, :], op0=ALU.mult, op1=ALU.add))
                    if e < EXPERTS - 1:
                        step(dve.tensor_tensor(slotf[:, :], slotf[:, :], past[:, :], ALU.add))
                step(dve.tensor_copy(slot_row[:, :, :].rearrange("a j b -> a (j b)"), rowsf[:, :]))
                step(dve.tensor_copy(slot_e[:, :, :].rearrange("a j b -> a (j b)"), slotf[:, :]))

            @block.scalar
            def _(act):
                act.wait_ge(weights_in, 16 * 5)

                def body(at):
                    if g := at(2):
                        act.wait_ge(x_turned, count(g, 1))
                        act.wait_ge(hidden, count(g, 2, back=2))
                        act.wait_ge(logits, count(g, 1, back=2))
                        act.copy(xT[par(g)][:, :], p_x[:, 0:NODES]).then_inc(x_sb, 1)
                    if g := at(3):
                        act.wait_ge(product, count(g, 1, back=2))
                        for f in range(4):
                            act.wait_ge(hidden, count(g, 2, f // 2 + 1))
                            act.activation(hT[par(g)][:, f, :], p_h[f // 2][:, (f % 2) * NODES:(f % 2 + 1) * NODES], ACT.Gelu, bias=b1[:, f:f + 1]).then_inc(gelu, 1)
                        act.wait_ge(picked, count(g, 8, 3))
                        act.wait_ge(weighed, count(g, 2, back=2))
                        act.activation(th[par(g)][:, :], gap[par(g)][:, :], ACT.Tanh, scale=0.5).then_inc(tanh, 1)

                sweep(act, 3, body)

            @block.tensor
            def _(pe):
                pe.wait_ge(weights_in, 16 * 5)
                pe.wait_ge(consts, 12)

                def body(at):
                    if g := at(4):
                        pe.wait_ge(picked, count(g, 8))
                        pe.wait_ge(placed, count(g, 8, 3, back=1))
                        m = both[par(g)][:, :, :].rearrange("p t e -> p (t e)")
                        nc.tensor.matmul(p_c[:, 0:TILES * EXPERTS], upper[:, :], m, start=True, stop=True)
                        nc.tensor.matmul(p_c[:, 64:64 + TILES * EXPERTS], ones[:, :], m, start=True, stop=True).then_inc(counted, 1)
                    if g := at(2):
                        pe.wait_ge(normed, count(g, 2))
                        pe.wait_ge(x_sb, count(g, 1, back=1))
                        for t in range(TILES):
                            mm = transpose(nc, p_x[:, t * P:(t + 1) * P], xn[par(g)][:, t, :], ident[:, :])
                        mm.then_inc(x_turned, 1)
                    if g := at(3):
                        pe.wait_ge(x_sb, count(g, 1))
                        pe.wait_ge(picked, count(g, 8, 5, back=1))
                        for t in range(TILES):
                            mm = nc.tensor.matmul(p_r[:, t * EXPERTS:(t + 1) * EXPERTS], xT[par(g)][:, t * P:(t + 1) * P], router[:, :], start=True, stop=True)
                        mm.then_inc(logits, 1)
                    if g := at(4):
                        pe.wait_ge(gelu, count(g, 4))
                        pe.wait_ge(added, count(g, 2, 1, back=1))
                        for t in range(TILES):
                            for f in range(4):
                                mm = nc.tensor.matmul(p_y[:, t * D:(t + 1) * D], hT[par(g)][:, f, t * P:(t + 1) * P], W2[:, f, :],
                                                      start=(f == 0), stop=(f == 3))
                        mm.then_inc(product, 1)
                    if g := at(3):
                        for k in range(2):
                            pe.wait_ge(gelu, count(g, 4, 2 * k + 2, back=1))
                            for f in (2 * k, 2 * k + 1):
                                mm = nc.tensor.matmul(p_h[k][:, (f % 2) * NODES:(f % 2 + 1) * NODES], W1[:, f * P:(f + 1) * P], xT[par(g)][:, :],
                                                      start=True, stop=True)
                            mm.then_inc(hidden, 1)

                sweep(pe, 4, body)


def one_of(table, g, n):
    n = n if isinstance(n, slice) else slice(n, n + 1)
    return one(table[:, bass.ds(pair(g), 1), par(g), n])


def experts(nc, outer, ident, slot_e, slot_row, rows_in, rows_out, d):
    with ExitStack() as ctx:
        def sb(name, shape, dt=F32):
            return ctx.enter_context(nc.sbuf_tensor(name, shape, dt))

        def two(name, shape, dt=F32):
            return [sb(name + "0", shape, dt), sb(name + "1", shape, dt)]

        def bank(name):
            return ctx.enter_context(nc.psum_tensor(name, [P, 512], F32))

        def sem(name):
            return outer.enter_context(nc.semaphore(name))

        W1 = sb("e_W1", [P, EXPERTS, FF])
        b1 = sb("e_b1", [P, EXPERTS, FF])
        W2 = sb("e_W2", [P, EXPERTS, 4 * D])
        b2 = sb("e_b2", [P, EXPERTS, D])
        xg = two("e_xg", [P, ROW])
        xT = two("e_xT", [P, P])
        to0 = two("e_to0", [P, 1], I32)
        to1 = two("e_to1", [P, 1], I32)
        to2 = two("e_to2", [P, 1], I32)
        hb = two("e_hb", [P, FF])
        hg = two("e_hg", [P, FF])
        hT = two("e_hT", [P, 4, P])
        y = two("e_y", [P, D])
        waited = two("e_waited", [P, 1])
        p_x = bank("e_px")
        p_h = [bank("e_ph0"), bank("e_ph1")]
        p_t = [bank("e_pt0"), bank("e_pt1")]
        p_y = bank("e_py")

        weights_in = sem("e_in")
        rows_here = [sem("e_rows_here0"), sem("e_rows_here1")]
        scattered = [sem("e_scattered0"), sem("e_scattered1")]
        relay = sem("e_relay")
        x_turned = sem("e_x_turned")
        x_sb = sem("e_x_sb")
        hidden = sem("e_hidden")
        biased = sem("e_biased")
        moved = sem("e_moved")
        gelu = sem("e_gelu")
        turned = sem("e_turned")
        turned_sb = sem("e_turned_sb")
        product = sem("e_product")
        result = sem("e_result")

        def expert(eng, s):
            return eng.value_load(one(slot_e[0:1, bass.ds(pair(s), 1), par(s):par(s) + 1]), min_val=0, max_val=EXPERTS - 1)

        with nc.Block() as block:
            @block.sync
            def _(sp):
                sp.dma_start(W1[:, :, :], d["e_W1"].rearrange("e p f -> p e f")).then_inc(weights_in, 16)
                sp.dma_start(W2[:, :, :].rearrange("p e (f n) -> p (e f) n", n=D), d["e_W2"].rearrange("e (f p) n -> p (e f) n", p=P)).then_inc(weights_in, 16)
                sp.dma_start(b1[:, :, :], d["e_b1"].partition_broadcast(P)).then_inc(weights_in, 16)
                sp.dma_start(b2[:, :, :], d["e_b2"].partition_broadcast(P)).then_inc(weights_in, 16)

                def body(at):
                    if s := at(0):
                        sp.wait_ge(x_sb, count(s, 2, back=2))
                        r = sp.value_load(one(slot_row[0:1, bass.ds(pair(s), 1), par(s):par(s) + 1]), min_val=0, max_val=ROWS - P)
                        sp.dma_start(xg[par(s)][:, :], rows_in[bass.ds(r, P), :]).then_inc(rows_here[par(s)], 16)

                sweep(sp, 0, body, SLOT_TILES)

            @block.vector
            def _(dve):
                dve.wait_ge(weights_in, 64)

                def body(at):
                    if s := at(5):
                        dve.wait_ge(scattered[par(s)], 16 * pair(s))
                        dve.wait_ge(moved, count(s, 1))
                        dve.tensor_copy(to2[par(s)][:, :], to1[par(s)][:, :]).then_inc(result, 1)
                    if s := at(3):
                        dve.wait_ge(result, count(s, 2, 1, back=2))
                        dve.wait_ge(x_sb, count(s, 2))
                        dve.tensor_copy(to1[par(s)][:, :], to0[par(s)][:, :]).then_inc(moved, 1)
                    if s := at(1):
                        dve.wait_ge(x_turned, count(s, 1))
                        dve.wait_ge(hidden, count(s, 1, back=2))
                        dve.tensor_copy(xT[par(s)][:, :], p_x[:, 0:P]).then_inc(x_sb, 1)
                        dve.wait_ge(moved, count(s, 1, back=2))
                        dve.tensor_copy(to0[par(s)][:, :], xg[par(s)][:, D:ROW].bitcast(I32)).then_inc(x_sb, 1)
                    if s := at(2):
                        dve.wait_ge(hidden, count(s, 1))
                        dve.wait_ge(gelu, count(s, 1, back=2))
                        e = expert(dve, s)
                        dve.tensor_tensor(hb[par(s)][:, :], p_h[par(s)][:, :], one(b1[:, bass.ds(e, 1), :]), ALU.add).then_inc(biased, 1)
                    if s := at(5):
                        dve.wait_ge(product, count(s, 1))
                        e = expert(dve, s)
                        dve.tensor_tensor(y[par(s)][:, :], p_y[:, 0:D], one(b2[:, bass.ds(e, 1), :]), ALU.add).then_inc(result, 1)

                sweep(dve, 5, body, SLOT_TILES)

            @block.gpsimd
            def _(pool):
                def body(at):
                    if s := at(5):
                        pool.wait_ge(result, count(s, 2))
                        pool.wait_ge(relay, count(s, 1, back=2))
                        pool.tensor_tensor(waited[par(s)][:, :], ident[:, 0:1], ident[:, 0:1], ALU.mult).then_inc(relay, 1)
                        pool.indirect_dma_start(out=rows_out, out_offset=bass.IndirectOffsetOnAxis(ap=to2[par(s)][:, :], axis=0),
                                                                in_=y[par(s)][:, :], in_offset=None).then_inc(scattered[par(s)], 16)

                sweep(pool, 5, body, SLOT_TILES)
                for b in range(2):
                    pool.wait_ge(scattered[b], 16 * (SLOT_TILES // 2))

            @block.scalar
            def _(act):
                def body(at):
                    if s := at(3):
                        act.wait_ge(biased, count(s, 1))
                        act.wait_ge(turned, count(s, 1, back=2))
                        act.activation(hg[par(s)][:, :], hb[par(s)][:, :], ACT.Gelu).then_inc(gelu, 1)
                    if s := at(4):
                        act.wait_ge(turned, count(s, 1))
                        act.wait_ge(product, count(s, 1, back=2))
                        act.copy(hT[par(s)][:, :, :].rearrange("p f n -> p (f n)"), p_t[par(s)][:, :]).then_inc(turned_sb, 1)

                sweep(act, 4, body, SLOT_TILES)

            @block.tensor
            def _(pe):
                pe.wait_ge(weights_in, 64)

                def body(at):
                    if s := at(1):
                        pe.wait_ge(rows_here[par(s)], loads(s))
                        pe.wait_ge(x_sb, count(s, 2, 1, back=1))
                        transpose(nc, p_x[:, 0:P], xg[par(s)][:, 0:D], ident[:, :]).then_inc(x_turned, 1)
                    if s := at(2):
                        pe.wait_ge(x_sb, count(s, 2, 1))
                        pe.wait_ge(biased, count(s, 1, back=2))
                        e = expert(pe, s)
                        nc.tensor.matmul(p_h[par(s)][:, :], xT[par(s)][:, :], one(W1[:, bass.ds(e, 1), :]), start=True, stop=True).then_inc(hidden, 1)
                    if s := at(4):
                        pe.wait_ge(gelu, count(s, 1))
                        pe.wait_ge(turned_sb, count(s, 1, back=2))
                        for f in range(4):
                            mm = transpose(nc, p_t[par(s)][:, f * P:(f + 1) * P], hg[par(s)][:, f * P:(f + 1) * P], ident[:, :])
                        mm.then_inc(turned, 1)
                    if s := at(5):
                        pe.wait_ge(turned_sb, count(s, 1))
                        pe.wait_ge(result, count(s, 2, back=1))
                        e = expert(pe, s)
                        for f in range(4):
                            mm = nc.tensor.matmul(p_y[:, 0:D], hT[par(s)][:, f, :], one(W2[:, bass.ds(e, 1), f * D:(f + 1) * D]), start=(f == 0), stop=(f == 3))
                        mm.then_inc(product, 1)

                sweep(pe, 5, body, SLOT_TILES)


def combine(nc, outer, X, weights, rows_out, out):
    with ExitStack() as ctx:
        def sb(name, shape, dt=F32):
            return ctx.enter_context(nc.sbuf_tensor(name, shape, dt))

        def two(name, shape, dt=F32):
            return [sb(name + "0", shape, dt), sb(name + "1", shape, dt)]

        def bank(name):
            return ctx.enter_context(nc.psum_tensor(name, [P, 512], F32))

        def sem(name):
            return outer.enter_context(nc.semaphore(name))

        y = [[sb(f"f_y{k}{b}", [P, TILES, D]) for b in range(2)] for k in range(CHOICES)]
        y_in = [sem("f_y_in0"), sem("f_y_in1")]
        added = sem("f_added")
        stored = sem("f_stored")
        yt = rows_out[0:CHOICES * TOKENS, :].rearrange("(k j b t p) d -> k j b p t d", k=CHOICES, b=2, t=TILES, p=P)
        ot = out.rearrange("(j b) (t p) d -> j b p t d", b=2, p=P)

        with nc.Block() as block:
            @block.sync
            def _(sp):
                def body(at):
                    if g := at(0):
                        sp.wait_ge(added, count(g, 4, back=2))
                        for k in range(CHOICES):
                            sp.dma_start(y[k][par(g)][:, :, :], yt[k, bass.ds(pair(g), 1), par(g)].rearrange("a p t d -> (a p) t d")).then_inc(y_in[par(g)], 16)

                sweep(sp, 0, body)

            @block.vector
            def _(dve):
                def body(at):
                    if g := at(0):
                        x = graph_rows(X, g)
                        dve.wait_ge(y_in[par(g)], 32 * pair(g) + 32)
                        for k in range(CHOICES):
                            if k:
                                dve.wait_ge(added, count(g, 4, TILES))
                            for t in range(TILES):
                                xt = x[:, t * D:(t + 1) * D]
                                dve.scalar_tensor_tensor(out=xt, in0=y[k][par(g)][:, t, :], scalar=one_of(weights, g, k * TILES + t), in1=xt,
                                                                  op0=ALU.mult, op1=ALU.add).then_inc(added, 1)

                sweep(dve, 0, body)

            @block.scalar
            def _(act):
                def body(at):
                    if g := at(0):
                        act.wait_ge(added, count(g, 4))
                        act.dma_start(ot[bass.ds(pair(g), 1), par(g)].rearrange("a p t d -> (a p) t d"),
                                      graph_rows(X, g).rearrange("p (t d) -> p t d", d=D)).then_inc(stored, 16)

                sweep(act, 0, body)
                act.wait_ge(stored, 16 * GRAPHS)


def setup(nc, outer, X, ident, mhalf, lneps, rmseps, epsi, WC, WS, biases, ids, d):
    with ExitStack() as ctx:
        def sb(name, shape, dt=F32):
            return ctx.enter_context(nc.sbuf_tensor(name, shape, dt))

        def two(name, shape, dt=F32):
            return [sb(name + "0", shape, dt), sb(name + "1", shape, dt)]

        def bank(name):
            return ctx.enter_context(nc.psum_tensor(name, [P, 512], F32))

        def sem(name):
            return outer.enter_context(nc.semaphore(name))

        eps = sb("s_eps", [P, 1])
        idi = sb("s_idi", [1, 64], I32)
        idf = sb("s_idf", [1, 64])
        ok = sb("s_ok", [1, 64])
        bs = sb("s_bs", [P, 4])
        x_in, small_in, ident_ready, steps = (sem(n) for n in ("s_x_in", "s_small_in", "s_ident", "s_steps"))

        with nc.Block() as block:
            @block.sync
            def _(sp):
                xt = d["x"].rearrange("g (t p) d -> p (g t) d", p=P)
                xs = X[:, :, :, :].rearrange("p j b (t d) -> p (j b t) d", d=D)
                for k in range(0, 64, 8):
                    sp.dma_start(xs[:, k:k + 8, :], xt[:, k:k + 8, :]).then_inc(x_in, 16)
                sp.dma_start(WS[:, :, :], d["WsT"]).then_inc(small_in, 16)
                sp.dma_start(eps[:, :], d["a_eps"].partition_broadcast(P)).then_inc(small_in, 16)
                sp.dma_start(idi[:, :], d["route"]).then_inc(small_in, 16)
                sp.dma_start(bs[:, :], d["bsT"]).then_inc(small_in, 16)
                sp.dma_start(biases[:, 0:EXPERTS0, :], d["brT"]).then_inc(small_in, 16)
                sp.wait_ge(x_in, 16 * 8)

            @block.gpsimd
            def _(pool):
                pool.memset(ident[:, :], 0.0).then_inc(ident_ready, 1)
                pool.wait_ge(ident_ready, 1)
                pool.affine_select(out=ident[:, :], in_=ident[:, :], compare_op=ALU.not_equal, fill=1.0, base=0,
                                   pattern=[[-1, P]], channel_multiplier=1).then_inc(ident_ready, 1)
                pool.memset(mhalf[:, :], -0.5).then_inc(ident_ready, 1)
                pool.memset(lneps[:, :], LN_EPS).then_inc(ident_ready, 1)
                pool.memset(rmseps[:, :], 512 * RMS_EPS).then_inc(ident_ready, 1)

            @block.vector
            def _(dve):
                n = 0

                def step(ins):
                    nonlocal n
                    ins.then_inc(steps, 1)
                    n += 1
                    dve.wait_ge(steps, n)

                dve.wait_ge(small_in, 16 * 5)
                dve.wait_ge(ident_ready, 2)
                step(dve.tensor_scalar(epsi[:, :], ident[:, :], eps[:, 0:1], None, ALU.mult))
                for l in range(2):
                    for k in range(2):
                        w = WS[:, l, k * HID + k * P:k * HID + (k + 1) * P]
                        step(dve.tensor_tensor(w, w, ident[:, :], ALU.add))
                for l in range(2):
                    step(dve.tensor_copy(WC[:, l, EXPERTS0, :], WS[:, l, :]))
                step(dve.tensor_copy(biases[:, EXPERTS0, :], bs[:, :]))
                for e in range(EXPERTS0):
                    step(dve.tensor_tensor(biases[:, e, :], biases[:, e, :], bs[:, :], ALU.add))
                step(dve.tensor_copy(idf[:, :], idi[:, :]))
                step(dve.tensor_scalar(ok[:, :], idf[:, :], 0.0, None, ALU.is_ge))
                step(dve.tensor_scalar(idf[:, :], idf[:, :], float(EXPERTS0), -float(EXPERTS0), ALU.min, ALU.add))
                step(dve.tensor_tensor(idf[:, :], idf[:, :], ok[:, :], ALU.mult))
                step(dve.tensor_scalar(idf[:, :], idf[:, :], float(EXPERTS0), None, ALU.add))
                step(dve.tensor_copy(ids[:, :, :].rearrange("a j b -> a (j b)"), idf[:, :]))


def program(nc, d, out):
    with ExitStack() as outer:
        sb = lambda name, shape, dt=F32: outer.enter_context(nc.sbuf_tensor(name, shape, dt))
        X = sb("X", [P, GRAPHS // 2, 2, TILES * D])
        ident = sb("ident", [P, P])
        mhalf = sb("mhalf", [P, 4])
        lneps = sb("lneps", [P, 4])
        rmseps = sb("rmseps", [P, 4])
        ids = sb("ids", [1, GRAPHS // 2, 4], I32)
        with ExitStack() as ab:
            sb2 = lambda name, shape: ab.enter_context(nc.sbuf_tensor(name, shape, F32))
            epsi = sb2("epsi", [P, P])
            WC = sb2("WC", [P, 2, EXPERTS0 + 1, 2 * HID])
            WS = sb2("WS", [P, 2, 2 * HID])
            biases = sb2("biases", [P, EXPERTS0 + 1, 4])
            setup(nc, outer, X, ident, mhalf, lneps, rmseps, epsi, WC, WS, biases, ids, d)
            gnn0(nc, outer, X, ident, mhalf, lneps, rmseps, epsi, WC, WS, d)
            ffn0(nc, outer, X, ident, mhalf, lneps, WC, biases, ids, d)
        gnn1(nc, outer, X, ident, mhalf, lneps, d)
        weights = sb("weights", [P, GRAPHS // 2, 2, CHOICES * TILES])
        slot_e = sb("slot_e", [1, SLOT_TILES // 2, 2], I32)
        slot_row = sb("slot_row", [1, SLOT_TILES // 2, 2], I32)
        rows_in = nc.dram_tensor("rows_in", (ROWS, ROW), F32).ap()
        rows_out = nc.dram_tensor("rows_out", (CHOICES * TOKENS + PAD_TILES * P, D), F32).ap()
        route(nc, outer, X, ident, mhalf, lneps, weights, slot_e, slot_row, rows_in, d)
        experts(nc, outer, ident, slot_e, slot_row, rows_in, rows_out, d)
        combine(nc, outer, X, weights, rows_out, out)


def kernel(**inputs):
    import numpy as np
    import concourse.bacc as bacc
    from concourse.bass_utils import run_bass_kernel_spmd as run

    v = {k: np.asarray(a) for k, a in inputs.items()}
    c = np.ascontiguousarray
    half = lambda w: w.reshape(*w.shape[:-1], 2, P)
    arrays = {
        "x": v["x"],
        "adj": v["adj"],
        "adjT": c(v["adj"].transpose(0, 2, 1).reshape(GRAPHS, TILES, P, NODES).transpose(0, 2, 1, 3)),
        "a_eps": v["L0_gnn_epsilon"].reshape(1),
        "a_W1": v["L0_gnn_W1"], "a_W2": v["L0_gnn_W2"], "a_b1": v["L0_gnn_b1"], "a_rmsw": v["L0_gnn_rms_weight"],
        "a_b2x2": c(np.stack([v["L0_gnn_b2"]] * 2)),
        "route": v["L0_ffn_route_id"].reshape(1, 64),
        "b_WiT": c(v["L0_ffn_Wi"].T), "b_bi": c(v["L0_ffn_bi"].reshape(2, P).T),
        "WrT": c(half(v["L0_ffn_Wr"]).transpose(4, 0, 1, 3, 2).reshape(P, 2, EXPERTS0, 2 * HID)),
        "WsT": c(half(v["L0_ffn_Ws"][:, 0]).transpose(3, 0, 2, 1).reshape(P, 2, 2 * HID)),
        "brT": c(half(v["L0_ffn_br"]).transpose(3, 1, 0, 2).reshape(P, EXPERTS0, 4)),
        "bsT": c(half(v["L0_ffn_bs"][:, 0]).transpose(2, 0, 1).reshape(P, 4)),
        "b_WoT": c(v["L0_ffn_Wo"].T), "b_box2": c(np.stack([v["L0_ffn_bo"]] * 2)),
        "c_fc_wT": c(v["L1_gnn_fc_w"].reshape(D, HEADS, D).transpose(2, 1, 0)), "c_fp_w": v["L1_gnn_fp_w"],
        "c_fc_bT": c(v["L1_gnn_fc_b"].reshape(HEADS, D).T), "c_qk_w": c(np.concatenate([v["L1_gnn_q_w"], v["L1_gnn_k_w"]], 1)),
        "d_router": v["L1_ffn_Wr"], "d_W1s": v["L1_ffn_W1s"], "d_W2s": v["L1_ffn_W2s"],
        "d_b1sT": c(v["L1_ffn_b1s"].reshape(4, P).T), "d_b2sx2": c(np.stack([v["L1_ffn_b2s"]] * 2)),
        "e_W1": v["L1_ffn_W1p"], "e_W2": v["L1_ffn_W2p"], "e_b1": v["L1_ffn_b1p"], "e_b2": v["L1_ffn_b2p"],
        "c_q_b": v["L1_gnn_q_b"], "c_k_b": v["L1_gnn_k_b"], "c_fp_bx2": c(np.stack([v["L1_gnn_fp_b"]] * 2)),
    }
    nc = bacc.Bacc("TRN2", target_bir_lowering=False, num_devices=1)
    d = {k: nc.dram_tensor("in_" + k, a.shape, mybir.dt.from_np(a.dtype), kind="ExternalInput").ap() for k, a in arrays.items()}
    out = nc.dram_tensor("out", (GRAPHS, NODES, D), F32, kind="ExternalOutput").ap()
    program(nc, d, out)
    r = run(nc, [{"in_" + k: c(a) for k, a in arrays.items()}], core_ids=[0])
    return r.results[0]["out"]
```

```python
from contextlib import ExitStack

import concourse.bass as bass
from concourse import mybir

F32 = mybir.dt.float32
BF16 = mybir.dt.bfloat16
I32 = mybir.dt.int32
ALU = mybir.AluOpType
ACT = mybir.ActivationFunctionType
AX = mybir.AxisListType

P = 128
GRAPHS = 32
TILES = 2
D = 128
NODES = P * TILES
LN_EPS = 1e-5
RMS_EPS = 1e-6


def pair(g):
    return g[0]


def par(g):
    return g[1]


def number(g):
    return 2 * g[0] + g[1]


def graph(i):
    return i // 2, i % 2


def count(g, each, k=None, back=0):
    n = each * (number(g) - back) + (each if k is None else k)
    return 0 if isinstance(n, int) and number(g) < back else n


def loads(g, back=0):
    return 16 * (pair(g) - back) + 16


def sweep(eng, depth, body, units=GRAPHS):
    first = (depth + 3) // 2 * 2

    def peeled(i):
        return lambda lag: graph(i - lag) if 0 <= i - lag < units else None

    for i in range(first):
        body(peeled(i))
    with eng.Fori(first // 2, units // 2) as j:
        for q in (0, 1):
            body(lambda lag: (j + (q - lag) // 2, (q - lag) % 2))
    for i in range(units, units + depth):
        body(peeled(i))


def one(ap):
    return ap.rearrange("p a d -> p (a d)")


def graph_rows(X, g):
    return one(X[:, bass.ds(pair(g), 1), par(g), :])


def transpose(nc, out, in_, ident):
    return nc.tensor.transpose(out, in_, ident)


def gnn0(nc, outer, X, ident, mhalf, lneps, rmseps, epsi, WC, WS, d):
    with ExitStack() as ctx:
        def sb(name, shape, dt=F32):
            return ctx.enter_context(nc.sbuf_tensor(name, shape, dt))

        def two(name, shape, dt=F32):
            return [sb(name + "0", shape, dt), sb(name + "1", shape, dt)]

        def bank(name):
            return ctx.enter_context(nc.psum_tensor(name, [P, 512], F32))

        def sem(name):
            return outer.enter_context(nc.semaphore(name))

        W1 = sb("a_W1", [P, 512])
        W2 = sb("a_W2", [P, 4, D])
        b1 = sb("a_b1", [P, 512])
        rmsw = sb("a_rmsw", [P, 512])
        b2 = sb("a_b2", [P, 2, D])
        AT = two("a_AT", [P, TILES, NODES])
        st = two("a_st", [P, TILES, 6])
        mv = two("a_mv", [P, TILES, 2])
        ve = two("a_ve", [P, TILES])
        rstd = two("a_rstd", [P, TILES])
        xln = two("a_xln", [P, TILES, D])
        aggT = two("a_aggT", [P, NODES])
        hb = two("a_hb", [P, TILES, 512])
        hn = two("a_hn", [P, TILES, 512])
        junk = two("a_junk", [P, TILES, 512])
        ssq = two("a_ssq", [P, TILES])
        ms = two("a_ms", [P, TILES])
        rr = two("a_rr", [P, TILES])
        hT = two("a_hT", [P, TILES, 4, P])
        tmp = two("a_tmp", [P, NODES])
        p_agg = bank("a_pagg")
        p_h = [bank("a_ph0"), bank("a_ph1")]
        p_t = [bank("a_pt0"), bank("a_pt1")]
        p_out = bank("a_pout")

        weights_in = sem("a_weights_in")
        rms_weight = sem("a_rms_weight")
        adj_in = [sem("a_adj_in0"), sem("a_adj_in1")]
        wr_in = [sem("a_wr_in0"), sem("a_wr_in1")]
        stats = sem("a_stats")
        scale = sem("a_scale")
        normed = sem("a_normed")
        self_loop = sem("a_self_loop")
        wr_sum = sem("a_wr_sum")
        agg = sem("a_agg")
        agg_sb = sem("a_agg_sb")
        hidden = sem("a_hidden")
        biased = sem("a_biased")
        squares = sem("a_squares")
        rms = sem("a_rms")
        scaled = sem("a_scaled")
        silu = sem("a_silu")
        turned = sem("a_turned")
        turned_sb = sem("a_turned_sb")
        product = sem("a_product")
        added = sem("a_added")

        adjT = d["adjT"].rearrange("(j b) p c n -> j b p c n", b=2)
        wr = d["WrT"].rearrange("p l e n -> l p e n")
        weight_dmas = 5

        with nc.Block() as block:
            @block.sync
            def _(sp):
                sp.dma_start(W1[:, :], d["a_W1"]).then_inc(weights_in, 16)
                sp.dma_start(W2[:, :, :], d["a_W2"].rearrange("(f p) n -> p f n", p=P)).then_inc(weights_in, 16)
                sp.dma_start(b1[:, :], d["a_b1"].partition_broadcast(P)).then_inc(weights_in, 16)
                sp.dma_start(rmsw[:, :], d["a_rmsw"].partition_broadcast(P)).then_inc(weights_in, 16)
                sp.dma_start(b2[:, :, :], d["a_b2x2"].partition_broadcast(P)).then_inc(weights_in, 16)

                def body(at):
                    if g := at(0):
                        sp.wait_ge(agg, count(g, 1, back=2))
                        sp.wait_ge(self_loop, count(g, 2, back=2))
                        sp.dma_start(AT[par(g)][:, :, :], adjT[bass.ds(pair(g), 1), par(g)].rearrange("a p c n -> (a p) c n")).then_inc(adj_in[par(g)], 16)
                        sp.wait_ge(wr_sum, count(g, 1, back=2))
                        sp.dma_start(WC[:, par(g), bass.ds(pair(g), 1), :], wr[par(g), :, bass.ds(pair(g), 1), :]).then_inc(wr_in[par(g)], 16)

                sweep(sp, 0, body)

            @block.vector
            def _(dve):
                dve.wait_ge(weights_in, 16 * weight_dmas)
                dve.tensor_scalar(rmsw[:, :], rmsw[:, :], 512 ** 0.5, None, ALU.mult).then_inc(rms_weight, 1)
                dve.wait_ge(rms_weight, 1)

                def body(at):
                    if g := at(1):
                        x = graph_rows(X, g)
                        dve.wait_ge(scale, count(g, 2))
                        dve.wait_ge(agg, count(g, 1, back=2))
                        for t in range(TILES):
                            dve.tensor_scalar(xln[par(g)][:, t, :], x[:, t * D:(t + 1) * D], mv[par(g)][:, t, 0:1],
                                                        rstd[par(g)][:, t:t + 1], ALU.subtract, ALU.mult).then_inc(normed, 1)
                    if g := at(0):
                        x = graph_rows(X, g)
                        for t in range(TILES):
                            dve.bn_stats(st[par(g)][:, t, :], x[:, t * D:(t + 1) * D]).then_inc(stats, 1)
                    if g := at(0):
                        dve.wait_ge(stats, count(g, 4, TILES))
                    if g := at(6):
                        x = graph_rows(X, g)
                        dve.wait_ge(product, count(g, 1))
                        dve.tensor_tensor(tmp[par(g)][:, :], p_out[:, 0:NODES], b2[:, :, :].rearrange("p a d -> p (a d)"), ALU.add).then_inc(added, 1)
                        dve.wait_ge(added, count(g, 2, 1))
                        dve.tensor_tensor(x, x, tmp[par(g)][:, :], ALU.add).then_inc(added, 1)
                    if g := at(0):
                        for t in range(TILES):
                            dve.bn_aggr(mv[par(g)][:, t, :], st[par(g)][:, t, :]).then_inc(stats, 1)
                    if g := at(3):
                        dve.wait_ge(rms, count(g, 2))
                        dve.wait_ge(biased, count(g, 2))
                        dve.wait_ge(turned, count(g, 2, back=2))
                        for t in range(TILES):
                            dve.scalar_tensor_tensor(out=hn[par(g)][:, t, :], in0=hb[par(g)][:, t, :],
                                                               scalar=rr[par(g)][:, t:t + 1], in1=rmsw[:, :],
                                                               op0=ALU.mult, op1=ALU.mult).then_inc(scaled, 1)
                    if g := at(2):
                        dve.wait_ge(squares, count(g, 2, back=2))
                        for t in range(TILES):
                            dve.wait_ge(hidden, count(g, 2, t + 1))
                            dve.tensor_tensor(hb[par(g)][:, t, :], p_h[t][:, :], b1[:, :], ALU.add).then_inc(biased, 1)

                sweep(dve, 6, body)

            @block.gpsimd
            def _(pool):
                def body(at):
                    if g := at(0):
                        pool.wait_ge(stats, count(g, 4))
                        pool.tensor_tensor(ve[par(g)][:, :], mv[par(g)][:, :, 1], lneps[:, 0:TILES], ALU.add).then_inc(scale, 1)
                        pool.wait_ge(scale, count(g, 2, 1))
                        pool.wait_ge(normed, count(g, 2, back=2))
                        pool.tensor_tensor(rstd[par(g)][:, :], ve[par(g)][:, :], mhalf[:, 0:TILES], ALU.pow).then_inc(scale, 1)
                        pool.wait_ge(adj_in[par(g)], loads(g))
                        for t in range(TILES):
                            a = AT[par(g)][:, t, t * P:(t + 1) * P]
                            pool.tensor_tensor(a, a, epsi[:, :], ALU.add).then_inc(self_loop, 1)
                        pool.wait_ge(wr_in[par(g)], loads(g))
                        w = one(WC[:, par(g), bass.ds(pair(g), 1), :])
                        pool.tensor_tensor(w, w, WS[:, par(g), :], ALU.add).then_inc(wr_sum, 1)
                    if g := at(2):
                        pool.wait_ge(squares, count(g, 2))
                        pool.tensor_tensor(ms[par(g)][:, :], ssq[par(g)][:, :], rmseps[:, 0:TILES], ALU.add).then_inc(rms, 1)
                        pool.wait_ge(rms, count(g, 2, 1))
                        pool.wait_ge(scaled, count(g, 2, back=2))
                        pool.tensor_tensor(rr[par(g)][:, :], ms[par(g)][:, :], mhalf[:, 0:TILES], ALU.pow).then_inc(rms, 1)

                sweep(pool, 2, body)

            @block.scalar
            def _(act):
                def body(at):
                    if g := at(1):
                        act.wait_ge(agg, count(g, 1))
                        act.wait_ge(hidden, count(g, 2, back=2))
                        act.copy(aggT[par(g)][:, :], p_agg[:, 0:NODES]).then_inc(agg_sb, 1)
                    if g := at(2):
                        for t in range(TILES):
                            act.wait_ge(biased, count(g, 2, t + 1))
                            act.wait_ge(rms, count(g, 2, back=2))
                            act.activation(junk[par(g)][:, t, :], hb[par(g)][:, t, :], ACT.Square, accum_out=ssq[par(g)][:, t:t + 1]).then_inc(squares, 1)
                    if g := at(3):
                        for t in range(TILES):
                            act.wait_ge(scaled, count(g, 2, t + 1))
                            act.activation(hn[par(g)][:, t, :], hn[par(g)][:, t, :], ACT.Silu).then_inc(silu, 1)
                    if g := at(4):
                        act.wait_ge(product, count(g, 1, back=2))
                        for t in range(TILES):
                            act.wait_ge(turned, count(g, 2, t + 1))
                            act.copy(hT[par(g)][:, t, :, :].rearrange("p f n -> p (f n)"), p_t[t][:, :]).then_inc(turned_sb, 1)

                sweep(act, 4, body)

            @block.tensor
            def _(pe):
                pe.wait_ge(weights_in, 16 * weight_dmas)

                def body(at):
                    if g := at(1):
                        pe.wait_ge(normed, count(g, 2))
                        pe.wait_ge(self_loop, count(g, 2))
                        pe.wait_ge(agg_sb, count(g, 1, back=1))
                        for t in range(TILES):
                            mm = nc.tensor.matmul(p_agg[:, 0:NODES], xln[par(g)][:, t, :], AT[par(g)][:, t, :],
                                                  start=(t == 0), stop=(t == TILES - 1))
                        mm.then_inc(agg, 1)
                    if g := at(2):
                        pe.wait_ge(agg_sb, count(g, 1))
                        for t in range(TILES):
                            pe.wait_ge(biased, count(g, 2, t + 1, back=1))
                            nc.tensor.matmul(p_h[t][:, :], aggT[par(g)][:, t * P:(t + 1) * P], W1[:, :], start=True, stop=True).then_inc(hidden, 1)
                    if g := at(4):
                        for t in range(TILES):
                            pe.wait_ge(silu, count(g, 2, t + 1))
                            pe.wait_ge(turned_sb, count(g, 2, t + 1, back=1))
                            for f in range(4):
                                mm = transpose(nc, p_t[t][:, f * P:(f + 1) * P], hn[par(g)][:, t, f * P:(f + 1) * P], ident[:, :])
                            mm.then_inc(turned, 1)
                    if g := at(5):
                        pe.wait_ge(turned_sb, count(g, 2))
                        pe.wait_ge(added, count(g, 2, 1, back=1))
                        for t in range(TILES):
                            for f in range(4):
                                mm = nc.tensor.matmul(p_out[:, t * D:(t + 1) * D], hT[par(g)][:, t, f, :], W2[:, f, :],
                                                      start=(f == 0), stop=(f == 3))
                        mm.then_inc(product, 1)

                sweep(pe, 5, body)


EXPERTS0 = 16
HID = 256


def ffn0(nc, outer, X, ident, mhalf, lneps, WC, biases, ids, d):
    with ExitStack() as ctx:
        def sb(name, shape, dt=F32):
            return ctx.enter_context(nc.sbuf_tensor(name, shape, dt))

        def two(name, shape, dt=F32):
            return [sb(name + "0", shape, dt), sb(name + "1", shape, dt)]

        def bank(name):
            return ctx.enter_context(nc.psum_tensor(name, [P, 512], F32))

        def sem(name):
            return outer.enter_context(nc.semaphore(name))

        Wi = sb("b_Wi", [P, HID])
        bi = sb("b_bi", [P, 2])
        Wo = sb("b_Wo", [P, 2, D])
        bo = sb("b_bo", [P, 2, D])
        st = two("b_st", [P, TILES, 6])
        mv = two("b_mv", [P, TILES, 2])
        ve = two("b_ve", [P, TILES])
        rstd = two("b_rstd", [P, TILES])
        xln = two("b_xln", [P, TILES, D])
        xT = two("b_xT", [P, NODES])
        hT = [two(f"b_hT{l}", [P, 2, NODES]) for l in range(3)]
        y = [two(f"b_y{l}", [P, TILES, HID]) for l in range(2)]
        tmp = two("b_tmp", [P, NODES])
        p_x = bank("b_px")
        p_h = bank("b_ph")
        p_y = [bank("b_py0"), bank("b_py1")]
        p_t = [bank("b_pt0"), bank("b_pt1")]
        p_out = bank("b_pout")

        weights_in = sem("b_weights_in")
        stats = sem("b_stats")
        scale = sem("b_scale")
        normed = sem("b_normed")
        x_turned = sem("b_x_turned")
        x_sb = sem("b_x_sb")
        first = sem("b_first")
        layer = [sem(f"b_layer{l}") for l in range(2)]
        layer_sb = [sem(f"b_layer_sb{l}") for l in range(2)]
        turned = [sem(f"b_turned{l}") for l in range(2)]
        relu = [sem(f"b_relu{l}") for l in range(3)]
        product = sem("b_product")
        added = sem("b_added")

        with nc.Block() as block:
            @block.sync
            def _(sp):
                sp.dma_start(Wi[:, :], d["b_WiT"]).then_inc(weights_in, 16)
                sp.dma_start(bi[:, :], d["b_bi"]).then_inc(weights_in, 16)
                sp.dma_start(Wo[:, :, :], d["b_WoT"].rearrange("(k p) n -> p k n", p=P)).then_inc(weights_in, 16)
                sp.dma_start(bo[:, :, :], d["b_box2"].partition_broadcast(P)).then_inc(weights_in, 16)

            @block.vector
            def _(dve):
                dve.wait_ge(weights_in, 64)

                def body(at):
                    if g := at(0):
                        x = graph_rows(X, g)
                        for t in range(TILES):
                            dve.bn_stats(st[par(g)][:, t, :], x[:, t * D:(t + 1) * D]).then_inc(stats, 1)
                        dve.wait_ge(stats, count(g, 4, TILES))
                    if g := at(1):
                        x = graph_rows(X, g)
                        dve.wait_ge(scale, count(g, 2))
                        dve.wait_ge(x_turned, count(g, 1, back=2))
                        for t in range(TILES):
                            dve.tensor_scalar(xln[par(g)][:, t, :], x[:, t * D:(t + 1) * D], mv[par(g)][:, t, 0:1],
                                                        rstd[par(g)][:, t:t + 1], ALU.subtract, ALU.mult).then_inc(normed, 1)
                    if g := at(0):
                        for t in range(TILES):
                            dve.bn_aggr(mv[par(g)][:, t, :], st[par(g)][:, t, :]).then_inc(stats, 1)
                    for l in range(2):
                        if g := at(4 + 2 * l):
                            dve.wait_ge(layer[l], count(g, 1))
                            dve.wait_ge(turned[l], count(g, 1, back=2))
                            dve.tensor_copy(y[l][par(g)][:, :, :].rearrange("p t n -> p (t n)"), p_y[l][:, :]).then_inc(layer_sb[l], 1)
                    if g := at(8):
                        x = graph_rows(X, g)
                        dve.wait_ge(product, count(g, 1))
                        dve.tensor_tensor(tmp[par(g)][:, :], p_out[:, 0:NODES], bo[:, :, :].rearrange("p a d -> p (a d)"), ALU.add).then_inc(added, 1)
                        dve.wait_ge(added, count(g, 2, 1))
                        dve.tensor_tensor(x, x, tmp[par(g)][:, :], ALU.add).then_inc(added, 1)

                sweep(dve, 8, body)

            @block.gpsimd
            def _(pool):
                def body(at):
                    if g := at(0):
                        pool.wait_ge(stats, count(g, 4))
                        pool.tensor_tensor(ve[par(g)][:, :], mv[par(g)][:, :, 1], lneps[:, 0:TILES], ALU.add).then_inc(scale, 1)
                        pool.wait_ge(scale, count(g, 2, 1))
                        pool.wait_ge(normed, count(g, 2, back=2))
                        pool.tensor_tensor(rstd[par(g)][:, :], ve[par(g)][:, :], mhalf[:, 0:TILES], ALU.pow).then_inc(scale, 1)

                sweep(pool, 0, body)

            @block.scalar
            def _(act):
                act.wait_ge(weights_in, 64)

                def body(at):
                    if g := at(2):
                        act.wait_ge(x_turned, count(g, 1))
                        act.wait_ge(first, count(g, 1, back=2))
                        act.copy(xT[par(g)][:, :], p_x[:, 0:NODES]).then_inc(x_sb, 1)
                    if g := at(3):
                        act.wait_ge(first, count(g, 1))
                        act.wait_ge(layer[0], count(g, 1, back=2))
                        for k in range(2):
                            act.activation(hT[0][par(g)][:, k, :], p_h[:, k * NODES:(k + 1) * NODES], ACT.Relu, bias=bi[:, k:k + 1]).then_inc(relu[0], 1)
                    for l in range(2):
                        if g := at(5 + 2 * l):
                            act.wait_ge(turned[l], count(g, 1))
                            act.wait_ge((product if l else layer[1]), count(g, 1, back=2))
                            for t in range(TILES):
                                e = act.value_load(ids[0:1, bass.ds(pair(g), 1), par(g) * 2 + t], min_val=0, max_val=EXPERTS0)
                                for k in range(2):
                                    act.activation(hT[l + 1][par(g)][:, k, t * P:(t + 1) * P],
                                                                  p_t[l][:, (2 * k + t) * P:(2 * k + t + 1) * P], ACT.Relu,
                                                                  bias=biases[:, bass.ds(e, 1), 2 * l + k]).then_inc(relu[l + 1], 1)

                sweep(act, 7, body)

            @block.tensor
            def _(pe):
                pe.wait_ge(weights_in, 64)

                def body(at):
                    if g := at(2):
                        pe.wait_ge(normed, count(g, 2))
                        pe.wait_ge(x_sb, count(g, 1, back=1))
                        for t in range(TILES):
                            mm = transpose(nc, p_x[:, t * P:(t + 1) * P], xln[par(g)][:, t, :], ident[:, :])
                        mm.then_inc(x_turned, 1)
                    if g := at(3):
                        pe.wait_ge(x_sb, count(g, 1))
                        pe.wait_ge(relu[0], count(g, 2, back=1))
                        for k in range(2):
                            mm = nc.tensor.matmul(p_h[:, k * NODES:(k + 1) * NODES], Wi[:, k * P:(k + 1) * P], xT[par(g)][:, :], start=True, stop=True)
                        mm.then_inc(first, 1)
                    for l in range(2):
                        if g := at(4 + 2 * l):
                            pe.wait_ge(relu[l], count(g, (4 if l else 2)))
                            pe.wait_ge(layer_sb[l], count(g, 1, back=1))
                            for t in range(TILES):
                                e = pe.value_load(ids[0:1, bass.ds(pair(g), 1), par(g) * 2 + t], min_val=0, max_val=EXPERTS0)
                                for k in range(2):
                                    mm = nc.tensor.matmul(p_y[l][:, t * HID:(t + 1) * HID], hT[l][par(g)][:, k, t * P:(t + 1) * P],
                                                          one(WC[:, l, bass.ds(e, 1), k * HID:(k + 1) * HID]), start=(k == 0), stop=(k == 1))
                            mm.then_inc(layer[l], 1)
                        if g := at(5 + 2 * l):
                            pe.wait_ge(layer_sb[l], count(g, 1))
                            pe.wait_ge(relu[l + 1], count(g, 4, back=1))
                            for t in range(TILES):
                                for k in range(2):
                                    mm = transpose(nc, p_t[l][:, (2 * k + t) * P:(2 * k + t + 1) * P], y[l][par(g)][:, t, k * P:(k + 1) * P], ident[:, :])
                            mm.then_inc(turned[l], 1)
                    if g := at(8):
                        pe.wait_ge(relu[2], count(g, 4))
                        pe.wait_ge(added, count(g, 2, 1, back=1))
                        for t in range(TILES):
                            for k in range(2):
                                mm = nc.tensor.matmul(p_out[:, t * D:(t + 1) * D], hT[2][par(g)][:, k, t * P:(t + 1) * P], Wo[:, k, :],
                                                      start=(k == 0), stop=(k == 1))
                        mm.then_inc(product, 1)

                sweep(pe, 8, body)


HEADS = 8
NEG = -1e9
PARTS = 3
LEAK = 0.01


def gnn1(nc, outer, X, ident, mhalf, lneps, d):
    with ExitStack() as ctx:
        def sb(name, shape, dt=F32):
            return ctx.enter_context(nc.sbuf_tensor(name, shape, dt))

        def two(name, shape, dt=F32):
            return [sb(name + "0", shape, dt), sb(name + "1", shape, dt)]

        def bank(name):
            return ctx.enter_context(nc.psum_tensor(name, [P, 512], F32))

        def sem(name):
            return outer.enter_context(nc.semaphore(name))

        values_w = sb("c_values_w", [P, HEADS * D])
        qk_w = sb("c_qk_w", [P, P])
        qk_c = sb("c_qk_c", [P, 1])
        out_c = sb("c_out_c", [P, TILES, D])
        pick = sb("c_pick", [P, HEADS], BF16)
        is_key = sb("c_is_key", [P, 1])
        no_key = sb("c_no_key", [P, 1])
        part1 = sb("c_part1", [P, 1])
        part2 = sb("c_part2", [P, 1])
        gnn1_weights(nc, outer, values_w, qk_w, qk_c, out_c, pick, is_key, no_key, part1, part2, d)

        AN = two("c_AN", [P, TILES, NODES])
        mask = two("c_mask", [P, TILES, NODES])
        st = two("c_st", [P, TILES, 6])
        mv = two("c_mv", [P, TILES, 2])
        ve = two("c_ve", [P, TILES])
        rstd = two("c_rstd", [P, TILES])
        f = two("c_f", [P, TILES * D])
        residual = sb("c_residual", [P, GRAPHS // 2, 2, TILES * D])
        fT = two("c_fT", [P, NODES])
        fT_late = two("c_fT_late", [P, NODES])
        rest = sb("c_rest", [P, NODES])
        part = sb("c_part", [P, NODES], BF16)
        qkT = sb("c_qkT", [P, NODES], BF16)
        keysT = two("c_keysT", [P, NODES], BF16)
        queriesT = two("c_queriesT", [P, NODES], BF16)
        head_keys = two("c_head_keys", [P, HEADS, NODES], BF16)
        top = two("c_top", [P, TILES * HEADS])
        peak = two("c_peak", [P, TILES * HEADS])
        shift = two("c_shift", [P, TILES * HEADS])
        L = two("c_L", [P, TILES, HEADS, NODES])
        E = two("c_E", [P, TILES, HEADS, NODES])
        total = two("c_total", [P, TILES * HEADS])
        inv = two("c_inv", [P, TILES * HEADS])
        V = two("c_V", [P, TILES, HEADS * D])
        ET = two("c_ET", [P, 512])
        z = two("c_z", [P, NODES])
        th = two("c_th", [P, NODES])
        sg = two("c_sg", [P, NODES])
        p_x = bank("c_px")
        p_qk = bank("c_pqk")
        p_k = [bank("c_pk0"), bank("c_pk1")]
        p_v = bank("c_pv")
        p_e = [bank("c_pe0"), bank("c_pe1")]
        p_out = bank("c_pout")

        adj_in = [sem("c_adj_in0"), sem("c_adj_in1")]
        stats = sem("c_stats")
        scale = sem("c_scale")
        masked = sem("c_masked")
        normed = sem("c_normed")
        kept = sem("c_kept")
        x_turned = sem("c_x_turned")
        x_sb = sem("c_x_sb")
        x_late = sem("c_x_late")
        qk = sem("c_qk")
        split = sem("c_split")
        headed = sem("c_headed")
        keys = sem("c_keys")
        summed = sem("c_summed")
        leaky = sem("c_leaky")
        shift_ready = sem("c_shift_ready")
        exped = sem("c_exped")
        inverse = sem("c_inverse")
        weighted = sem("c_weighted")
        values = sem("c_values")
        values_sb = sem("c_values_sb")
        e_turned = sem("c_e_turned")
        e_sb = sem("c_e_sb")
        attended = sem("c_attended")
        z_ready = sem("c_z_ready")
        tanh = sem("c_tanh")
        added = sem("c_added")

        adj = d["adj"].rearrange("(j b) (t p) m -> j b p t m", b=2, p=P)

        with nc.Block() as block:
            @block.sync
            def _(sp):
                def body(at):
                    if g := at(0):
                        sp.wait_ge(masked, count(g, 1, back=2))
                        sp.dma_start(AN[par(g)][:, :, :], adj[bass.ds(pair(g), 1), par(g)].rearrange("a p t m -> (a p) t m")).then_inc(adj_in[par(g)], 16)

                sweep(sp, 0, body)

            @block.vector
            def _(dve):
                def body(at):
                    g0, g3, g4, g5, g8 = at(0), at(3), at(4), at(5), at(8)

                    def maxima(h):
                        if g := g4:
                            for t in range(TILES):
                                n = t * HEADS + h
                                dve.tensor_tensor_reduce(L[par(g)][:, t, h, :], p_k[h % 2][:, t * NODES:(t + 1) * NODES],
                                                                   mask[par(g)][:, t, :], 1.0, -3.4e38, ALU.add, ALU.max, top[par(g)][:, n:n + 1]).then_inc(summed, 1)

                    def leak(h):
                        if g := g4:
                            dve.wait_ge(summed, count(g, 16, 2 * h + 2))
                            e = L[par(g)][:, :, h, :]
                            dve.scalar_tensor_tensor(out=e, in0=e, scalar=LEAK, in1=e, op0=ALU.mult, op1=ALU.max).then_inc(leaky, 1)

                    def split_step(k):
                        if g := g3:
                            if k:
                                dve.wait_ge(split, count(g, 7, k))
                            if k == 0:
                                dve.wait_ge(split, count(g, 7, back=1))
                                dve.wait_ge(qk, count(g, 1))
                                dve.tensor_scalar(rest[:, :], p_qk[:, 0:NODES], qk_c[:, 0:1], None, ALU.add).then_inc(split, 1)
                            elif k == 2:
                                dve.scalar_tensor_tensor(out=rest[:, :], in0=part[:, :], scalar=part1[:, 0:1], in1=rest[:, :],
                                                         op0=ALU.mult, op1=ALU.add).then_inc(split, 1)
                            elif k == 4:
                                dve.scalar_tensor_tensor(out=qkT[:, :], in0=part[:, :], scalar=part2[:, 0:1], in1=rest[:, :],
                                                         op0=ALU.mult, op1=ALU.add).then_inc(split, 1)
                            elif k == 5:
                                dve.wait_ge(headed, count(g, 1, back=2))
                                dve.tensor_scalar(keysT[par(g)][:, :], qkT[:, :], is_key[:, 0:1], no_key[:, 0:1], ALU.mult, ALU.add).then_inc(split, 1)
                            elif k == 6:
                                dve.wait_ge(keys, count(g, 8, back=2))
                                dve.tensor_scalar(queriesT[par(g)][:, :], qkT[:, :], no_key[:, 0:1], is_key[:, 0:1], ALU.mult, ALU.add).then_inc(split, 1)
                            else:
                                dve.tensor_copy(part[:, :], rest[:, :]).then_inc(split, 1)

                    if g := at(6):
                        dve.wait_ge(exped, count(g, 16))
                        dve.wait_ge(weighted, count(g, 2, back=2))
                        dve.reciprocal(inv[par(g)][:, HEADS:], total[par(g)][:, HEADS:]).then_inc(inverse, 1)
                    if g := at(7):
                        dve.wait_ge(attended, count(g, 8))
                        dve.wait_ge(kept, count(g, 1))
                        dve.wait_ge(tanh, count(g, 1, back=2))
                        dve.tensor_tensor(z[par(g)][:, :], p_out[:, 0:NODES], graph_rows(residual, g), ALU.add).then_inc(z_ready, 1)
                    if g := g0:
                        x = graph_rows(X, g)
                        for t in range(TILES):
                            dve.bn_stats(st[par(g)][:, t, :], x[:, t * D:(t + 1) * D]).then_inc(stats, 1)
                    split_step(0)
                    if g := g4:
                        dve.wait_ge(adj_in[par(g)], loads(g))
                        dve.tensor_scalar(mask[par(g)][:, :, :].rearrange("p t m -> p (t m)"), AN[par(g)][:, :, :].rearrange("p t m -> p (t m)"),
                                                    1.0, -NEG, ALU.subtract, ALU.mult).then_inc(masked, 1)
                        dve.wait_ge(exped, count(g, 16, back=2))
                        dve.wait_ge(masked, count(g, 1))
                        dve.wait_ge(keys, count(g, 8, 1))
                        dve.wait_ge(x_sb, count(g, 1))
                        dve.wait_ge(values, count(g, 4, back=2))
                        dve.tensor_copy(fT_late[par(g)][:, :], fT[par(g)][:, :]).then_inc(x_late, 1)
                    maxima(0)
                    split_step(1)
                    if g := g4:
                        dve.wait_ge(keys, count(g, 8, 2))
                    if g := g0:
                        dve.wait_ge(stats, count(g, 4, TILES))
                    if g := at(1):
                        x = graph_rows(X, g)
                        dve.wait_ge(scale, count(g, 2))
                        dve.wait_ge(x_turned, count(g, 1, back=2))
                        dve.wait_ge(kept, count(g, 1, back=2))
                        for t in range(TILES):
                            dve.tensor_scalar(f[par(g)][:, t * D:(t + 1) * D], x[:, t * D:(t + 1) * D], mv[par(g)][:, t, 0:1],
                                                        rstd[par(g)][:, t:t + 1], ALU.subtract, ALU.mult).then_inc(normed, 1)
                    maxima(1)
                    if g := g0:
                        for t in range(TILES):
                            dve.bn_aggr(mv[par(g)][:, t, :], st[par(g)][:, t, :]).then_inc(stats, 1)
                    for h in range(2, HEADS):
                        if h < 7:
                            split_step(h)
                        if (g := g8) and h == 3:
                            dve.wait_ge(tanh, count(g, 1))
                            dve.tensor_scalar(sg[par(g)][:, :], th[par(g)][:, :], 0.5, 0.5, ALU.mult, ALU.add).then_inc(added, 1)
                        if (g := g8) and h == 4:
                            x = graph_rows(X, g)
                            dve.wait_ge(added, count(g, 2, 1))
                            dve.tensor_tensor(x, x, sg[par(g)][:, :], ALU.add).then_inc(added, 1)
                        if (g := g5) and h == 5:
                            dve.wait_ge(exped, count(g, 16, HEADS))
                            dve.wait_ge(weighted, count(g, 2, 1, back=2))
                            dve.reciprocal(inv[par(g)][:, 0:HEADS], total[par(g)][:, 0:HEADS]).then_inc(inverse, 1)
                        if g := g4:
                            dve.wait_ge(keys, count(g, 8, h + 1))
                        leak(h - 2)
                        maxima(h)
                    leak(6)
                    if g := g4:
                        dve.wait_ge(summed, count(g, 16))
                        dve.scalar_tensor_tensor(out=peak[par(g)][:, :], in0=top[par(g)][:, :], scalar=LEAK, in1=top[par(g)][:, :],
                                                                op0=ALU.mult, op1=ALU.max).then_inc(shift_ready, 1)
                    leak(7)
                    if g := g4:
                        dve.wait_ge(shift_ready, count(g, 2, 1))
                        dve.tensor_scalar(shift[par(g)][:, :], peak[par(g)][:, :], -1.0, None, ALU.mult).then_inc(shift_ready, 1)

                sweep(dve, 8, body)

            @block.gpsimd
            def _(pool):
                def body(at):
                    for t, g in ((1, at(6)), (0, at(5))):
                        if (h := at(3)) and t == 0:
                            pool.wait_ge(keys, count(h, 8, back=2))
                            pool.wait_ge(split, count(h, 7, 6))
                            pool.tensor_tensor(head_keys[par(h)][:, :, :], keysT[par(h)][:, :].unsqueeze(1).to_broadcast([P, HEADS, NODES]),
                                               pick[:, :].unsqueeze(2).to_broadcast([P, HEADS, NODES]), ALU.mult).then_inc(headed, 1)
                        if g:
                            pool.wait_ge(inverse, count(g, 2, t + 1))
                            e = E[par(g)][:, t, :, :]
                            w = inv[par(g)][:, t * HEADS:(t + 1) * HEADS].unsqueeze(2).to_broadcast([P, HEADS, NODES])
                            pool.tensor_tensor(e, e, w, ALU.mult).then_inc(weighted, 1)
                    if g := at(0):
                        pool.wait_ge(stats, count(g, 4))
                        pool.tensor_tensor(ve[par(g)][:, :], mv[par(g)][:, :, 1], lneps[:, 0:TILES], ALU.add).then_inc(scale, 1)
                        pool.wait_ge(scale, count(g, 2, 1))
                        pool.wait_ge(normed, count(g, 2, back=2))
                        pool.tensor_tensor(rstd[par(g)][:, :], ve[par(g)][:, :], mhalf[:, 0:TILES], ALU.pow).then_inc(scale, 1)
                    if g := at(1):
                        pool.wait_ge(normed, count(g, 2))
                        pool.tensor_tensor(graph_rows(residual, g), f[par(g)][:, :], out_c[:, :, :].rearrange("p t d -> p (t d)"), ALU.add).then_inc(kept, 1)

                sweep(pool, 6, body)

            @block.scalar
            def _(act):
                def body(at):
                    g5, g6 = at(5), at(6)
                    for w in range(8):
                        if g := g6:
                            act.wait_ge(e_turned, count(g, 8, w + 1))
                            if w < 2:
                                act.wait_ge(attended, count(g, 8, w + 7, back=1))
                            else:
                                act.wait_ge(attended, count(g, 8, w - 1))
                            act.copy(ET[w % 2][:, :], p_e[w % 2][:, :]).then_inc(e_sb, 1)
                        if g := g5:
                            if w % 2 == 1:
                                u = w // 2
                                act.wait_ge(values, count(g, 4, u + 1))
                                act.wait_ge(attended, count(g, 8, back=2))
                                act.copy(V[par(g)][:, u // 2, (u % 2) * 512:(u % 2 + 1) * 512], p_v[:, :]).then_inc(values_sb, 1)
                            if w == 0:
                                act.wait_ge(shift_ready, count(g, 2))
                                act.wait_ge(leaky, count(g, 8))
                                act.wait_ge(e_turned, count(g, 8, back=2))
                                act.wait_ge(inverse, count(g, 2, back=2))
                            for n in (2 * w, 2 * w + 1):
                                t, h = n // HEADS, n % HEADS
                                act.activation(E[par(g)][:, t, h, :], L[par(g)][:, t, h, :], ACT.Exp, bias=shift[par(g)][:, n:n + 1],
                                                        accum_out=total[par(g)][:, n:n + 1]).then_inc(exped, 1)
                        if (g := at(2)) and w == 1:
                            act.wait_ge(x_turned, count(g, 1))
                            act.wait_ge(x_late, count(g, 1, back=2))
                            act.wait_ge(qk, count(g, 1, back=2))
                            act.copy(fT[par(g)][:, :], p_x[:, 0:NODES]).then_inc(x_sb, 1)
                    if g := at(7):
                        act.wait_ge(z_ready, count(g, 1))
                        act.wait_ge(added, count(g, 2, back=2))
                        act.activation(th[par(g)][:, :], z[par(g)][:, :], ACT.Tanh, scale=0.5).then_inc(tanh, 1)

                sweep(act, 7, body)

            @block.tensor
            def _(pe):
                def body(at):
                    g4, g5, g6 = at(4), at(5), at(6)

                    def logits(h):
                        if g := g4:
                            if h < 2:
                                pe.wait_ge(summed, count(g, 16, 2 * h + 14, back=1))
                            else:
                                pe.wait_ge(summed, count(g, 16, 2 * h - 2))
                            for t in range(TILES):
                                mm = nc.tensor.matmul(p_k[h % 2][:, t * NODES:(t + 1) * NODES], queriesT[par(g)][:, t * P:(t + 1) * P],
                                                      head_keys[par(g)][:, h, :], start=True, stop=True)
                            mm.then_inc(keys, 1)

                    def value_rows(u):
                        if g := g5:
                            if u:
                                pe.wait_ge(values_sb, count(g, 4, u))
                            else:
                                pe.wait_ge(values_sb, count(g, 4, back=1))
                            nc.tensor.matmul(p_v[:, :], fT_late[par(g)][:, (u // 2) * P:(u // 2 + 1) * P],
                                                       values_w[:, (u % 2) * 512:(u % 2 + 1) * 512], start=True, stop=True).then_inc(values, 1)

                    def turn(w):
                        if g := g6:
                            t, u = w // 4, w % 4
                            pe.wait_ge(weighted, count(g, 2, t + 1))
                            if w < 2:
                                pe.wait_ge(e_sb, count(g, 8, w + 7, back=1))
                            else:
                                pe.wait_ge(e_sb, count(g, 8, w - 1))
                            for k in range(2):
                                for m in range(2):
                                    mm = transpose(nc, p_e[w % 2][:, (2 * k + m) * P:(2 * k + m + 1) * P], E[par(g)][:, t, 2 * u + k, m * P:(m + 1) * P], ident[:, :])
                            mm.then_inc(e_turned, 1)

                    def attend(w):
                        if g := g6:
                            t, u = w // 4, w % 4
                            if w == 0:
                                pe.wait_ge(z_ready, count(g, 1, back=1))
                                pe.wait_ge(values_sb, count(g, 4))
                            pe.wait_ge(e_sb, count(g, 8, w + 1))
                            for k in range(2):
                                for m in range(2):
                                    mm = nc.tensor.matmul(p_out[:, t * D:(t + 1) * D], ET[w % 2][:, (2 * k + m) * P:(2 * k + m + 1) * P],
                                                          V[par(g)][:, m, (2 * u + k) * D:(2 * u + k + 1) * D],
                                                          start=(w == 0 and k == 0 and m == 0), stop=(w == 7 and k == 1 and m == 1),
                                                          skip_group_check=True)
                            mm.then_inc(attended, 1)

                    if g := at(2):
                        pe.wait_ge(normed, count(g, 2))
                        pe.wait_ge(x_sb, count(g, 1, back=1))
                        for t in range(TILES):
                            mm = transpose(nc, p_x[:, t * P:(t + 1) * P], f[par(g)][:, t * D:(t + 1) * D], ident[:, :])
                        mm.then_inc(x_turned, 1)
                    if g := at(3):
                        pe.wait_ge(x_sb, count(g, 1))
                        pe.wait_ge(split, count(g, 7, 1, back=1))
                        nc.tensor.matmul(p_qk[:, 0:NODES], qk_w[:, :], fT[par(g)][:, :], start=True, stop=True).then_inc(qk, 1)
                    if g := g4:
                        pe.wait_ge(split, count(g, 7))
                        pe.wait_ge(headed, count(g, 1))
                    if g := g5:
                        pe.wait_ge(x_late, count(g, 1))
                    for w in range(8):
                        turn(w)
                        logits(w)
                        if w:
                            attend(w - 1)
                        if w % 2 == 0:
                            value_rows(w // 2)
                    attend(7)

                sweep(pe, 6, body)


def gnn1_weights(nc, outer, values_w, qk_all, qk_c, out_c, pick, is_key, no_key, part1, part2, d):
    with ExitStack() as ctx:
        def sb(name, shape, dt=F32):
            return ctx.enter_context(nc.sbuf_tensor(name, shape, dt))

        def two(name, shape, dt=F32):
            return [sb(name + "0", shape, dt), sb(name + "1", shape, dt)]

        def bank(name):
            return ctx.enter_context(nc.psum_tensor(name, [P, 512], F32))

        def sem(name):
            return outer.enter_context(nc.semaphore(name))

        fc_w = sb("w_fc_w", [P, HEADS, D])
        fp_w = sb("w_fp_w", [P, HEADS, D])
        fc_b = sb("w_fc_b", [P, HEADS])
        qk_w = sb("w_qk_w", [P, 2])
        q_b = sb("w_q_b", [1, 1])
        k_b = sb("w_k_b", [1, 1])
        fp_b = sb("w_fp_b", [P, TILES, D])
        fc_b_wide = sb("w_fc_b_wide", [P, HEADS, P])
        key_cols = sb("w_key_cols", [P, P])
        query_cols = sb("w_query_cols", [P, P])
        key_ones = sb("w_key_ones", [1, P])
        query_ones = sb("w_query_ones", [1, P])
        pick_key = sb("w_pick_key", [P, HEADS])
        pick_query = sb("w_pick_query", [P, HEADS])
        p_w = [bank("w_pw0"), bank("w_pw1")]
        p_qk = bank("w_pqk")
        p_c = bank("w_pc")
        weights_in, picks, wide, products, steps = (sem(n) for n in ("w_in", "w_picks", "w_wide", "w_products", "w_steps"))

        with nc.Block() as block:
            @block.sync
            def _(sp):
                for to, of in ((fc_w[:, :, :], d["c_fc_wT"]), (fp_w[:, :, :], d["c_fp_w"].rearrange("(h p) n -> p h n", p=P)),
                               (fc_b[:, :], d["c_fc_bT"]), (qk_w[:, :], d["c_qk_w"]), (q_b[:, :], d["c_q_b"].partition_broadcast(1)),
                               (k_b[:, :], d["c_k_b"].partition_broadcast(1)), (fp_b[:, :, :], d["c_fp_bx2"].partition_broadcast(P))):
                    sp.dma_start(to, of).then_inc(weights_in, 16)

            @block.gpsimd
            def _(pool):
                pool.memset(pick_key[:, :], 0.0).then_inc(picks, 1)
                pool.memset(pick_query[:, :], 0.0).then_inc(picks, 1)
                pool.memset(part1[:, :], -1.0).then_inc(picks, 1)
                pool.memset(part2[:, :], -1.0).then_inc(picks, 1)
                for k in range(PARTS):
                    pool.wait_ge(picks, 4 + 2 * k)
                    for to, row in ((pick_key, 32 * k), (pick_query, 32 * k + HEADS)):
                        pool.affine_select(out=to[:, :], in_=to[:, :], compare_op=ALU.not_equal, fill=1.0, base=-row,
                                           pattern=[[-1, HEADS]], channel_multiplier=1).then_inc(picks, 1)
                pool.affine_select(out=part1[:, :], in_=part1[:, :], compare_op=ALU.is_ge, fill=0.0, base=-32,
                                   pattern=[[0, 1]], channel_multiplier=1).then_inc(picks, 1)
                pool.affine_select(out=part2[:, :], in_=part2[:, :], compare_op=ALU.is_ge, fill=0.0, base=-64,
                                   pattern=[[0, 1]], channel_multiplier=1).then_inc(picks, 1)

            @block.vector
            def _(dve):
                dve.wait_ge(weights_in, 16 * 7)
                dve.tensor_copy(fc_b_wide[:, :, :], fc_b[:, :].unsqueeze(2).to_broadcast([P, HEADS, P])).then_inc(wide, 1)
                for to in (qk_all, key_cols, query_cols, key_ones, query_ones):
                    dve.memset(to[:, :], 0.0).then_inc(steps, 1)
                dve.wait_ge(steps, 5)
                for k in range(PARTS):
                    keys, queries = slice(32 * k, 32 * k + HEADS), slice(32 * k + HEADS, 32 * k + 2 * HEADS)
                    dve.tensor_copy(key_cols[:, keys], fc_b[:, :]).then_inc(wide, 1)
                    dve.tensor_copy(query_cols[:, queries], fc_b[:, :]).then_inc(wide, 1)
                    dve.memset(key_ones[:, keys], 1.0).then_inc(wide, 1)
                    dve.memset(query_ones[:, queries], 1.0).then_inc(wide, 1)
                dve.wait_ge(picks, 4 + 2 * PARTS)
                dve.tensor_tensor(pick[:, :], pick_key[:, :], pick_query[:, :], ALU.add)
                dve.tensor_reduce(is_key[:, :], pick_key[:, :], AX.X, ALU.add).then_inc(steps, 1)
                dve.wait_ge(steps, 6)
                dve.tensor_scalar(no_key[:, :], is_key[:, :], -1.0, 1.0, ALU.mult, ALU.add)
                dve.wait_ge(products, 1)
                for k in range(2):
                    dve.tensor_copy(values_w[:, k * 512:(k + 1) * 512], p_w[k][:, :])
                qk = p_qk[:, 0:2 * HEADS].rearrange("p (h w) -> p h w", w=2)
                for k in range(PARTS):
                    dve.tensor_copy(qk_all[:, 32 * k:32 * k + HEADS], qk[:, :, 1])
                    dve.tensor_copy(qk_all[:, 32 * k + HEADS:32 * k + 2 * HEADS], qk[:, :, 0])
                dve.tensor_copy(qk_c[:, :], p_qk[:, 64:65])
                for t in range(TILES):
                    dve.tensor_tensor(out_c[:, t, :], p_c[:, 0:D], fp_b[:, t, :], ALU.add)

            @block.tensor
            def _(pe):
                pe.wait_ge(weights_in, 16 * 7)
                pe.wait_ge(wide, 1 + 4 * PARTS)
                for h in range(HEADS):
                    nc.tensor.matmul(p_w[h // 4][:, (h % 4) * D:(h % 4 + 1) * D], fc_w[:, h, :], fp_w[:, h, :], start=True, stop=True)
                    nc.tensor.matmul(p_qk[:, 2 * h:2 * h + 2], fc_w[:, h, :], qk_w[:, :], start=True, stop=True)
                for k, (to, of) in enumerate(((key_cols[:, :], qk_w[:, 1:2]), (query_cols[:, :], qk_w[:, 0:1]), (key_ones[:, :], k_b[:, :]), (query_ones[:, :], q_b[:, :]))):
                    nc.tensor.matmul(p_qk[:, 64:65], to, of, start=(k == 0), stop=(k == 3))
                for h in range(HEADS):
                    mm = nc.tensor.matmul(p_c[:, 0:D], fc_b_wide[:, h, :], fp_w[:, h, :], start=(h == 0), stop=(h == HEADS - 1))
                mm.then_inc(products, 1)


EXPERTS = 8
CHOICES = 2
FF = 512
TOKENS = GRAPHS * NODES
SLOT = TILES * P
REGION = TOKENS + SLOT
SLOTS = TOKENS * CHOICES // SLOT + EXPERTS
SPARE_TILES = EXPERTS * TILES
ROWS = EXPERTS * REGION + SPARE_TILES * P
PAD_TILES = EXPERTS * TILES + SPARE_TILES
MOST = TOKENS // SLOT
ROW = D + 1


def route(nc, outer, X, ident, mhalf, lneps, weights, slot_e, slot_row, rows_in, expert_weights, expert_weights_in, d):
    with ExitStack() as ctx:
        def sb(name, shape, dt=F32):
            return ctx.enter_context(nc.sbuf_tensor(name, shape, dt))

        def two(name, shape, dt=F32):
            return [sb(name + "0", shape, dt), sb(name + "1", shape, dt)]

        def bank(name):
            return ctx.enter_context(nc.psum_tensor(name, [P, 512], F32))

        def sem(name):
            return outer.enter_context(nc.semaphore(name))

        router = sb("d_router", [P, EXPERTS])
        W1 = sb("d_W1", [P, FF])
        b1 = sb("d_b1", [P, 4])
        W2 = sb("d_W2", [P, 4, D])
        b2 = sb("d_b2", [P, TILES, D])
        upper = sb("d_upper", [P, P])
        ones = sb("d_ones", [P, P])
        iota8 = sb("d_iota8", [P, EXPERTS])
        start8 = sb("d_start8", [P, TILES, EXPERTS])
        target = sb("d_target", [P, GRAPHS // 2, 2, CHOICES * TILES], I32)
        padding = sb("d_padding", [P, PAD_TILES, ROW])
        dump = sb("d_dump", [P, PAD_TILES], I32)
        lastf = sb("d_lastf", [1, EXPERTS])
        last = sb("d_last", [1, EXPERTS], I32)
        st = two("d_st", [P, TILES, 6])
        mv = two("d_mv", [P, TILES, 2])
        ve = two("d_ve", [P, TILES])
        rstd = two("d_rstd", [P, TILES])
        xn = two("d_xn", [P, TILES, D])
        xT = two("d_xT", [P, NODES])
        hT = two("d_hT", [P, 4, NODES])
        tmp = two("d_tmp", [P, NODES])
        pay = [two(f"d_pay{k}", [P, TILES, ROW]) for k in range(CHOICES)]
        best = two("d_best", [P, TILES, 8])
        besti = two("d_besti", [P, TILES, 8], mybir.dt.uint32)
        gap = two("d_gap", [P, TILES])
        th = two("d_th", [P, TILES])
        bestf = two("d_bestf", [P, TILES, CHOICES])
        hot = two("d_hot", [P, TILES, CHOICES, EXPERTS])
        both = two("d_both", [P, TILES, EXPERTS])
        carry = two("d_carry", [P, EXPERTS])
        carry1 = two("d_carry1", [P, EXPERTS])
        rank = two("d_rank", [P, TILES, EXPERTS])
        chosen = two("d_chosen", [P, TILES, CHOICES, EXPERTS])
        rowf = two("d_rowf", [P, TILES * CHOICES])
        row = two("d_row", [P, TILES * CHOICES], I32)
        waited = two("d_waited", [P, 1])
        multiples = sb("d_multiples", [1, EXPERTS, MOST])
        over = sb("d_over", [1, EXPERTS, MOST])
        taken_slots = sb("d_taken_slots", [1, EXPERTS])
        end = sb("d_end", [1, EXPERTS])
        skip = sb("d_skip", [1, EXPERTS])
        slot = sb("d_slot", [1, SLOTS])
        slotf = sb("d_slotf", [1, SLOTS])
        past = sb("d_past", [1, SLOTS])
        rowsf = sb("d_rowsf", [1, SLOTS])
        p_x = bank("d_px")
        p_h = [bank("d_ph0"), bank("d_ph1")]
        p_y = bank("d_py")
        p_r = bank("d_pr")
        p_c = bank("d_pc")

        weights_in, consts, table, padded, spare_rows = (sem(n) for n in ("d_in", "d_consts", "d_table", "d_padded", "d_spare_rows"))
        scattered = [sem("d_scattered0"), sem("d_scattered1")]
        relay = sem("d_relay")
        stats = sem("d_stats")
        scale = sem("d_scale")
        normed = sem("d_normed")
        x_turned = sem("d_x_turned")
        x_sb = sem("d_x_sb")
        logits = sem("d_logits")
        hidden = sem("d_hidden")
        gelu = sem("d_gelu")
        product = sem("d_product")
        added = sem("d_added")
        payload = sem("d_payload")
        packed = sem("d_packed")
        picked = sem("d_picked")
        tanh = sem("d_tanh")
        counted = sem("d_counted")
        placed = sem("d_placed")
        weighed = sem("d_weighed")

        def pad(eng, experts):
            eng.wait_ge(table, 3)
            for e in experts:
                r = eng.value_load(last[0:1, e:e + 1], min_val=0, max_val=ROWS - SLOT)
                eng.dma_start(rows_in[bass.ds(r, SLOT), :].rearrange("(t p) d -> p t d", p=P),
                              padding[:, e * TILES:(e + 1) * TILES, :]).then_inc(padded, 16)
            eng.wait_ge(padded, 16 * EXPERTS)

        with nc.Block() as block:
            @block.sync
            def _(sp):
                for to, of in ((router[:, :], d["d_router"]), (W1[:, :], d["d_W1s"]), (b1[:, :], d["d_b1sT"]),
                               (W2[:, :, :], d["d_W2s"].rearrange("(f p) n -> p f n", p=P)), (b2[:, :, :], d["d_b2sx2"].partition_broadcast(P))):
                    sp.dma_start(to, of).then_inc(weights_in, 16)
                W1e, b1e, W2e, b2e = expert_weights
                sp.dma_start(W1e[:, :, :], d["e_W1"].rearrange("e p f -> p e f")).then_inc(expert_weights_in, 16)
                sp.dma_start(W2e[:, :, :].rearrange("p e (f n) -> p (e f) n", n=D), d["e_W2"].rearrange("e (f p) n -> p (e f) n", p=P)).then_inc(expert_weights_in, 16)
                sp.dma_start(b1e[:, :, :], d["e_b1"].partition_broadcast(P)).then_inc(expert_weights_in, 16)
                sp.dma_start(b2e[:, :, :], d["e_b2x2"].partition_broadcast(P)).then_inc(expert_weights_in, 16)
                sp.wait_ge(consts, 11)
                sp.wait_ge(table, 1)
                for k in range(SPARE_TILES):
                    r = EXPERTS * REGION + k * P
                    sp.dma_start(rows_in[r:r + P, :], padding[:, EXPERTS * TILES + k, :]).then_inc(spare_rows, 16)
                sp.wait_ge(spare_rows, 16 * SPARE_TILES)
                pad(sp, range(0, EXPERTS, 2))

            @block.gpsimd
            def _(pool):
                n = 0

                def made(ins):
                    nonlocal n
                    n += 1
                    ins.then_inc(consts, 1)

                made(pool.memset(ones[:, :], 1.0))
                pool.wait_ge(consts, 1)
                made(pool.affine_select(out=upper[:, :], in_=ones[:, :], compare_op=ALU.is_ge, fill=0.0, base=-1,
                                        pattern=[[1, P]], channel_multiplier=-1))
                made(pool.iota(iota8[:, :], [[1, EXPERTS]], base=0, channel_multiplier=0, allow_small_or_imprecise_dtypes=True))
                made(pool.iota(start8[:, :, :], [[0, TILES], [REGION, EXPERTS]], base=0, channel_multiplier=0, allow_small_or_imprecise_dtypes=True))
                for k in range(CHOICES):
                    made(pool.iota(target[:, :, :, k * TILES:(k + 1) * TILES], [[NODES, GRAPHS], [P, TILES]], base=k * TOKENS, channel_multiplier=1))
                made(pool.iota(dump[:, :], [[P, PAD_TILES]], base=CHOICES * TOKENS, channel_multiplier=1))
                made(pool.memset(padding[:, :, 0:D], 0.0))
                made(pool.iota(multiples[:, :, :], [[0, EXPERTS], [SLOT, MOST]], base=0, channel_multiplier=0, allow_small_or_imprecise_dtypes=True))
                made(pool.iota(slot[:, :], [[1, SLOTS]], base=0, channel_multiplier=0, allow_small_or_imprecise_dtypes=True))
                made(pool.memset(carry[0][:, :], 0.0))
                assert n == 11

                def body(at):
                    if g := at(4):
                        pool.wait_ge(payload, count(g, 2))
                        pool.wait_ge(packed, count(g, 2))
                        pool.wait_ge(placed, count(g, 8))
                        pool.wait_ge(relay, count(g, 1, back=2))
                        pool.tensor_tensor(waited[par(g)][:, :], ident[:, 0:1], ident[:, 0:1], ALU.mult).then_inc(relay, 1)
                        for t in range(TILES):
                            for k in range(CHOICES):
                                n = t * CHOICES + k
                                pool.indirect_dma_start(
                                    out=rows_in, out_offset=bass.IndirectOffsetOnAxis(ap=row[par(g)][:, n:n + 1], axis=0),
                                    in_=pay[k][par(g)][:, t, :], in_offset=None).then_inc(scattered[par(g)], 16)
                    if g := at(0):
                        pool.wait_ge(stats, count(g, 4))
                        pool.tensor_tensor(ve[par(g)][:, :], mv[par(g)][:, :, 1], lneps[:, 0:TILES], ALU.add).then_inc(scale, 1)
                        pool.wait_ge(scale, count(g, 2, 1))
                        pool.wait_ge(normed, count(g, 2, back=2))
                        pool.tensor_tensor(rstd[par(g)][:, :], ve[par(g)][:, :], mhalf[:, 0:TILES], ALU.pow).then_inc(scale, 1)

                sweep(pool, 4, body)
                for b in range(2):
                    pool.wait_ge(scattered[b], 16 * 4 * (GRAPHS // 2))

            @block.vector
            def _(dve):
                dve.wait_ge(weights_in, 16 * 5)
                dve.wait_ge(consts, 11)
                dve.tensor_copy(padding[:, :, D:ROW].bitcast(I32), dump[:, :].unsqueeze(2)).then_inc(table, 1)

                def body(at):
                    g0, g3, g4 = at(0), at(3), at(4)
                    if g := at(5):
                        x = graph_rows(X, g)
                        dve.wait_ge(product, count(g, 1))
                        dve.tensor_tensor(tmp[par(g)][:, :], p_y[:, 0:NODES], b2[:, :, :].rearrange("p t d -> p (t d)"), ALU.add).then_inc(added, 1)
                    if g := g4:
                        dve.wait_ge(counted, count(g, 1))
                        dve.tensor_tensor(carry1[par(g)][:, :], carry[par(g)][:, :], p_c[:, 64:64 + EXPERTS], ALU.add).then_inc(placed, 1)
                        dve.tensor_tensor(rank[par(g)][:, :, :].rearrange("p t e -> p (t e)"), p_c[:, 0:TILES * EXPERTS],
                                               start8[:, :, :].rearrange("p t e -> p (t e)"), ALU.add).then_inc(placed, 1)
                    if g := at(5):
                        x = graph_rows(X, g)
                        dve.wait_ge(added, count(g, 2, 1))
                        if g3:
                            dve.wait_ge(logits, count(g3, 1))
                        dve.tensor_tensor(x, x, tmp[par(g)][:, :], ALU.add).then_inc(added, 1)
                    elif g3:
                        dve.wait_ge(logits, count(g3, 1))
                    if g := g3:
                        for t in range(TILES):
                            dve.max(best[par(g)][:, t, :], p_r[:, t * EXPERTS:(t + 1) * EXPERTS]).then_inc(picked, 1)
                    if g := g4:
                        a, b = par(g), 1 - par(g)
                        dve.wait_ge(placed, count(g, 8, 2))
                        dve.tensor_tensor(carry[b][:, :], carry1[a][:, :], p_c[:, 64 + EXPERTS:64 + 2 * EXPERTS], ALU.add).then_inc(placed, 1)
                        dve.tensor_tensor(rank[a][:, 0, :], rank[a][:, 0, :], carry[a][:, :], ALU.add).then_inc(placed, 1)
                        dve.tensor_tensor(rank[a][:, 1, :], rank[a][:, 1, :], carry1[a][:, :], ALU.add).then_inc(placed, 1)
                    if g := g3:
                        dve.wait_ge(picked, count(g, 8, 2))
                        dve.tensor_tensor(gap[par(g)][:, :], best[par(g)][:, :, 0], best[par(g)][:, :, 1], ALU.subtract).then_inc(picked, 1)
                        for t in range(TILES):
                            dve.max_index(besti[par(g)][:, t, :], best[par(g)][:, t, :], p_r[:, t * EXPERTS:(t + 1) * EXPERTS]).then_inc(picked, 1)
                    if g := g4:
                        a = par(g)
                        dve.wait_ge(placed, count(g, 8, 5))
                        dve.tensor_tensor(chosen[a][:, :, :, :], hot[a][:, :, :, :],
                                               rank[a][:, :, :].unsqueeze(2).to_broadcast([P, TILES, CHOICES, EXPERTS]), ALU.mult).then_inc(placed, 1)
                    if g := g3:
                        dve.wait_ge(picked, count(g, 8, 5))
                        dve.tensor_copy(bestf[par(g)][:, :, :], besti[par(g)][:, :, 0:CHOICES]).then_inc(picked, 1)
                    if g := g0:
                        x = graph_rows(X, g)
                        for t in range(TILES):
                            dve.bn_stats(st[par(g)][:, t, :], x[:, t * D:(t + 1) * D]).then_inc(stats, 1)
                    if g := g4:
                        a = par(g)
                        dve.wait_ge(placed, count(g, 8, 6))
                        dve.tensor_reduce(rowf[a][:, :], chosen[a][:, :, :, :].rearrange("p t k e -> p (t k) e"), AX.X, ALU.add).then_inc(placed, 1)
                    if g := g3:
                        dve.wait_ge(picked, count(g, 8, 6))
                        dve.wait_ge(placed, count(g, 8, back=2))
                        dve.tensor_tensor(hot[par(g)][:, :, :, :].rearrange("p t k e -> p (t k) e"),
                                               iota8[:, :].unsqueeze(1).to_broadcast([P, TILES * CHOICES, EXPERTS]),
                                               bestf[par(g)][:, :, :].rearrange("p t k -> p (t k)").unsqueeze(2).to_broadcast([P, TILES * CHOICES, EXPERTS]),
                                               ALU.is_equal).then_inc(picked, 1)
                    if g := g4:
                        a = par(g)
                        dve.wait_ge(placed, count(g, 8, 7))
                        dve.tensor_copy(row[a][:, :], rowf[a][:, :]).then_inc(placed, 1)
                        dve.wait_ge(tanh, count(g, 1))
                        for k, sign in ((0, 0.5), (1, -0.5)):
                            dve.tensor_scalar(one_of(weights, g, slice(k * TILES, k * TILES + TILES)), th[a][:, :], sign, 0.5, ALU.mult, ALU.add).then_inc(weighed, 1)
                    if g := g3:
                        dve.wait_ge(picked, count(g, 8, 7))
                        dve.wait_ge(counted, count(g, 1, back=2))
                        dve.tensor_tensor(both[par(g)][:, :, :], hot[par(g)][:, :, 0, :], hot[par(g)][:, :, 1, :], ALU.add).then_inc(picked, 1)
                        dve.wait_ge(scattered[par(g)], 16 * 4 * pair(g))
                        for k in range(CHOICES):
                            dve.tensor_copy(pay[k][par(g)][:, :, D].bitcast(I32), one_of(target, g, slice(k * TILES, k * TILES + TILES))).then_inc(packed, 1)
                    if g := g0:
                        dve.wait_ge(stats, count(g, 4, TILES))
                    if g := at(1):
                        x = graph_rows(X, g)
                        dve.wait_ge(scale, count(g, 2))
                        dve.wait_ge(x_turned, count(g, 1, back=2))
                        dve.wait_ge(payload, count(g, 2, back=2))
                        for t in range(TILES):
                            dve.tensor_scalar(xn[par(g)][:, t, :], x[:, t * D:(t + 1) * D], mv[par(g)][:, t, 0:1],
                                                        rstd[par(g)][:, t:t + 1], ALU.subtract, ALU.mult).then_inc(normed, 1)
                    if g := g0:
                        for t in range(TILES):
                            dve.bn_aggr(mv[par(g)][:, t, :], st[par(g)][:, t, :]).then_inc(stats, 1)

                sweep(dve, 5, body)

                n = 1

                def step(ins):
                    nonlocal n
                    ins.then_inc(table, 1)
                    n += 1
                    dve.wait_ge(table, n)

                taken = carry[0]
                dve.wait_ge(placed, count(graph(GRAPHS - 1), 8))
                step(dve.tensor_tensor(lastf[:, :], taken[0:1, :], start8[0:1, 0, :], ALU.add))
                step(dve.tensor_copy(last[:, :], lastf[:, :]))
                step(dve.tensor_tensor(over[:, :, :], taken[0:1, :].unsqueeze(2).to_broadcast([1, EXPERTS, MOST]), multiples[:, :, :], ALU.is_gt))
                step(dve.tensor_reduce(taken_slots[:, :], over[:, :, :], AX.X, ALU.add))
                step(dve.tensor_copy(end[:, :], taken_slots[:, :]))
                for e in range(1, EXPERTS):
                    step(dve.tensor_tensor(end[:, e:e + 1], end[:, e - 1:e], taken_slots[:, e:e + 1], ALU.add))
                step(dve.tensor_scalar(skip[:, :], taken_slots[:, :], -float(SLOT), float(REGION), ALU.mult, ALU.add))
                step(dve.tensor_scalar(rowsf[:, :], slot[:, :], float(SLOT), None, ALU.mult))
                step(dve.memset(slotf[:, :], 0.0))
                for e in range(EXPERTS):
                    step(dve.tensor_scalar(past[:, :], slot[:, :], end[:, e:e + 1], None, ALU.is_ge))
                    step(dve.scalar_tensor_tensor(out=rowsf[:, :], in0=past[:, :], scalar=skip[:, e:e + 1], in1=rowsf[:, :], op0=ALU.mult, op1=ALU.add))
                    if e < EXPERTS - 1:
                        step(dve.tensor_tensor(slotf[:, :], slotf[:, :], past[:, :], ALU.add))
                step(dve.tensor_copy(slot_row[:, :, :].rearrange("a j b -> a (j b)"), rowsf[:, :]))
                step(dve.tensor_copy(slot_e[:, :, :].rearrange("a j b -> a (j b)"), slotf[:, :]))

            @block.scalar
            def _(act):
                act.wait_ge(weights_in, 16 * 5)

                def body(at):
                    if g := at(2):
                        act.wait_ge(x_turned, count(g, 1))
                        act.wait_ge(hidden, count(g, 2, back=2))
                        act.wait_ge(logits, count(g, 1, back=2))
                        act.copy(xT[par(g)][:, :], p_x[:, 0:NODES]).then_inc(x_sb, 1)
                    if g := at(3):
                        act.wait_ge(scattered[par(g)], 16 * 4 * pair(g))
                        for k in range(CHOICES):
                            act.copy(pay[k][par(g)][:, :, 0:D], xn[par(g)][:, :, :]).then_inc(payload, 1)
                        act.wait_ge(product, count(g, 1, back=2))
                        for f in range(4):
                            act.wait_ge(hidden, count(g, 2, f // 2 + 1))
                            act.activation(hT[par(g)][:, f, :], p_h[f // 2][:, (f % 2) * NODES:(f % 2 + 1) * NODES], ACT.Gelu, bias=b1[:, f:f + 1]).then_inc(gelu, 1)
                        act.wait_ge(picked, count(g, 8, 3))
                        act.wait_ge(weighed, count(g, 2, back=2))
                        act.activation(th[par(g)][:, :], gap[par(g)][:, :], ACT.Tanh, scale=0.5).then_inc(tanh, 1)

                sweep(act, 3, body)
                pad(act, range(1, EXPERTS, 2))

            @block.tensor
            def _(pe):
                pe.wait_ge(weights_in, 16 * 5)
                pe.wait_ge(consts, 11)

                def body(at):
                    if g := at(4):
                        pe.wait_ge(picked, count(g, 8))
                        pe.wait_ge(placed, count(g, 8, 3, back=1))
                        m = both[par(g)][:, :, :].rearrange("p t e -> p (t e)")
                        nc.tensor.matmul(p_c[:, 0:TILES * EXPERTS], upper[:, :], m, start=True, stop=True)
                        nc.tensor.matmul(p_c[:, 64:64 + TILES * EXPERTS], ones[:, :], m, start=True, stop=True).then_inc(counted, 1)
                    if g := at(2):
                        pe.wait_ge(normed, count(g, 2))
                        pe.wait_ge(x_sb, count(g, 1, back=1))
                        for t in range(TILES):
                            mm = transpose(nc, p_x[:, t * P:(t + 1) * P], xn[par(g)][:, t, :], ident[:, :])
                        mm.then_inc(x_turned, 1)
                    if g := at(3):
                        pe.wait_ge(x_sb, count(g, 1))
                        pe.wait_ge(picked, count(g, 8, 5, back=1))
                        for t in range(TILES):
                            mm = nc.tensor.matmul(p_r[:, t * EXPERTS:(t + 1) * EXPERTS], xT[par(g)][:, t * P:(t + 1) * P], router[:, :], start=True, stop=True)
                        mm.then_inc(logits, 1)
                    if g := at(4):
                        pe.wait_ge(gelu, count(g, 4))
                        pe.wait_ge(added, count(g, 2, 1, back=1))
                        for t in range(TILES):
                            for f in range(4):
                                mm = nc.tensor.matmul(p_y[:, t * D:(t + 1) * D], hT[par(g)][:, f, t * P:(t + 1) * P], W2[:, f, :],
                                                      start=(f == 0), stop=(f == 3))
                        mm.then_inc(product, 1)
                    if g := at(3):
                        for k in range(2):
                            pe.wait_ge(gelu, count(g, 4, 2 * k + 2, back=1))
                            for f in (2 * k, 2 * k + 1):
                                mm = nc.tensor.matmul(p_h[k][:, (f % 2) * NODES:(f % 2 + 1) * NODES], W1[:, f * P:(f + 1) * P], xT[par(g)][:, :],
                                                      start=True, stop=True)
                            mm.then_inc(hidden, 1)

                sweep(pe, 4, body)


def one_of(table, g, n):
    n = n if isinstance(n, slice) else slice(n, n + 1)
    return one(table[:, bass.ds(pair(g), 1), par(g), n])


def experts(nc, outer, ident, slot_e, slot_row, rows_in, rows_out, expert_weights, weights_in):
    with ExitStack() as ctx:
        def sb(name, shape, dt=F32):
            return ctx.enter_context(nc.sbuf_tensor(name, shape, dt))

        def two(name, shape, dt=F32):
            return [sb(name + "0", shape, dt), sb(name + "1", shape, dt)]

        def bank(name):
            return ctx.enter_context(nc.psum_tensor(name, [P, 512], F32))

        def sem(name):
            return outer.enter_context(nc.semaphore(name))

        W1, b1, W2, b2 = expert_weights
        xg = two("e_xg", [P, TILES, ROW])
        xT = two("e_xT", [P, NODES])
        to0 = two("e_to0", [P, TILES], I32)
        to1 = two("e_to1", [P, TILES], I32)
        to2 = two("e_to2", [P, TILES], I32)
        to3 = two("e_to3", [P, TILES], I32)
        hb = two("e_hb", [P, TILES, FF])
        hg = two("e_hg", [P, TILES, FF])
        hT = two("e_hT", [P, TILES, 4, P])
        y = two("e_y", [P, TILES, D])
        waited = two("e_waited", [P, 1])
        p_x = bank("e_px")
        p_h = [bank("e_ph0"), bank("e_ph1")]
        p_t = [bank("e_pt0"), bank("e_pt1")]
        p_y = [bank("e_py0"), bank("e_py1")]

        rows_here = [sem("e_rows_here0"), sem("e_rows_here1")]
        scattered = [sem("e_scattered0"), sem("e_scattered1")]
        relay = sem("e_relay")
        x_turned = sem("e_x_turned")
        x_sb = sem("e_x_sb")
        hidden = sem("e_hidden")
        biased = sem("e_biased")
        moved = sem("e_moved")
        gelu = sem("e_gelu")
        turned = sem("e_turned")
        turned_sb = sem("e_turned_sb")
        product = sem("e_product")
        aimed = sem("e_aimed")
        sent = sem("e_sent")
        result = sem("e_result")

        def expert(eng, s):
            return eng.value_load(one(slot_e[0:1, bass.ds(pair(s), 1), par(s):par(s) + 1]), min_val=0, max_val=EXPERTS - 1)

        with nc.Block() as block:
            @block.sync
            def _(sp):
                def body(at):
                    if s := at(0):
                        sp.wait_ge(x_sb, count(s, 2, back=2))
                        r = sp.value_load(one(slot_row[0:1, bass.ds(pair(s), 1), par(s):par(s) + 1]), min_val=0, max_val=ROWS - SLOT)
                        sp.dma_start(xg[par(s)][:, :, :], rows_in[bass.ds(r, SLOT), :].rearrange("(t p) d -> p t d", p=P)).then_inc(rows_here[par(s)], 16)

                sweep(sp, 0, body, SLOTS)

            @block.vector
            def _(dve):
                dve.wait_ge(weights_in, 64)

                def body(at):
                    if s := at(5):
                        dve.wait_ge(sent, count(s, 1, back=2))
                        dve.wait_ge(moved, count(s, 1))
                        dve.tensor_copy(to2[par(s)][:, :], to1[par(s)][:, :]).then_inc(aimed, 1)
                    if s := at(1):
                        dve.wait_ge(x_turned, count(s, 1))
                        dve.wait_ge(hidden, count(s, 2, back=2))
                        dve.tensor_copy(xT[par(s)][:, :], p_x[:, 0:NODES]).then_inc(x_sb, 1)
                    if s := at(6):
                        dve.wait_ge(product, count(s, 1))
                        dve.wait_ge(scattered[par(s)], 16 * TILES * pair(s))
                        dve.wait_ge(aimed, count(s, 1))
                        dve.tensor_copy(to3[par(s)][:, :], to2[par(s)][:, :]).then_inc(sent, 1)
                        e = expert(dve, s)
                        dve.tensor_tensor(y[par(s)][:, :, :].rearrange("p t d -> p (t d)"), p_y[par(s)][:, 0:TILES * D], one(b2[:, bass.ds(e, 1), :]), ALU.add).then_inc(result, 1)
                    if s := at(3):
                        dve.wait_ge(aimed, count(s, 1, back=2))
                        dve.wait_ge(x_sb, count(s, 2))
                        dve.tensor_copy(to1[par(s)][:, :], to0[par(s)][:, :]).then_inc(moved, 1)
                    if s := at(1):
                        dve.wait_ge(moved, count(s, 1, back=2))
                        dve.tensor_copy(to0[par(s)][:, :], xg[par(s)][:, :, D].bitcast(I32)).then_inc(x_sb, 1)
                    if s := at(2):
                        e = expert(dve, s)
                        dve.wait_ge(gelu, count(s, 2, back=2))
                        for t in range(TILES):
                            dve.wait_ge(hidden, count(s, 2, t + 1))
                            dve.tensor_tensor(hb[par(s)][:, t, :], p_h[t][:, :], one(b1[:, bass.ds(e, 1), :]), ALU.add).then_inc(biased, 1)

                sweep(dve, 6, body, SLOTS)

            @block.gpsimd
            def _(pool):
                def body(at):
                    if s := at(6):
                        pool.wait_ge(sent, count(s, 1))
                        pool.wait_ge(result, count(s, 1))
                        pool.wait_ge(relay, count(s, 1, back=2))
                        pool.tensor_tensor(waited[par(s)][:, :], ident[:, 0:1], ident[:, 0:1], ALU.mult).then_inc(relay, 1)
                        for t in range(TILES):
                            pool.indirect_dma_start(out=rows_out, out_offset=bass.IndirectOffsetOnAxis(ap=to3[par(s)][:, t:t + 1], axis=0),
                                                                    in_=y[par(s)][:, t, :], in_offset=None).then_inc(scattered[par(s)], 16)

                sweep(pool, 6, body, SLOTS)
                for b in range(2):
                    pool.wait_ge(scattered[b], 16 * TILES * (SLOTS // 2))

            @block.scalar
            def _(act):
                def body(at):
                    if s := at(3):
                        act.wait_ge(turned, count(s, 2, back=2))
                        for t in range(TILES):
                            act.wait_ge(biased, count(s, 2, t + 1))
                            act.activation(hg[par(s)][:, t, :], hb[par(s)][:, t, :], ACT.Gelu).then_inc(gelu, 1)
                    if s := at(4):
                        act.wait_ge(product, count(s, 1, back=2))
                        for t in range(TILES):
                            act.wait_ge(turned, count(s, 2, t + 1))
                            act.copy(hT[par(s)][:, t, :, :].rearrange("p f n -> p (f n)"), p_t[t][:, :]).then_inc(turned_sb, 1)

                sweep(act, 4, body, SLOTS)

            @block.tensor
            def _(pe):
                pe.wait_ge(weights_in, 64)

                def body(at):
                    if s := at(1):
                        pe.wait_ge(rows_here[par(s)], loads(s))
                        pe.wait_ge(x_sb, count(s, 2, 1, back=1))
                        for t in range(TILES):
                            mm = transpose(nc, p_x[:, t * P:(t + 1) * P], xg[par(s)][:, t, 0:D], ident[:, :])
                        mm.then_inc(x_turned, 1)
                    if s := at(4):
                        for t in range(TILES):
                            pe.wait_ge(gelu, count(s, 2, t + 1))
                            pe.wait_ge(turned_sb, count(s, 2, t + 1, back=1))
                            for f in range(4):
                                mm = transpose(nc, p_t[t][:, f * P:(f + 1) * P], hg[par(s)][:, t, f * P:(f + 1) * P], ident[:, :])
                            mm.then_inc(turned, 1)
                    if s := at(5):
                        pe.wait_ge(turned_sb, count(s, 2))
                        pe.wait_ge(result, count(s, 1, back=2))
                        e = expert(pe, s)
                        for t in range(TILES):
                            for f in range(4):
                                mm = nc.tensor.matmul(p_y[par(s)][:, t * D:(t + 1) * D], hT[par(s)][:, t, f, :], one(W2[:, bass.ds(e, 1), f * D:(f + 1) * D]), start=(f == 0), stop=(f == 3))
                        mm.then_inc(product, 1)
                    if s := at(2):
                        pe.wait_ge(x_sb, count(s, 2, 1))
                        pe.wait_ge(biased, count(s, 2, back=1))
                        e = expert(pe, s)
                        for t in range(TILES):
                            nc.tensor.matmul(p_h[t][:, :], xT[par(s)][:, t * P:(t + 1) * P], one(W1[:, bass.ds(e, 1), :]), start=True, stop=True).then_inc(hidden, 1)

                sweep(pe, 5, body, SLOTS)


UNIT = 4 * TILES
UNITS = GRAPHS // 4


def combine(nc, outer, X, weights, rows_out, out):
    with ExitStack() as ctx:
        def sb(name, shape, dt=F32):
            return ctx.enter_context(nc.sbuf_tensor(name, shape, dt))

        def two(name, shape, dt=F32):
            return [sb(name + "0", shape, dt), sb(name + "1", shape, dt)]

        def bank(name):
            return ctx.enter_context(nc.psum_tensor(name, [P, 512], F32))

        def sem(name):
            return outer.enter_context(nc.semaphore(name))

        y = [[sb(f"f_y{k}{b}", [P, UNIT, D]) for b in range(2)] for k in range(CHOICES)]
        y_in = [sem("f_y_in0"), sem("f_y_in1")]
        added = sem("f_added")
        stored = sem("f_stored")
        yt = rows_out[0:CHOICES * TOKENS, :].rearrange("(k j v t p) d -> k j v p t d", k=CHOICES, v=2, t=UNIT, p=P)
        ot = out.rearrange("g n d -> (g n) d").rearrange("(j v t p) d -> j v p t d", v=2, t=UNIT, p=P)
        Xu = X[:, :, :, :].rearrange("p (j v w) b (t d) -> p j v (w b t) d", v=2, w=2, t=TILES)
        Wu = weights[:, :, :, :].rearrange("p (j v w) b (k t) -> p j v (w b) k t", v=2, w=2, t=TILES)

        with nc.Block() as block:
            @block.sync
            def _(sp):
                def body(at):
                    if g := at(0):
                        sp.wait_ge(added, count(g, 2 * UNIT, back=2))
                        for k in range(CHOICES):
                            sp.dma_start(y[k][par(g)][:, :, :], yt[k, bass.ds(pair(g), 1), par(g)].rearrange("a p t d -> (a p) t d")).then_inc(y_in[par(g)], 16)

                sweep(sp, 0, body, UNITS)

            @block.vector
            def _(dve):
                def body(at):
                    if g := at(0):
                        dve.wait_ge(y_in[par(g)], 32 * pair(g) + 32)
                        for k in range(CHOICES):
                            if k:
                                dve.wait_ge(added, count(g, 2 * UNIT, UNIT))
                            for t in range(UNIT):
                                x = Xu[:, bass.ds(pair(g), 1), par(g), t, :].rearrange("p a d -> p (a d)")
                                w = Wu[:, bass.ds(pair(g), 1), par(g), t // TILES, k, t % TILES:t % TILES + 1].rearrange("p a d -> p (a d)")
                                dve.scalar_tensor_tensor(out=x, in0=y[k][par(g)][:, t, :], scalar=w, in1=x,
                                                                  op0=ALU.mult, op1=ALU.add).then_inc(added, 1)

                sweep(dve, 0, body, UNITS)

            @block.scalar
            def _(act):
                def body(at):
                    if g := at(0):
                        act.wait_ge(added, count(g, 2 * UNIT))
                        act.dma_start(ot[bass.ds(pair(g), 1), par(g)].rearrange("a p t d -> (a p) t d"),
                                      Xu[:, bass.ds(pair(g), 1), par(g)].rearrange("p a t d -> p (a t) d")).then_inc(stored, 16)

                sweep(act, 0, body, UNITS)
                act.wait_ge(stored, 16 * (UNITS))


def setup(nc, outer, X, ident, mhalf, lneps, rmseps, epsi, WC, WS, biases, ids, d):
    with ExitStack() as ctx:
        def sb(name, shape, dt=F32):
            return ctx.enter_context(nc.sbuf_tensor(name, shape, dt))

        def two(name, shape, dt=F32):
            return [sb(name + "0", shape, dt), sb(name + "1", shape, dt)]

        def bank(name):
            return ctx.enter_context(nc.psum_tensor(name, [P, 512], F32))

        def sem(name):
            return outer.enter_context(nc.semaphore(name))

        eps = sb("s_eps", [P, 1])
        idi = sb("s_idi", [1, 64], I32)
        idf = sb("s_idf", [1, 64])
        ok = sb("s_ok", [1, 64])
        bs = sb("s_bs", [P, 4])
        x_in, small_in, ident_ready, steps = (sem(n) for n in ("s_x_in", "s_small_in", "s_ident", "s_steps"))

        with nc.Block() as block:
            @block.sync
            def _(sp):
                xt = d["x"].rearrange("g (t p) d -> p (g t) d", p=P)
                xs = X[:, :, :, :].rearrange("p j b (t d) -> p (j b t) d", d=D)
                for k in range(0, 64, 8):
                    sp.dma_start(xs[:, k:k + 8, :], xt[:, k:k + 8, :]).then_inc(x_in, 16)
                sp.dma_start(WS[:, :, :], d["WsT"]).then_inc(small_in, 16)
                sp.dma_start(eps[:, :], d["a_eps"].partition_broadcast(P)).then_inc(small_in, 16)
                sp.dma_start(idi[:, :], d["route"]).then_inc(small_in, 16)
                sp.dma_start(bs[:, :], d["bsT"]).then_inc(small_in, 16)
                sp.dma_start(biases[:, 0:EXPERTS0, :], d["brT"]).then_inc(small_in, 16)
                sp.wait_ge(x_in, 16 * 8)

            @block.gpsimd
            def _(pool):
                pool.memset(ident[:, :], 0.0).then_inc(ident_ready, 1)
                pool.wait_ge(ident_ready, 1)
                pool.affine_select(out=ident[:, :], in_=ident[:, :], compare_op=ALU.not_equal, fill=1.0, base=0,
                                   pattern=[[-1, P]], channel_multiplier=1).then_inc(ident_ready, 1)
                pool.memset(mhalf[:, :], -0.5).then_inc(ident_ready, 1)
                pool.memset(lneps[:, :], LN_EPS).then_inc(ident_ready, 1)
                pool.memset(rmseps[:, :], 512 * RMS_EPS).then_inc(ident_ready, 1)

            @block.vector
            def _(dve):
                n = 0

                def step(ins):
                    nonlocal n
                    ins.then_inc(steps, 1)
                    n += 1
                    dve.wait_ge(steps, n)

                dve.wait_ge(small_in, 16 * 5)
                dve.wait_ge(ident_ready, 2)
                step(dve.tensor_scalar(epsi[:, :], ident[:, :], eps[:, 0:1], None, ALU.mult))
                for l in range(2):
                    for k in range(2):
                        w = WS[:, l, k * HID + k * P:k * HID + (k + 1) * P]
                        step(dve.tensor_tensor(w, w, ident[:, :], ALU.add))
                for l in range(2):
                    step(dve.tensor_copy(WC[:, l, EXPERTS0, :], WS[:, l, :]))
                step(dve.tensor_copy(biases[:, EXPERTS0, :], bs[:, :]))
                for e in range(EXPERTS0):
                    step(dve.tensor_tensor(biases[:, e, :], biases[:, e, :], bs[:, :], ALU.add))
                step(dve.tensor_copy(idf[:, :], idi[:, :]))
                step(dve.tensor_scalar(ok[:, :], idf[:, :], 0.0, None, ALU.is_ge))
                step(dve.tensor_scalar(idf[:, :], idf[:, :], float(EXPERTS0), -float(EXPERTS0), ALU.min, ALU.add))
                step(dve.tensor_tensor(idf[:, :], idf[:, :], ok[:, :], ALU.mult))
                step(dve.tensor_scalar(idf[:, :], idf[:, :], float(EXPERTS0), None, ALU.add))
                step(dve.tensor_copy(ids[:, :, :].rearrange("a j b -> a (j b)"), idf[:, :]))


def program(nc, d, out):
    with ExitStack() as outer:
        sb = lambda name, shape, dt=F32: outer.enter_context(nc.sbuf_tensor(name, shape, dt))
        X = sb("X", [P, GRAPHS // 2, 2, TILES * D])
        ident = sb("ident", [P, P])
        mhalf = sb("mhalf", [P, 4])
        lneps = sb("lneps", [P, 4])
        rmseps = sb("rmseps", [P, 4])
        ids = sb("ids", [1, GRAPHS // 2, 4], I32)
        with ExitStack() as ab:
            sb2 = lambda name, shape: ab.enter_context(nc.sbuf_tensor(name, shape, F32))
            epsi = sb2("epsi", [P, P])
            WC = sb2("WC", [P, 2, EXPERTS0 + 1, 2 * HID])
            WS = sb2("WS", [P, 2, 2 * HID])
            biases = sb2("biases", [P, EXPERTS0 + 1, 4])
            setup(nc, outer, X, ident, mhalf, lneps, rmseps, epsi, WC, WS, biases, ids, d)
            gnn0(nc, outer, X, ident, mhalf, lneps, rmseps, epsi, WC, WS, d)
            ffn0(nc, outer, X, ident, mhalf, lneps, WC, biases, ids, d)
        gnn1(nc, outer, X, ident, mhalf, lneps, d)
        weights = sb("weights", [P, GRAPHS // 2, 2, CHOICES * TILES])
        slot_e = sb("slot_e", [1, SLOTS // 2, 2], I32)
        slot_row = sb("slot_row", [1, SLOTS // 2, 2], I32)
        rows_in = nc.dram_tensor("rows_in", (ROWS, ROW), F32).ap()
        rows_out = nc.dram_tensor("rows_out", (CHOICES * TOKENS + PAD_TILES * P, D), F32).ap()
        with ExitStack() as de:
            expert_weights = [de.enter_context(nc.sbuf_tensor(name, [P, EXPERTS, width], F32))
                              for name, width in (("e_W1", FF), ("e_b1", FF), ("e_W2", 4 * D), ("e_b2", TILES * D))]
            expert_weights_in = outer.enter_context(nc.semaphore("e_weights_in"))
            route(nc, outer, X, ident, mhalf, lneps, weights, slot_e, slot_row, rows_in, expert_weights, expert_weights_in, d)
            experts(nc, outer, ident, slot_e, slot_row, rows_in, rows_out, expert_weights, expert_weights_in)
        combine(nc, outer, X, weights, rows_out, out)


def kernel(**inputs):
    import numpy as np
    import concourse.bacc as bacc
    from concourse.bass_utils import run_bass_kernel_spmd as run

    v = {k: np.asarray(a) for k, a in inputs.items()}
    c = np.ascontiguousarray
    half = lambda w: w.reshape(*w.shape[:-1], 2, P)
    arrays = {
        "x": v["x"],
        "adj": v["adj"],
        "adjT": c(v["adj"].transpose(0, 2, 1).reshape(GRAPHS, TILES, P, NODES).transpose(0, 2, 1, 3)),
        "a_eps": v["L0_gnn_epsilon"].reshape(1),
        "a_W1": v["L0_gnn_W1"], "a_W2": v["L0_gnn_W2"], "a_b1": v["L0_gnn_b1"], "a_rmsw": v["L0_gnn_rms_weight"],
        "a_b2x2": c(np.stack([v["L0_gnn_b2"]] * 2)),
        "route": v["L0_ffn_route_id"].reshape(1, 64),
        "b_WiT": c(v["L0_ffn_Wi"].T), "b_bi": c(v["L0_ffn_bi"].reshape(2, P).T),
        "WrT": c(half(v["L0_ffn_Wr"]).transpose(4, 0, 1, 3, 2).reshape(P, 2, EXPERTS0, 2 * HID)),
        "WsT": c(half(v["L0_ffn_Ws"][:, 0]).transpose(3, 0, 2, 1).reshape(P, 2, 2 * HID)),
        "brT": c(half(v["L0_ffn_br"]).transpose(3, 1, 0, 2).reshape(P, EXPERTS0, 4)),
        "bsT": c(half(v["L0_ffn_bs"][:, 0]).transpose(2, 0, 1).reshape(P, 4)),
        "b_WoT": c(v["L0_ffn_Wo"].T), "b_box2": c(np.stack([v["L0_ffn_bo"]] * 2)),
        "c_fc_wT": c(v["L1_gnn_fc_w"].reshape(D, HEADS, D).transpose(2, 1, 0)), "c_fp_w": v["L1_gnn_fp_w"],
        "c_fc_bT": c(v["L1_gnn_fc_b"].reshape(HEADS, D).T), "c_qk_w": c(np.concatenate([v["L1_gnn_q_w"], v["L1_gnn_k_w"]], 1)),
        "d_router": v["L1_ffn_Wr"], "d_W1s": v["L1_ffn_W1s"], "d_W2s": v["L1_ffn_W2s"],
        "d_b1sT": c(v["L1_ffn_b1s"].reshape(4, P).T), "d_b2sx2": c(np.stack([v["L1_ffn_b2s"]] * 2)),
        "e_W1": v["L1_ffn_W1p"], "e_W2": v["L1_ffn_W2p"], "e_b1": v["L1_ffn_b1p"], "e_b2x2": c(np.stack([v["L1_ffn_b2p"]] * 2, 1).reshape(EXPERTS, TILES * D)),
        "c_q_b": v["L1_gnn_q_b"], "c_k_b": v["L1_gnn_k_b"], "c_fp_bx2": c(np.stack([v["L1_gnn_fp_b"]] * 2)),
    }
    nc = bacc.Bacc("TRN2", target_bir_lowering=False, num_devices=1)
    d = {k: nc.dram_tensor("in_" + k, a.shape, mybir.dt.from_np(a.dtype), kind="ExternalInput").ap() for k, a in arrays.items()}
    out = nc.dram_tensor("out", (GRAPHS, NODES, D), F32, kind="ExternalOutput").ap()
    program(nc, d, out)
    r = run(nc, [{"in_" + k: c(a) for k, a in arrays.items()}], core_ids=[0])
    return r.results[0]["out"]
```

```python
from contextlib import ExitStack

import concourse.bass as bass
from concourse import mybir

F32 = mybir.dt.float32
BF16 = mybir.dt.bfloat16
I32 = mybir.dt.int32
ALU = mybir.AluOpType
ACT = mybir.ActivationFunctionType
AX = mybir.AxisListType

P = 128
GRAPHS = 32
TILES = 2
D = 128
NODES = P * TILES
LN_EPS = 1e-5
RMS_EPS = 1e-6


def pair(g):
    return g[0]


def par(g):
    return g[1]


def number(g):
    return 2 * g[0] + g[1]


def graph(i):
    return i // 2, i % 2


def count(g, each, k=None, back=0):
    n = each * (number(g) - back) + (each if k is None else k)
    return 0 if isinstance(n, int) and number(g) < back else n


def loads(g, back=0):
    return 16 * (pair(g) - back) + 16


def sweep(eng, depth, body, units=GRAPHS):
    first = (depth + 3) // 2 * 2

    def peeled(i):
        return lambda lag: graph(i - lag) if 0 <= i - lag < units else None

    for i in range(first):
        body(peeled(i))
    with eng.Fori(first // 2, units // 2) as j:
        for q in (0, 1):
            body(lambda lag: (j + (q - lag) // 2, (q - lag) % 2))
    for i in range(units, units + depth):
        body(peeled(i))


def one(ap):
    return ap.rearrange("p a d -> p (a d)")


def graph_rows(X, g):
    return one(X[:, bass.ds(pair(g), 1), par(g), :])


def transpose(nc, out, in_, ident):
    return nc.tensor.transpose(out, in_, ident)


def load_gnn0(eng, weights, weights_in, d):
    W1, W2, b1, rmsw, b2 = weights
    for to, of in ((W1[:, :], d["a_W1"]), (W2[:, :, :], d["a_W2"].rearrange("(f p) n -> p f n", p=P)), (b1[:, :], d["a_b1"].partition_broadcast(P)),
                   (rmsw[:, :], d["a_rmsw"].partition_broadcast(P)), (b2[:, :, :], d["a_b2x2"].partition_broadcast(P))):
        eng.dma_start(to, of).then_inc(weights_in, 16)


def load_ffn0(eng, weights, weights_in, d):
    Wi, bi, Wo, bo = weights
    for to, of in ((Wi[:, :], d["b_WiT"]), (bi[:, :], d["b_bi"]), (Wo[:, :, :], d["b_WoT"].rearrange("(k p) n -> p k n", p=P)),
                   (bo[:, :, :], d["b_box2"].partition_broadcast(P))):
        eng.dma_start(to, of).then_inc(weights_in, 16)


def load_gnn1(eng, weights, weights_in, d):
    fc_w, fp_w, fc_b, qk_w, q_b, k_b, fp_b = weights
    for to, of in ((fc_w[:, :, :], d["c_fc_wT"]), (fp_w[:, :, :], d["c_fp_w"].rearrange("(h p) n -> p h n", p=P)),
                   (fc_b[:, :], d["c_fc_bT"]), (qk_w[:, :], d["c_qk_w"]), (q_b[:, :], d["c_q_b"].partition_broadcast(1)),
                   (k_b[:, :], d["c_k_b"].partition_broadcast(1)), (fp_b[:, :, :], d["c_fp_bx2"].partition_broadcast(P))):
        eng.dma_start(to, of).then_inc(weights_in, 16)


def load_route(eng, weights, weights_in, d):
    router, W1, b1, W2, b2 = weights
    for to, of in ((router[:, :], d["d_router"]), (W1[:, :], d["d_W1s"]), (b1[:, :], d["d_b1sT"]),
                   (W2[:, :, :], d["d_W2s"].rearrange("(f p) n -> p f n", p=P)), (b2[:, :, :], d["d_b2sx2"].partition_broadcast(P))):
        eng.dma_start(to, of).then_inc(weights_in, 16)


def gnn0(nc, outer, X, x_rest_in, ident, mhalf, lneps, rmseps, epsi, WC, WS, gnn0_weights, weights_in, ffn0_weights, ffn0_weights_in, d):
    with ExitStack() as ctx:
        def sb(name, shape, dt=F32):
            return ctx.enter_context(nc.sbuf_tensor(name, shape, dt))

        def two(name, shape, dt=F32):
            return [sb(name + "0", shape, dt), sb(name + "1", shape, dt)]

        def bank(name):
            return ctx.enter_context(nc.psum_tensor(name, [P, 512], F32))

        def sem(name):
            return outer.enter_context(nc.semaphore(name))

        W1, W2, b1, rmsw, b2 = gnn0_weights
        AT = two("a_AT", [P, TILES, NODES])
        st = two("a_st", [P, TILES, 6])
        mv = two("a_mv", [P, TILES, 2])
        ve = two("a_ve", [P, TILES])
        rstd = two("a_rstd", [P, TILES])
        xln = two("a_xln", [P, TILES, D])
        aggT = two("a_aggT", [P, NODES])
        hb = two("a_hb", [P, TILES, 512])
        hn = two("a_hn", [P, TILES, 512])
        junk = two("a_junk", [P, TILES, 512])
        ssq = two("a_ssq", [P, TILES])
        ms = two("a_ms", [P, TILES])
        rr = two("a_rr", [P, TILES])
        hT = two("a_hT", [P, TILES, 4, P])
        tmp = two("a_tmp", [P, NODES])
        p_agg = bank("a_pagg")
        p_h = [bank("a_ph0"), bank("a_ph1")]
        p_t = [bank("a_pt0"), bank("a_pt1")]
        p_out = bank("a_pout")

        rms_weight = sem("a_rms_weight")
        adj_in = [sem("a_adj_in0"), sem("a_adj_in1")]
        wr_in = [sem("a_wr_in0"), sem("a_wr_in1")]
        stats = sem("a_stats")
        scale = sem("a_scale")
        normed = sem("a_normed")
        self_loop = sem("a_self_loop")
        wr_sum = sem("a_wr_sum")
        agg = sem("a_agg")
        agg_sb = sem("a_agg_sb")
        hidden = sem("a_hidden")
        biased = sem("a_biased")
        squares = sem("a_squares")
        rms = sem("a_rms")
        scaled = sem("a_scaled")
        silu = sem("a_silu")
        turned = sem("a_turned")
        turned_sb = sem("a_turned_sb")
        product = sem("a_product")
        added = sem("a_added")

        adjT = d["adjT"].rearrange("(j b) p c n -> j b p c n", b=2)
        wr = d["WrT"].rearrange("p l e n -> l p e n")

        with nc.Block() as block:
            @block.sync
            def _(sp):
                load_ffn0(sp, ffn0_weights, ffn0_weights_in, d)

                def body(at):
                    if g := at(0):
                        sp.wait_ge(agg, count(g, 1, back=2))
                        sp.wait_ge(self_loop, count(g, 2, back=2))
                        sp.dma_start(AT[par(g)][:, :, :], adjT[bass.ds(pair(g), 1), par(g)].rearrange("a p c n -> (a p) c n")).then_inc(adj_in[par(g)], 16)
                        sp.wait_ge(wr_sum, count(g, 1, back=2))
                        sp.dma_start(WC[:, par(g), bass.ds(pair(g), 1), :], wr[par(g), :, bass.ds(pair(g), 1), :]).then_inc(wr_in[par(g)], 16)

                sweep(sp, 0, body)

            @block.vector
            def _(dve):
                dve.wait_ge(weights_in, 16 * 5)
                dve.tensor_scalar(rmsw[:, :], rmsw[:, :], 512 ** 0.5, None, ALU.mult).then_inc(rms_weight, 1)
                dve.wait_ge(rms_weight, 1)

                def body(at):
                    if g := at(1):
                        x = graph_rows(X, g)
                        dve.wait_ge(scale, count(g, 2))
                        dve.wait_ge(agg, count(g, 1, back=2))
                        for t in range(TILES):
                            dve.tensor_scalar(xln[par(g)][:, t, :], x[:, t * D:(t + 1) * D], mv[par(g)][:, t, 0:1],
                                                        rstd[par(g)][:, t:t + 1], ALU.subtract, ALU.mult).then_inc(normed, 1)
                    if g := at(0):
                        x = graph_rows(X, g)
                        if isinstance(pair(g), int) and number(g) == 4:
                            dve.wait_ge(x_rest_in, 16 * 7)
                        for t in range(TILES):
                            dve.bn_stats(st[par(g)][:, t, :], x[:, t * D:(t + 1) * D]).then_inc(stats, 1)
                    if g := at(0):
                        dve.wait_ge(stats, count(g, 4, TILES))
                    if g := at(6):
                        x = graph_rows(X, g)
                        dve.wait_ge(product, count(g, 1))
                        dve.tensor_tensor(tmp[par(g)][:, :], p_out[:, 0:NODES], b2[:, :, :].rearrange("p a d -> p (a d)"), ALU.add).then_inc(added, 1)
                        dve.wait_ge(added, count(g, 2, 1))
                        dve.tensor_tensor(x, x, tmp[par(g)][:, :], ALU.add).then_inc(added, 1)
                    if g := at(0):
                        for t in range(TILES):
                            dve.bn_aggr(mv[par(g)][:, t, :], st[par(g)][:, t, :]).then_inc(stats, 1)
                    if g := at(3):
                        dve.wait_ge(rms, count(g, 2))
                        dve.wait_ge(biased, count(g, 2))
                        dve.wait_ge(turned, count(g, 2, back=2))
                        for t in range(TILES):
                            dve.scalar_tensor_tensor(out=hn[par(g)][:, t, :], in0=hb[par(g)][:, t, :],
                                                               scalar=rr[par(g)][:, t:t + 1], in1=rmsw[:, :],
                                                               op0=ALU.mult, op1=ALU.mult).then_inc(scaled, 1)
                    if g := at(2):
                        dve.wait_ge(squares, count(g, 2, back=2))
                        for t in range(TILES):
                            dve.wait_ge(hidden, count(g, 2, t + 1))
                            dve.tensor_tensor(hb[par(g)][:, t, :], p_h[t][:, :], b1[:, :], ALU.add).then_inc(biased, 1)

                sweep(dve, 6, body)

            @block.gpsimd
            def _(pool):
                def body(at):
                    if g := at(0):
                        pool.wait_ge(stats, count(g, 4))
                        pool.tensor_tensor(ve[par(g)][:, :], mv[par(g)][:, :, 1], lneps[:, 0:TILES], ALU.add).then_inc(scale, 1)
                        pool.wait_ge(scale, count(g, 2, 1))
                        pool.wait_ge(normed, count(g, 2, back=2))
                        pool.tensor_tensor(rstd[par(g)][:, :], ve[par(g)][:, :], mhalf[:, 0:TILES], ALU.pow).then_inc(scale, 1)
                        pool.wait_ge(adj_in[par(g)], loads(g))
                        for t in range(TILES):
                            a = AT[par(g)][:, t, t * P:(t + 1) * P]
                            pool.tensor_tensor(a, a, epsi[:, :], ALU.add).then_inc(self_loop, 1)
                        pool.wait_ge(wr_in[par(g)], loads(g))
                        w = one(WC[:, par(g), bass.ds(pair(g), 1), :])
                        pool.tensor_tensor(w, w, WS[:, par(g), :], ALU.add).then_inc(wr_sum, 1)
                    if g := at(2):
                        pool.wait_ge(squares, count(g, 2))
                        pool.tensor_tensor(ms[par(g)][:, :], ssq[par(g)][:, :], rmseps[:, 0:TILES], ALU.add).then_inc(rms, 1)
                        pool.wait_ge(rms, count(g, 2, 1))
                        pool.wait_ge(scaled, count(g, 2, back=2))
                        pool.tensor_tensor(rr[par(g)][:, :], ms[par(g)][:, :], mhalf[:, 0:TILES], ALU.pow).then_inc(rms, 1)

                sweep(pool, 2, body)

            @block.scalar
            def _(act):
                def body(at):
                    if g := at(1):
                        act.wait_ge(agg, count(g, 1))
                        act.wait_ge(hidden, count(g, 2, back=2))
                        act.copy(aggT[par(g)][:, :], p_agg[:, 0:NODES]).then_inc(agg_sb, 1)
                    if g := at(2):
                        for t in range(TILES):
                            act.wait_ge(biased, count(g, 2, t + 1))
                            act.wait_ge(rms, count(g, 2, back=2))
                            act.activation(junk[par(g)][:, t, :], hb[par(g)][:, t, :], ACT.Square, accum_out=ssq[par(g)][:, t:t + 1]).then_inc(squares, 1)
                    if g := at(3):
                        for t in range(TILES):
                            act.wait_ge(scaled, count(g, 2, t + 1))
                            act.activation(hn[par(g)][:, t, :], hn[par(g)][:, t, :], ACT.Silu).then_inc(silu, 1)
                    if g := at(4):
                        act.wait_ge(product, count(g, 1, back=2))
                        for t in range(TILES):
                            act.wait_ge(turned, count(g, 2, t + 1))
                            act.copy(hT[par(g)][:, t, :, :].rearrange("p f n -> p (f n)"), p_t[t][:, :]).then_inc(turned_sb, 1)

                sweep(act, 4, body)

            @block.tensor
            def _(pe):
                pe.wait_ge(weights_in, 16 * 5)

                def body(at):
                    if g := at(1):
                        pe.wait_ge(normed, count(g, 2))
                        pe.wait_ge(self_loop, count(g, 2))
                        pe.wait_ge(agg_sb, count(g, 1, back=1))
                        for t in range(TILES):
                            mm = nc.tensor.matmul(p_agg[:, 0:NODES], xln[par(g)][:, t, :], AT[par(g)][:, t, :],
                                                  start=(t == 0), stop=(t == TILES - 1))
                        mm.then_inc(agg, 1)
                    if g := at(2):
                        pe.wait_ge(agg_sb, count(g, 1))
                        for t in range(TILES):
                            pe.wait_ge(biased, count(g, 2, t + 1, back=1))
                            nc.tensor.matmul(p_h[t][:, :], aggT[par(g)][:, t * P:(t + 1) * P], W1[:, :], start=True, stop=True).then_inc(hidden, 1)
                    if g := at(4):
                        for t in range(TILES):
                            pe.wait_ge(silu, count(g, 2, t + 1))
                            pe.wait_ge(turned_sb, count(g, 2, t + 1, back=1))
                            for f in range(4):
                                mm = transpose(nc, p_t[t][:, f * P:(f + 1) * P], hn[par(g)][:, t, f * P:(f + 1) * P], ident[:, :])
                            mm.then_inc(turned, 1)
                    if g := at(5):
                        pe.wait_ge(turned_sb, count(g, 2))
                        pe.wait_ge(added, count(g, 2, 1, back=1))
                        for t in range(TILES):
                            for f in range(4):
                                mm = nc.tensor.matmul(p_out[:, t * D:(t + 1) * D], hT[par(g)][:, t, f, :], W2[:, f, :],
                                                      start=(f == 0), stop=(f == 3))
                        mm.then_inc(product, 1)

                sweep(pe, 5, body)


EXPERTS0 = 16
HID = 256


def ffn0(nc, outer, X, ident, mhalf, lneps, WC, biases, ids, weights, weights_in, gnn1_raw, gnn1_raw_in, d):
    with ExitStack() as ctx:
        def sb(name, shape, dt=F32):
            return ctx.enter_context(nc.sbuf_tensor(name, shape, dt))

        def two(name, shape, dt=F32):
            return [sb(name + "0", shape, dt), sb(name + "1", shape, dt)]

        def bank(name):
            return ctx.enter_context(nc.psum_tensor(name, [P, 512], F32))

        def sem(name):
            return outer.enter_context(nc.semaphore(name))

        Wi, bi, Wo, bo = weights
        st = two("b_st", [P, TILES, 6])
        mv = two("b_mv", [P, TILES, 2])
        ve = two("b_ve", [P, TILES])
        rstd = two("b_rstd", [P, TILES])
        xln = two("b_xln", [P, TILES, D])
        xT = two("b_xT", [P, NODES])
        hT = [two(f"b_hT{l}", [P, 2, NODES]) for l in range(3)]
        W_here = [two(f"b_W_here{l}", [P, TILES, 2 * HID]) for l in range(2)]
        tmp = two("b_tmp", [P, NODES])
        p_x = bank("b_px")
        p_h = bank("b_ph")
        p_y = [bank("b_py0"), bank("b_py1")]
        p_out = bank("b_pout")

        stats = sem("b_stats")
        scale = sem("b_scale")
        normed = sem("b_normed")
        x_turned = sem("b_x_turned")
        x_sb = sem("b_x_sb")
        first = sem("b_first")
        here = [sem(f"b_here{l}") for l in range(2)]
        layer = [sem(f"b_layer{l}") for l in range(2)]
        relu = [sem(f"b_relu{l}") for l in range(3)]
        product = sem("b_product")
        added = sem("b_added")

        with nc.Block() as block:
            @block.sync
            def _(sp):
                load_gnn1(sp, gnn1_raw, gnn1_raw_in, d)

            @block.vector
            def _(dve):
                dve.wait_ge(weights_in, 64)

                def body(at):
                    if g := at(0):
                        x = graph_rows(X, g)
                        for t in range(TILES):
                            dve.bn_stats(st[par(g)][:, t, :], x[:, t * D:(t + 1) * D]).then_inc(stats, 1)
                    if g := at(7):
                        dve.wait_ge(product, count(g, 1))
                        dve.tensor_tensor(tmp[par(g)][:, :], p_out[:, 0:NODES], bo[:, :, :].rearrange("p a d -> p (a d)"), ALU.add).then_inc(added, 1)
                    for l in range(2):
                        if g := at(3 + l):
                            for t in range(TILES):
                                e = dve.value_load(ids[0:1, bass.ds(pair(g), 1), par(g) * 2 + t], min_val=0, max_val=EXPERTS0)
                                if t == 0:
                                    dve.wait_ge(layer[l], count(g, 1, back=2))
                                dve.tensor_copy(W_here[l][par(g)][:, t, :], one(WC[:, l, bass.ds(e, 1), :])).then_inc(here[l], 1)
                    if g := at(1):
                        x = graph_rows(X, g)
                        dve.wait_ge(scale, count(g, 2))
                        dve.wait_ge(x_turned, count(g, 1, back=2))
                        for t in range(TILES):
                            dve.tensor_scalar(xln[par(g)][:, t, :], x[:, t * D:(t + 1) * D], mv[par(g)][:, t, 0:1],
                                                        rstd[par(g)][:, t:t + 1], ALU.subtract, ALU.mult).then_inc(normed, 1)
                    if g := at(0):
                        dve.wait_ge(stats, count(g, 4, TILES))
                    if g := at(7):
                        x = graph_rows(X, g)
                        dve.wait_ge(added, count(g, 2, 1))
                        dve.tensor_tensor(x, x, tmp[par(g)][:, :], ALU.add).then_inc(added, 1)
                    if g := at(0):
                        for t in range(TILES):
                            dve.bn_aggr(mv[par(g)][:, t, :], st[par(g)][:, t, :]).then_inc(stats, 1)

                sweep(dve, 7, body)

            @block.gpsimd
            def _(pool):
                def body(at):
                    if g := at(0):
                        pool.wait_ge(stats, count(g, 4))
                        pool.tensor_tensor(ve[par(g)][:, :], mv[par(g)][:, :, 1], lneps[:, 0:TILES], ALU.add).then_inc(scale, 1)
                        pool.wait_ge(scale, count(g, 2, 1))
                        pool.wait_ge(normed, count(g, 2, back=2))
                        pool.tensor_tensor(rstd[par(g)][:, :], ve[par(g)][:, :], mhalf[:, 0:TILES], ALU.pow).then_inc(scale, 1)

                sweep(pool, 0, body)

            @block.scalar
            def _(act):
                act.wait_ge(weights_in, 64)

                def body(at):
                    if g := at(2):
                        act.wait_ge(x_turned, count(g, 1))
                        act.wait_ge(first, count(g, 1, back=2))
                        act.copy(xT[par(g)][:, :], p_x[:, 0:NODES]).then_inc(x_sb, 1)
                    if g := at(3):
                        act.wait_ge(first, count(g, 1))
                        act.wait_ge(layer[0], count(g, 1, back=2))
                        for k in range(2):
                            act.activation(hT[0][par(g)][:, k, :], p_h[:, k * NODES:(k + 1) * NODES], ACT.Relu, bias=bi[:, k:k + 1]).then_inc(relu[0], 1)
                    for l in range(2):
                        if g := at(4 + l):
                            for t in range(TILES):
                                e = act.value_load(ids[0:1, bass.ds(pair(g), 1), par(g) * 2 + t], min_val=0, max_val=EXPERTS0)
                                if t == 0:
                                    act.wait_ge((product if l else layer[1]), count(g, 1, back=2))
                                    act.wait_ge(layer[l], count(g, 1))
                                for k in range(2):
                                    act.activation(hT[l + 1][par(g)][:, k, t * P:(t + 1) * P],
                                                                  p_y[l][:, (2 * k + t) * P:(2 * k + t + 1) * P], ACT.Relu,
                                                                  bias=biases[:, bass.ds(e, 1), 2 * l + k]).then_inc(relu[l + 1], 1)

                sweep(act, 5, body)

            @block.tensor
            def _(pe):
                pe.wait_ge(weights_in, 64)

                def body(at):
                    if g := at(2):
                        pe.wait_ge(normed, count(g, 2))
                        pe.wait_ge(x_sb, count(g, 1, back=1))
                        for t in range(TILES):
                            mm = transpose(nc, p_x[:, t * P:(t + 1) * P], xln[par(g)][:, t, :], ident[:, :])
                        mm.then_inc(x_turned, 1)
                    if g := at(3):
                        pe.wait_ge(x_sb, count(g, 1))
                        pe.wait_ge(relu[0], count(g, 2, back=1))
                        for k in range(2):
                            mm = nc.tensor.matmul(p_h[:, k * NODES:(k + 1) * NODES], Wi[:, k * P:(k + 1) * P], xT[par(g)][:, :], start=True, stop=True)
                        mm.then_inc(first, 1)
                    for l in range(2):
                        if g := at(4 + l):
                            pe.wait_ge(relu[l], count(g, (4 if l else 2)))
                            pe.wait_ge(relu[l + 1], count(g, 4, back=1))
                            pe.wait_ge(here[l], count(g, 2))
                            for t in range(TILES):
                                for k in range(2):
                                    for m in range(2):
                                        mm = nc.tensor.matmul(p_y[l][:, (2 * k + t) * P:(2 * k + t + 1) * P],
                                                              W_here[l][par(g)][:, t, m * HID + k * P:m * HID + (k + 1) * P],
                                                              hT[l][par(g)][:, m, t * P:(t + 1) * P], start=(m == 0), stop=(m == 1))
                            mm.then_inc(layer[l], 1)
                    if g := at(6):
                        pe.wait_ge(relu[2], count(g, 4))
                        pe.wait_ge(added, count(g, 2, 1, back=1))
                        for t in range(TILES):
                            for k in range(2):
                                mm = nc.tensor.matmul(p_out[:, t * D:(t + 1) * D], hT[2][par(g)][:, k, t * P:(t + 1) * P], Wo[:, k, :],
                                                      start=(k == 0), stop=(k == 1))
                        mm.then_inc(product, 1)

                sweep(pe, 6, body)


HEADS = 8
NEG = -1e9
PARTS = 3
LEAK = 0.01


def gnn1(nc, outer, X, ident, mhalf, lneps, raw, raw_in, route_weights, route_weights_in, d):
    with ExitStack() as ctx:
        def sb(name, shape, dt=F32):
            return ctx.enter_context(nc.sbuf_tensor(name, shape, dt))

        def two(name, shape, dt=F32):
            return [sb(name + "0", shape, dt), sb(name + "1", shape, dt)]

        def bank(name):
            return ctx.enter_context(nc.psum_tensor(name, [P, 512], F32))

        def sem(name):
            return outer.enter_context(nc.semaphore(name))

        values_w = sb("c_values_w", [P, HEADS * D])
        qk_w = sb("c_qk_w", [P, P])
        qk_c = sb("c_qk_c", [P, 1])
        out_c = sb("c_out_c", [P, TILES, D])
        pick = sb("c_pick", [P, HEADS], BF16)
        is_key = sb("c_is_key", [P, 1])
        no_key = sb("c_no_key", [P, 1])
        part1 = sb("c_part1", [P, 1])
        part2 = sb("c_part2", [P, 1])
        gnn1_weights(nc, outer, values_w, qk_w, qk_c, out_c, pick, is_key, no_key, part1, part2, raw, raw_in)

        AN = two("c_AN", [P, TILES, NODES])
        mask = two("c_mask", [P, TILES, NODES])
        st = two("c_st", [P, TILES, 6])
        mv = two("c_mv", [P, TILES, 2])
        ve = two("c_ve", [P, TILES])
        rstd = two("c_rstd", [P, TILES])
        f = two("c_f", [P, TILES * D])
        residual = sb("c_residual", [P, GRAPHS // 2, 2, TILES * D])
        fT = two("c_fT", [P, NODES])
        fT_late = two("c_fT_late", [P, NODES])
        rest = sb("c_rest", [P, NODES])
        part = sb("c_part", [P, NODES], BF16)
        qkT = sb("c_qkT", [P, NODES], BF16)
        keysT = two("c_keysT", [P, NODES], BF16)
        queriesT = two("c_queriesT", [P, NODES], BF16)
        head_keys = two("c_head_keys", [P, HEADS, NODES], BF16)
        top = two("c_top", [P, TILES * HEADS])
        peak = two("c_peak", [P, TILES * HEADS])
        shift = two("c_shift", [P, TILES * HEADS])
        L = two("c_L", [P, TILES, HEADS, NODES])
        E = two("c_E", [P, TILES, HEADS, NODES])
        total = two("c_total", [P, TILES * HEADS])
        inv = two("c_inv", [P, TILES * HEADS])
        V = two("c_V", [P, TILES, HEADS * D])
        ET = two("c_ET", [P, 512])
        z = two("c_z", [P, NODES])
        th = two("c_th", [P, NODES])
        sg = two("c_sg", [P, NODES])
        p_x = bank("c_px")
        p_qk = bank("c_pqk")
        p_k = [bank("c_pk0"), bank("c_pk1")]
        p_v = bank("c_pv")
        p_e = [bank("c_pe0"), bank("c_pe1")]
        p_out = bank("c_pout")

        adj_in = [sem("c_adj_in0"), sem("c_adj_in1")]
        stats = sem("c_stats")
        scale = sem("c_scale")
        masked = sem("c_masked")
        normed = sem("c_normed")
        kept = sem("c_kept")
        x_turned = sem("c_x_turned")
        x_sb = sem("c_x_sb")
        x_late = sem("c_x_late")
        qk = sem("c_qk")
        split = sem("c_split")
        headed = sem("c_headed")
        keys = sem("c_keys")
        summed = sem("c_summed")
        leaky = sem("c_leaky")
        shift_ready = sem("c_shift_ready")
        exped = sem("c_exped")
        inverse = sem("c_inverse")
        weighted = sem("c_weighted")
        values = sem("c_values")
        values_sb = sem("c_values_sb")
        e_turned = sem("c_e_turned")
        e_sb = sem("c_e_sb")
        attended = sem("c_attended")
        z_ready = sem("c_z_ready")
        tanh = sem("c_tanh")
        added = sem("c_added")

        adj = d["adj"].rearrange("(j b) (t p) m -> j b p t m", b=2, p=P)

        with nc.Block() as block:
            @block.sync
            def _(sp):
                load_route(sp, route_weights, route_weights_in, d)

                def body(at):
                    if g := at(0):
                        sp.wait_ge(masked, count(g, 1, back=2))
                        sp.dma_start(AN[par(g)][:, :, :], adj[bass.ds(pair(g), 1), par(g)].rearrange("a p t m -> (a p) t m")).then_inc(adj_in[par(g)], 16)

                sweep(sp, 0, body)

            @block.vector
            def _(dve):
                def body(at):
                    g0, g3, g4, g5, g8 = at(0), at(3), at(4), at(5), at(8)

                    def maxima(h):
                        if g := g4:
                            for t in range(TILES):
                                n = t * HEADS + h
                                dve.tensor_tensor_reduce(L[par(g)][:, t, h, :], p_k[h % 2][:, t * NODES:(t + 1) * NODES],
                                                                   mask[par(g)][:, t, :], 1.0, -3.4e38, ALU.add, ALU.max, top[par(g)][:, n:n + 1]).then_inc(summed, 1)

                    def leak(h):
                        if g := g4:
                            dve.wait_ge(summed, count(g, 16, 2 * h + 2))
                            e = L[par(g)][:, :, h, :]
                            dve.scalar_tensor_tensor(out=e, in0=e, scalar=LEAK, in1=e, op0=ALU.mult, op1=ALU.max).then_inc(leaky, 1)

                    def split_step(k):
                        if g := g3:
                            if k:
                                dve.wait_ge(split, count(g, 7, k))
                            if k == 0:
                                dve.wait_ge(split, count(g, 7, back=1))
                                dve.wait_ge(qk, count(g, 1))
                                dve.tensor_scalar(rest[:, :], p_qk[:, 0:NODES], qk_c[:, 0:1], None, ALU.add).then_inc(split, 1)
                            elif k == 2:
                                dve.scalar_tensor_tensor(out=rest[:, :], in0=part[:, :], scalar=part1[:, 0:1], in1=rest[:, :],
                                                         op0=ALU.mult, op1=ALU.add).then_inc(split, 1)
                            elif k == 4:
                                dve.scalar_tensor_tensor(out=qkT[:, :], in0=part[:, :], scalar=part2[:, 0:1], in1=rest[:, :],
                                                         op0=ALU.mult, op1=ALU.add).then_inc(split, 1)
                            elif k == 5:
                                dve.wait_ge(headed, count(g, 2, back=2))
                                dve.tensor_scalar(keysT[par(g)][:, :], qkT[:, :], is_key[:, 0:1], no_key[:, 0:1], ALU.mult, ALU.add).then_inc(split, 1)
                            elif k == 6:
                                dve.wait_ge(keys, count(g, 8, back=2))
                                dve.tensor_scalar(queriesT[par(g)][:, :], qkT[:, :], no_key[:, 0:1], is_key[:, 0:1], ALU.mult, ALU.add).then_inc(split, 1)
                            else:
                                dve.tensor_copy(part[:, :], rest[:, :]).then_inc(split, 1)

                    if g := at(6):
                        dve.wait_ge(exped, count(g, 16))
                        dve.wait_ge(weighted, count(g, 2, back=2))
                        dve.reciprocal(inv[par(g)][:, HEADS:], total[par(g)][:, HEADS:]).then_inc(inverse, 1)
                    if g := at(7):
                        dve.wait_ge(attended, count(g, 8))
                        dve.wait_ge(kept, count(g, 1))
                        dve.wait_ge(tanh, count(g, 1, back=2))
                        dve.tensor_tensor(z[par(g)][:, :], p_out[:, 0:NODES], graph_rows(residual, g), ALU.add).then_inc(z_ready, 1)
                    if g := g0:
                        x = graph_rows(X, g)
                        for t in range(TILES):
                            dve.bn_stats(st[par(g)][:, t, :], x[:, t * D:(t + 1) * D]).then_inc(stats, 1)
                    split_step(0)
                    if g := g4:
                        dve.wait_ge(adj_in[par(g)], loads(g))
                        dve.tensor_scalar(mask[par(g)][:, :, :].rearrange("p t m -> p (t m)"), AN[par(g)][:, :, :].rearrange("p t m -> p (t m)"),
                                                    1.0, -NEG, ALU.subtract, ALU.mult).then_inc(masked, 1)
                        dve.wait_ge(exped, count(g, 16, back=2))
                        dve.wait_ge(masked, count(g, 1))
                        dve.wait_ge(keys, count(g, 8, 1))
                        dve.wait_ge(x_sb, count(g, 1))
                        dve.wait_ge(values, count(g, 4, back=2))
                        dve.tensor_copy(fT_late[par(g)][:, :], fT[par(g)][:, :]).then_inc(x_late, 1)
                    maxima(0)
                    split_step(1)
                    if g := g4:
                        dve.wait_ge(keys, count(g, 8, 2))
                    if g := g0:
                        dve.wait_ge(stats, count(g, 4, TILES))
                    if g := at(1):
                        x = graph_rows(X, g)
                        dve.wait_ge(scale, count(g, 2))
                        dve.wait_ge(x_turned, count(g, 1, back=2))
                        dve.wait_ge(kept, count(g, 1, back=2))
                        for t in range(TILES):
                            dve.tensor_scalar(f[par(g)][:, t * D:(t + 1) * D], x[:, t * D:(t + 1) * D], mv[par(g)][:, t, 0:1],
                                                        rstd[par(g)][:, t:t + 1], ALU.subtract, ALU.mult).then_inc(normed, 1)
                    maxima(1)
                    if g := g0:
                        for t in range(TILES):
                            dve.bn_aggr(mv[par(g)][:, t, :], st[par(g)][:, t, :]).then_inc(stats, 1)
                    for h in range(2, HEADS):
                        if h < 7:
                            split_step(h)
                        if (g := g8) and h == 3:
                            dve.wait_ge(tanh, count(g, 1))
                            dve.tensor_scalar(sg[par(g)][:, :], th[par(g)][:, :], 0.5, 0.5, ALU.mult, ALU.add).then_inc(added, 1)
                        if (g := g8) and h == 4:
                            x = graph_rows(X, g)
                            dve.wait_ge(added, count(g, 2, 1))
                            dve.tensor_tensor(x, x, sg[par(g)][:, :], ALU.add).then_inc(added, 1)
                        if (g := g5) and h == 5:
                            dve.wait_ge(exped, count(g, 16, HEADS))
                            dve.wait_ge(weighted, count(g, 2, 1, back=2))
                            dve.reciprocal(inv[par(g)][:, 0:HEADS], total[par(g)][:, 0:HEADS]).then_inc(inverse, 1)
                        if g := g4:
                            dve.wait_ge(keys, count(g, 8, h + 1))
                        leak(h - 2)
                        maxima(h)
                    leak(6)
                    if g := g4:
                        dve.wait_ge(summed, count(g, 16))
                        dve.scalar_tensor_tensor(out=peak[par(g)][:, :], in0=top[par(g)][:, :], scalar=LEAK, in1=top[par(g)][:, :],
                                                                op0=ALU.mult, op1=ALU.max).then_inc(shift_ready, 1)
                    leak(7)
                    if g := g4:
                        dve.wait_ge(shift_ready, count(g, 2, 1))
                        dve.tensor_scalar(shift[par(g)][:, :], peak[par(g)][:, :], -1.0, None, ALU.mult).then_inc(shift_ready, 1)

                sweep(dve, 8, body)

            @block.gpsimd
            def _(pool):
                def body(at):
                    def weigh(t, g):
                        if g:
                            pool.wait_ge(inverse, count(g, 2, t + 1))
                            e = E[par(g)][:, t, :, :]
                            w = inv[par(g)][:, t * HEADS:(t + 1) * HEADS].unsqueeze(2).to_broadcast([P, HEADS, NODES])
                            pool.tensor_tensor(e, e, w, ALU.mult).then_inc(weighted, 1)

                    def head(k, g):
                        if g:
                            half = slice(k * HEADS // 2, (k + 1) * HEADS // 2)
                            pool.wait_ge(keys, count(g, 8, back=2))
                            pool.wait_ge(split, count(g, 7, 6))
                            pool.tensor_tensor(head_keys[par(g)][:, half, :], keysT[par(g)][:, :].unsqueeze(1).to_broadcast([P, HEADS // 2, NODES]),
                                               pick[:, half].unsqueeze(2).to_broadcast([P, HEADS // 2, NODES]), ALU.mult).then_inc(headed, 1)

                    weigh(1, at(6))
                    head(0, at(3))
                    weigh(0, at(5))
                    head(1, at(3))
                    if g := at(0):
                        pool.wait_ge(stats, count(g, 4))
                        pool.tensor_tensor(ve[par(g)][:, :], mv[par(g)][:, :, 1], lneps[:, 0:TILES], ALU.add).then_inc(scale, 1)
                        pool.wait_ge(scale, count(g, 2, 1))
                        pool.wait_ge(normed, count(g, 2, back=2))
                        pool.tensor_tensor(rstd[par(g)][:, :], ve[par(g)][:, :], mhalf[:, 0:TILES], ALU.pow).then_inc(scale, 1)
                    if g := at(1):
                        pool.wait_ge(normed, count(g, 2))
                        pool.tensor_tensor(graph_rows(residual, g), f[par(g)][:, :], out_c[:, :, :].rearrange("p t d -> p (t d)"), ALU.add).then_inc(kept, 1)

                sweep(pool, 6, body)

            @block.scalar
            def _(act):
                def body(at):
                    g5, g6 = at(5), at(6)
                    for w in range(8):
                        if g := g6:
                            act.wait_ge(e_turned, count(g, 8, w + 1))
                            if w < 2:
                                act.wait_ge(attended, count(g, 8, w + 7, back=1))
                            else:
                                act.wait_ge(attended, count(g, 8, w - 1))
                            act.copy(ET[w % 2][:, :], p_e[w % 2][:, :]).then_inc(e_sb, 1)
                        if g := g5:
                            if w % 2 == 1:
                                u = w // 2
                                act.wait_ge(values, count(g, 4, u + 1))
                                act.wait_ge(attended, count(g, 8, back=2))
                                act.copy(V[par(g)][:, u // 2, (u % 2) * 512:(u % 2 + 1) * 512], p_v[:, :]).then_inc(values_sb, 1)
                            if w == 0:
                                act.wait_ge(shift_ready, count(g, 2))
                                act.wait_ge(leaky, count(g, 8))
                                act.wait_ge(e_turned, count(g, 8, back=2))
                                act.wait_ge(inverse, count(g, 2, back=2))
                            for n in (2 * w, 2 * w + 1):
                                t, h = n // HEADS, n % HEADS
                                act.activation(E[par(g)][:, t, h, :], L[par(g)][:, t, h, :], ACT.Exp, bias=shift[par(g)][:, n:n + 1],
                                                        accum_out=total[par(g)][:, n:n + 1]).then_inc(exped, 1)
                        if (g := at(2)) and w == 1:
                            act.wait_ge(x_turned, count(g, 1))
                            act.wait_ge(x_late, count(g, 1, back=2))
                            act.wait_ge(qk, count(g, 1, back=2))
                            act.copy(fT[par(g)][:, :], p_x[:, 0:NODES]).then_inc(x_sb, 1)
                    if g := at(7):
                        act.wait_ge(z_ready, count(g, 1))
                        act.wait_ge(added, count(g, 2, back=2))
                        act.activation(th[par(g)][:, :], z[par(g)][:, :], ACT.Tanh, scale=0.5).then_inc(tanh, 1)

                sweep(act, 7, body)

            @block.tensor
            def _(pe):
                def body(at):
                    g4, g5, g6 = at(4), at(5), at(6)

                    def logits(h):
                        if g := g4:
                            if h == HEADS // 2:
                                pe.wait_ge(headed, count(g, 2))
                            if h < 2:
                                pe.wait_ge(summed, count(g, 16, 2 * h + 14, back=1))
                            else:
                                pe.wait_ge(summed, count(g, 16, 2 * h - 2))
                            for t in range(TILES):
                                mm = nc.tensor.matmul(p_k[h % 2][:, t * NODES:(t + 1) * NODES], queriesT[par(g)][:, t * P:(t + 1) * P],
                                                      head_keys[par(g)][:, h, :], start=True, stop=True)
                            mm.then_inc(keys, 1)

                    def value_rows(u):
                        if g := g5:
                            if u:
                                pe.wait_ge(values_sb, count(g, 4, u))
                            else:
                                pe.wait_ge(values_sb, count(g, 4, back=1))
                            nc.tensor.matmul(p_v[:, :], fT_late[par(g)][:, (u // 2) * P:(u // 2 + 1) * P],
                                                       values_w[:, (u % 2) * 512:(u % 2 + 1) * 512], start=True, stop=True).then_inc(values, 1)

                    def turn(w):
                        if g := g6:
                            t, u = w // 4, w % 4
                            pe.wait_ge(weighted, count(g, 2, t + 1))
                            if w < 2:
                                pe.wait_ge(e_sb, count(g, 8, w + 7, back=1))
                            else:
                                pe.wait_ge(e_sb, count(g, 8, w - 1))
                            for k in range(2):
                                for m in range(2):
                                    mm = transpose(nc, p_e[w % 2][:, (2 * k + m) * P:(2 * k + m + 1) * P], E[par(g)][:, t, 2 * u + k, m * P:(m + 1) * P], ident[:, :])
                            mm.then_inc(e_turned, 1)

                    def attend(w):
                        if g := g6:
                            t, u = w // 4, w % 4
                            if w == 0:
                                pe.wait_ge(z_ready, count(g, 1, back=1))
                                pe.wait_ge(values_sb, count(g, 4))
                            pe.wait_ge(e_sb, count(g, 8, w + 1))
                            for k in range(2):
                                for m in range(2):
                                    mm = nc.tensor.matmul(p_out[:, t * D:(t + 1) * D], ET[w % 2][:, (2 * k + m) * P:(2 * k + m + 1) * P],
                                                          V[par(g)][:, m, (2 * u + k) * D:(2 * u + k + 1) * D],
                                                          start=(w == 0 and k == 0 and m == 0), stop=(w == 7 and k == 1 and m == 1),
                                                          skip_group_check=True)
                            mm.then_inc(attended, 1)

                    if g := at(2):
                        pe.wait_ge(normed, count(g, 2))
                        pe.wait_ge(x_sb, count(g, 1, back=1))
                        for t in range(TILES):
                            mm = transpose(nc, p_x[:, t * P:(t + 1) * P], f[par(g)][:, t * D:(t + 1) * D], ident[:, :])
                        mm.then_inc(x_turned, 1)
                    if g := at(3):
                        pe.wait_ge(x_sb, count(g, 1))
                        pe.wait_ge(split, count(g, 7, 1, back=1))
                        nc.tensor.matmul(p_qk[:, 0:NODES], qk_w[:, :], fT[par(g)][:, :], start=True, stop=True).then_inc(qk, 1)
                    if g := g4:
                        pe.wait_ge(split, count(g, 7))
                        pe.wait_ge(headed, count(g, 2, 1))
                    if g := g5:
                        pe.wait_ge(x_late, count(g, 1))
                    for w in range(8):
                        turn(w)
                        logits(w)
                        if w:
                            attend(w - 1)
                        if w % 2 == 0:
                            value_rows(w // 2)
                    attend(7)

                sweep(pe, 6, body)


def gnn1_weights(nc, outer, values_w, qk_all, qk_c, out_c, pick, is_key, no_key, part1, part2, raw, weights_in):
    with ExitStack() as ctx:
        def sb(name, shape, dt=F32):
            return ctx.enter_context(nc.sbuf_tensor(name, shape, dt))

        def bank(name):
            return ctx.enter_context(nc.psum_tensor(name, [P, 512], F32))

        def sem(name):
            return outer.enter_context(nc.semaphore(name))

        fc_w, fp_w, fc_b, qk_w, q_b, k_b, fp_b = raw
        fc_b_wide = sb("w_fc_b_wide", [P, HEADS, P])
        key_cols = sb("w_key_cols", [P, P])
        query_cols = sb("w_query_cols", [P, P])
        key_ones = sb("w_key_ones", [1, P])
        query_ones = sb("w_query_ones", [1, P])
        pick_key = sb("w_pick_key", [P, HEADS])
        pick_query = sb("w_pick_query", [P, HEADS])
        p_w = [bank("w_pw0"), bank("w_pw1")]
        p_qk = bank("w_pqk")
        p_c = bank("w_pc")
        picks, wide, products, steps = (sem(n) for n in ("w_picks", "w_wide", "w_products", "w_steps"))

        with nc.Block() as block:
            @block.gpsimd
            def _(pool):
                pool.memset(pick_key[:, :], 0.0).then_inc(picks, 1)
                pool.memset(pick_query[:, :], 0.0).then_inc(picks, 1)
                pool.memset(part1[:, :], -1.0).then_inc(picks, 1)
                pool.memset(part2[:, :], -1.0).then_inc(picks, 1)
                for k in range(PARTS):
                    pool.wait_ge(picks, 4 + 2 * k)
                    for to, row in ((pick_key, 32 * k), (pick_query, 32 * k + HEADS)):
                        pool.affine_select(out=to[:, :], in_=to[:, :], compare_op=ALU.not_equal, fill=1.0, base=-row,
                                           pattern=[[-1, HEADS]], channel_multiplier=1).then_inc(picks, 1)
                pool.affine_select(out=part1[:, :], in_=part1[:, :], compare_op=ALU.is_ge, fill=0.0, base=-32,
                                   pattern=[[0, 1]], channel_multiplier=1).then_inc(picks, 1)
                pool.affine_select(out=part2[:, :], in_=part2[:, :], compare_op=ALU.is_ge, fill=0.0, base=-64,
                                   pattern=[[0, 1]], channel_multiplier=1).then_inc(picks, 1)

            @block.vector
            def _(dve):
                dve.wait_ge(weights_in, 16 * 7)
                dve.tensor_copy(fc_b_wide[:, :, :], fc_b[:, :].unsqueeze(2).to_broadcast([P, HEADS, P])).then_inc(wide, 1)
                for to in (qk_all, key_cols, query_cols, key_ones, query_ones):
                    dve.memset(to[:, :], 0.0).then_inc(steps, 1)
                dve.wait_ge(steps, 5)
                for k in range(PARTS):
                    keys, queries = slice(32 * k, 32 * k + HEADS), slice(32 * k + HEADS, 32 * k + 2 * HEADS)
                    dve.tensor_copy(key_cols[:, keys], fc_b[:, :]).then_inc(wide, 1)
                    dve.tensor_copy(query_cols[:, queries], fc_b[:, :]).then_inc(wide, 1)
                    dve.memset(key_ones[:, keys], 1.0).then_inc(wide, 1)
                    dve.memset(query_ones[:, queries], 1.0).then_inc(wide, 1)
                dve.wait_ge(picks, 4 + 2 * PARTS)
                dve.tensor_tensor(pick[:, :], pick_key[:, :], pick_query[:, :], ALU.add)
                dve.tensor_reduce(is_key[:, :], pick_key[:, :], AX.X, ALU.add).then_inc(steps, 1)
                dve.wait_ge(steps, 6)
                dve.tensor_scalar(no_key[:, :], is_key[:, :], -1.0, 1.0, ALU.mult, ALU.add)
                for k in range(2):
                    dve.wait_ge(products, k + 1)
                    dve.tensor_copy(values_w[:, k * 512:(k + 1) * 512], p_w[k][:, :])
                dve.wait_ge(products, 3)
                qk = p_qk[:, 0:2 * HEADS].rearrange("p (h w) -> p h w", w=2)
                for k in range(PARTS):
                    dve.tensor_copy(qk_all[:, 32 * k:32 * k + HEADS], qk[:, :, 1])
                    dve.tensor_copy(qk_all[:, 32 * k + HEADS:32 * k + 2 * HEADS], qk[:, :, 0])
                dve.tensor_copy(qk_c[:, :], p_qk[:, 64:65])
                dve.wait_ge(products, 4)
                for t in range(TILES):
                    dve.tensor_tensor(out_c[:, t, :], p_c[:, 0:D], fp_b[:, t, :], ALU.add)

            @block.tensor
            def _(pe):
                pe.wait_ge(weights_in, 16 * 7)
                for h in range(HEADS):
                    mm = nc.tensor.matmul(p_w[h // 4][:, (h % 4) * D:(h % 4 + 1) * D], fc_w[:, h, :], fp_w[:, h, :], start=True, stop=True)
                    if h % 4 == 3:
                        mm.then_inc(products, 1)
                for h in range(HEADS):
                    nc.tensor.matmul(p_qk[:, 2 * h:2 * h + 2], fc_w[:, h, :], qk_w[:, :], start=True, stop=True)
                pe.wait_ge(wide, 1 + 4 * PARTS)
                for k, (to, of) in enumerate(((key_cols[:, :], qk_w[:, 1:2]), (query_cols[:, :], qk_w[:, 0:1]), (key_ones[:, :], k_b[:, :]), (query_ones[:, :], q_b[:, :]))):
                    mm = nc.tensor.matmul(p_qk[:, 64:65], to, of, start=(k == 0), stop=(k == 3))
                mm.then_inc(products, 1)
                for h in range(HEADS):
                    mm = nc.tensor.matmul(p_c[:, 0:D], fc_b_wide[:, h, :], fp_w[:, h, :], start=(h == 0), stop=(h == HEADS - 1))
                mm.then_inc(products, 1)


EXPERTS = 8
CHOICES = 2
FF = 512
TOKENS = GRAPHS * NODES
SLOT = TILES * P
REGION = TOKENS + SLOT
SLOTS = TOKENS * CHOICES // SLOT + EXPERTS
SPARE_TILES = EXPERTS * TILES
ROWS = EXPERTS * REGION + SPARE_TILES * P
PAD_TILES = EXPERTS * TILES + SPARE_TILES
MOST = TOKENS // SLOT
ROW = D + 1


def route(nc, outer, X, ident, mhalf, lneps, weights, slot_e, slot_row, rows_in, route_weights, weights_in, expert_weights, expert_weights_in, d):
    with ExitStack() as ctx:
        def sb(name, shape, dt=F32):
            return ctx.enter_context(nc.sbuf_tensor(name, shape, dt))

        def two(name, shape, dt=F32):
            return [sb(name + "0", shape, dt), sb(name + "1", shape, dt)]

        def bank(name):
            return ctx.enter_context(nc.psum_tensor(name, [P, 512], F32))

        def sem(name):
            return outer.enter_context(nc.semaphore(name))

        router, W1, b1, W2, b2 = route_weights
        upper = sb("d_upper", [P, P])
        ones = sb("d_ones", [P, P])
        iota8 = sb("d_iota8", [P, EXPERTS])
        start8 = sb("d_start8", [P, TILES, EXPERTS])
        target = sb("d_target", [P, GRAPHS // 2, 2, CHOICES * TILES], I32)
        padding = sb("d_padding", [P, PAD_TILES, ROW])
        dump = sb("d_dump", [P, PAD_TILES], I32)
        lastf = sb("d_lastf", [1, EXPERTS])
        last = sb("d_last", [1, EXPERTS], I32)
        st = two("d_st", [P, TILES, 6])
        mv = two("d_mv", [P, TILES, 2])
        ve = two("d_ve", [P, TILES])
        rstd = two("d_rstd", [P, TILES])
        xn = two("d_xn", [P, TILES, D])
        xT = two("d_xT", [P, NODES])
        hT = two("d_hT", [P, 4, NODES])
        tmp = two("d_tmp", [P, NODES])
        pay = [two(f"d_pay{k}", [P, TILES, ROW]) for k in range(CHOICES)]
        best = two("d_best", [P, TILES, 8])
        besti = two("d_besti", [P, TILES, 8], mybir.dt.uint32)
        gap = two("d_gap", [P, TILES])
        th = two("d_th", [P, TILES])
        bestf = two("d_bestf", [P, TILES, CHOICES])
        hot = two("d_hot", [P, TILES, CHOICES, EXPERTS])
        both = two("d_both", [P, TILES, EXPERTS])
        carry = two("d_carry", [P, EXPERTS])
        carry1 = two("d_carry1", [P, EXPERTS])
        rank = two("d_rank", [P, TILES, EXPERTS])
        chosen = two("d_chosen", [P, TILES, CHOICES, EXPERTS])
        rowf = two("d_rowf", [P, TILES * CHOICES])
        row = two("d_row", [P, TILES * CHOICES], I32)
        waited = two("d_waited", [P, 1])
        multiples = sb("d_multiples", [1, EXPERTS, MOST])
        over = sb("d_over", [1, EXPERTS, MOST])
        taken_slots = sb("d_taken_slots", [1, EXPERTS])
        end = sb("d_end", [1, EXPERTS])
        skip = sb("d_skip", [1, EXPERTS])
        slot = sb("d_slot", [1, SLOTS])
        slotf = sb("d_slotf", [1, SLOTS])
        past = sb("d_past", [1, SLOTS, EXPERTS])
        skipped = sb("d_skipped", [1, SLOTS])
        rowsf = sb("d_rowsf", [1, SLOTS])
        p_x = bank("d_px")
        p_h = [bank("d_ph0"), bank("d_ph1")]
        p_y = bank("d_py")
        p_r = bank("d_pr")
        p_c = bank("d_pc")

        consts, table, padded, spare_rows = (sem(n) for n in ("d_consts", "d_table", "d_padded", "d_spare_rows"))
        scattered = [sem("d_scattered0"), sem("d_scattered1")]
        relay = sem("d_relay")
        stats = sem("d_stats")
        scale = sem("d_scale")
        normed = sem("d_normed")
        x_turned = sem("d_x_turned")
        x_sb = sem("d_x_sb")
        logits = sem("d_logits")
        hidden = sem("d_hidden")
        gelu = sem("d_gelu")
        product = sem("d_product")
        added = sem("d_added")
        payload = sem("d_payload")
        packed = sem("d_packed")
        picked = sem("d_picked")
        tanh = sem("d_tanh")
        counted = sem("d_counted")
        placed = sem("d_placed")
        weighed = sem("d_weighed")

        def pad(eng, experts):
            eng.wait_ge(table, 3)
            for e in experts:
                r = eng.value_load(last[0:1, e:e + 1], min_val=0, max_val=ROWS - SLOT)
                eng.dma_start(rows_in[bass.ds(r, SLOT), :].rearrange("(t p) d -> p t d", p=P),
                              padding[:, e * TILES:(e + 1) * TILES, :]).then_inc(padded, 16)
            eng.wait_ge(padded, 16 * EXPERTS)

        with nc.Block() as block:
            @block.sync
            def _(sp):
                W1e, b1e, W2e, b2e = expert_weights
                sp.dma_start(W1e[:, :, :], d["e_W1"].rearrange("e p f -> p e f")).then_inc(expert_weights_in, 16)
                sp.dma_start(W2e[:, :, :].rearrange("p e (f n) -> p (e f) n", n=D), d["e_W2"].rearrange("e (f p) n -> p (e f) n", p=P)).then_inc(expert_weights_in, 16)
                sp.dma_start(b1e[:, :, :], d["e_b1T"]).then_inc(expert_weights_in, 16)
                sp.dma_start(b2e[:, :, :], d["e_b2x2"].partition_broadcast(P)).then_inc(expert_weights_in, 16)
                sp.wait_ge(consts, 11)
                sp.wait_ge(table, 1)
                for k in range(SPARE_TILES):
                    r = EXPERTS * REGION + k * P
                    sp.dma_start(rows_in[r:r + P, :], padding[:, EXPERTS * TILES + k, :]).then_inc(spare_rows, 16)
                sp.wait_ge(spare_rows, 16 * SPARE_TILES)
                pad(sp, range(0, EXPERTS, 2))

            @block.gpsimd
            def _(pool):
                n = 0

                def made(ins):
                    nonlocal n
                    n += 1
                    ins.then_inc(consts, 1)

                made(pool.memset(ones[:, :], 1.0))
                pool.wait_ge(consts, 1)
                made(pool.affine_select(out=upper[:, :], in_=ones[:, :], compare_op=ALU.is_ge, fill=0.0, base=-1,
                                        pattern=[[1, P]], channel_multiplier=-1))
                made(pool.iota(iota8[:, :], [[1, EXPERTS]], base=0, channel_multiplier=0, allow_small_or_imprecise_dtypes=True))
                made(pool.iota(start8[:, :, :], [[0, TILES], [REGION, EXPERTS]], base=0, channel_multiplier=0, allow_small_or_imprecise_dtypes=True))
                for k in range(CHOICES):
                    made(pool.iota(target[:, :, :, k * TILES:(k + 1) * TILES], [[NODES, GRAPHS], [P, TILES]], base=k * TOKENS, channel_multiplier=1))
                made(pool.iota(dump[:, :], [[P, PAD_TILES]], base=CHOICES * TOKENS, channel_multiplier=1))
                made(pool.memset(padding[:, :, 0:D], 0.0))
                made(pool.iota(multiples[:, :, :], [[0, EXPERTS], [SLOT, MOST]], base=0, channel_multiplier=0, allow_small_or_imprecise_dtypes=True))
                made(pool.iota(slot[:, :], [[1, SLOTS]], base=0, channel_multiplier=0, allow_small_or_imprecise_dtypes=True))
                made(pool.memset(carry[0][:, :], 0.0))
                assert n == 11

                def body(at):
                    if g := at(4):
                        pool.wait_ge(payload, count(g, 2))
                        pool.wait_ge(packed, count(g, 2))
                        pool.wait_ge(placed, count(g, 8))
                        pool.wait_ge(relay, count(g, 1, back=2))
                        pool.tensor_tensor(waited[par(g)][:, :], ident[:, 0:1], ident[:, 0:1], ALU.mult).then_inc(relay, 1)
                        for t in range(TILES):
                            for k in range(CHOICES):
                                n = t * CHOICES + k
                                pool.indirect_dma_start(
                                    out=rows_in, out_offset=bass.IndirectOffsetOnAxis(ap=row[par(g)][:, n:n + 1], axis=0),
                                    in_=pay[k][par(g)][:, t, :], in_offset=None).then_inc(scattered[par(g)], 16)
                    if g := at(0):
                        pool.wait_ge(stats, count(g, 4))
                        pool.tensor_tensor(ve[par(g)][:, :], mv[par(g)][:, :, 1], lneps[:, 0:TILES], ALU.add).then_inc(scale, 1)
                        pool.wait_ge(scale, count(g, 2, 1))
                        pool.wait_ge(normed, count(g, 2, back=2))
                        pool.tensor_tensor(rstd[par(g)][:, :], ve[par(g)][:, :], mhalf[:, 0:TILES], ALU.pow).then_inc(scale, 1)

                sweep(pool, 4, body)
                for b in range(2):
                    pool.wait_ge(scattered[b], 16 * 4 * (GRAPHS // 2))

            @block.vector
            def _(dve):
                dve.wait_ge(weights_in, 16 * 5)
                dve.wait_ge(consts, 11)
                dve.tensor_copy(padding[:, :, D:ROW].bitcast(I32), dump[:, :].unsqueeze(2)).then_inc(table, 1)

                def body(at):
                    g0, g3, g4 = at(0), at(3), at(4)
                    if g := at(5):
                        x = graph_rows(X, g)
                        dve.wait_ge(product, count(g, 1))
                        dve.tensor_tensor(tmp[par(g)][:, :], p_y[:, 0:NODES], b2[:, :, :].rearrange("p t d -> p (t d)"), ALU.add).then_inc(added, 1)
                    if g := g4:
                        dve.wait_ge(counted, count(g, 1))
                        dve.tensor_tensor(carry1[par(g)][:, :], carry[par(g)][:, :], p_c[:, 64:64 + EXPERTS], ALU.add).then_inc(placed, 1)
                        dve.tensor_tensor(rank[par(g)][:, :, :].rearrange("p t e -> p (t e)"), p_c[:, 0:TILES * EXPERTS],
                                               start8[:, :, :].rearrange("p t e -> p (t e)"), ALU.add).then_inc(placed, 1)
                    if g := at(5):
                        x = graph_rows(X, g)
                        dve.wait_ge(added, count(g, 2, 1))
                        if g3:
                            dve.wait_ge(logits, count(g3, 1))
                        dve.tensor_tensor(x, x, tmp[par(g)][:, :], ALU.add).then_inc(added, 1)
                    elif g3:
                        dve.wait_ge(logits, count(g3, 1))
                    if g := g3:
                        for t in range(TILES):
                            dve.max(best[par(g)][:, t, :], p_r[:, t * EXPERTS:(t + 1) * EXPERTS]).then_inc(picked, 1)
                    if g := g4:
                        a, b = par(g), 1 - par(g)
                        dve.wait_ge(placed, count(g, 8, 2))
                        dve.tensor_tensor(carry[b][:, :], carry1[a][:, :], p_c[:, 64 + EXPERTS:64 + 2 * EXPERTS], ALU.add).then_inc(placed, 1)
                        dve.tensor_tensor(rank[a][:, 0, :], rank[a][:, 0, :], carry[a][:, :], ALU.add).then_inc(placed, 1)
                        dve.tensor_tensor(rank[a][:, 1, :], rank[a][:, 1, :], carry1[a][:, :], ALU.add).then_inc(placed, 1)
                    if g := g3:
                        dve.wait_ge(picked, count(g, 8, 2))
                        dve.tensor_tensor(gap[par(g)][:, :], best[par(g)][:, :, 0], best[par(g)][:, :, 1], ALU.subtract).then_inc(picked, 1)
                        for t in range(TILES):
                            dve.max_index(besti[par(g)][:, t, :], best[par(g)][:, t, :], p_r[:, t * EXPERTS:(t + 1) * EXPERTS]).then_inc(picked, 1)
                    if g := g4:
                        a = par(g)
                        dve.wait_ge(placed, count(g, 8, 5))
                        dve.tensor_tensor(chosen[a][:, :, :, :], hot[a][:, :, :, :],
                                               rank[a][:, :, :].unsqueeze(2).to_broadcast([P, TILES, CHOICES, EXPERTS]), ALU.mult).then_inc(placed, 1)
                    if g := g3:
                        dve.wait_ge(picked, count(g, 8, 5))
                        dve.tensor_copy(bestf[par(g)][:, :, :], besti[par(g)][:, :, 0:CHOICES]).then_inc(picked, 1)
                    if g := g0:
                        x = graph_rows(X, g)
                        for t in range(TILES):
                            dve.bn_stats(st[par(g)][:, t, :], x[:, t * D:(t + 1) * D]).then_inc(stats, 1)
                    if g := g4:
                        a = par(g)
                        dve.wait_ge(placed, count(g, 8, 6))
                        dve.tensor_reduce(rowf[a][:, :], chosen[a][:, :, :, :].rearrange("p t k e -> p (t k) e"), AX.X, ALU.add).then_inc(placed, 1)
                    if g := g3:
                        dve.wait_ge(picked, count(g, 8, 6))
                        dve.wait_ge(placed, count(g, 8, back=2))
                        dve.tensor_tensor(hot[par(g)][:, :, :, :].rearrange("p t k e -> p (t k) e"),
                                               iota8[:, :].unsqueeze(1).to_broadcast([P, TILES * CHOICES, EXPERTS]),
                                               bestf[par(g)][:, :, :].rearrange("p t k -> p (t k)").unsqueeze(2).to_broadcast([P, TILES * CHOICES, EXPERTS]),
                                               ALU.is_equal).then_inc(picked, 1)
                    if g := g4:
                        a = par(g)
                        dve.wait_ge(placed, count(g, 8, 7))
                        dve.tensor_copy(row[a][:, :], rowf[a][:, :]).then_inc(placed, 1)
                        dve.wait_ge(tanh, count(g, 1))
                        for k, sign in ((0, 0.5), (1, -0.5)):
                            dve.tensor_scalar(one_of(weights, g, slice(k * TILES, k * TILES + TILES)), th[a][:, :], sign, 0.5, ALU.mult, ALU.add).then_inc(weighed, 1)
                    if g := g3:
                        dve.wait_ge(picked, count(g, 8, 7))
                        dve.wait_ge(counted, count(g, 1, back=2))
                        dve.tensor_tensor(both[par(g)][:, :, :], hot[par(g)][:, :, 0, :], hot[par(g)][:, :, 1, :], ALU.add).then_inc(picked, 1)
                        dve.wait_ge(scattered[par(g)], 16 * 4 * pair(g))
                        for k in range(CHOICES):
                            dve.tensor_copy(pay[k][par(g)][:, :, D].bitcast(I32), one_of(target, g, slice(k * TILES, k * TILES + TILES))).then_inc(packed, 1)
                    if g := g0:
                        dve.wait_ge(stats, count(g, 4, TILES))
                    if g := at(1):
                        x = graph_rows(X, g)
                        dve.wait_ge(scale, count(g, 2))
                        dve.wait_ge(x_turned, count(g, 1, back=2))
                        dve.wait_ge(payload, count(g, 2, back=2))
                        for t in range(TILES):
                            dve.tensor_scalar(xn[par(g)][:, t, :], x[:, t * D:(t + 1) * D], mv[par(g)][:, t, 0:1],
                                                        rstd[par(g)][:, t:t + 1], ALU.subtract, ALU.mult).then_inc(normed, 1)
                    if g := g0:
                        for t in range(TILES):
                            dve.bn_aggr(mv[par(g)][:, t, :], st[par(g)][:, t, :]).then_inc(stats, 1)

                sweep(dve, 5, body)

                n = 1

                def step(ins):
                    nonlocal n
                    ins.then_inc(table, 1)
                    n += 1
                    dve.wait_ge(table, n)

                taken = carry[0]
                dve.wait_ge(placed, count(graph(GRAPHS - 1), 8))
                step(dve.tensor_tensor(lastf[:, :], taken[0:1, :], start8[0:1, 0, :], ALU.add))
                step(dve.tensor_copy(last[:, :], lastf[:, :]))
                step(dve.tensor_tensor(over[:, :, :], taken[0:1, :].unsqueeze(2).to_broadcast([1, EXPERTS, MOST]), multiples[:, :, :], ALU.is_gt))
                step(dve.tensor_reduce(taken_slots[:, :], over[:, :, :], AX.X, ALU.add))
                step(dve.tensor_copy(end[:, :], taken_slots[:, :]))
                for e in range(1, EXPERTS):
                    step(dve.tensor_tensor(end[:, e:e + 1], end[:, e - 1:e], taken_slots[:, e:e + 1], ALU.add))
                step(dve.tensor_scalar(skip[:, :], taken_slots[:, :], -float(SLOT), float(REGION), ALU.mult, ALU.add))
                step(dve.tensor_scalar(rowsf[:, :], slot[:, :], float(SLOT), None, ALU.mult))
                wide = [1, SLOTS, EXPERTS]
                step(dve.tensor_tensor(past[:, :, :], slot[:, :].unsqueeze(2).to_broadcast(wide), end[:, :].unsqueeze(1).to_broadcast(wide), ALU.is_ge))
                step(dve.tensor_reduce(slotf[:, :], past[:, :, 0:EXPERTS - 1], AX.X, ALU.add))
                step(dve.tensor_tensor(past[:, :, :], past[:, :, :], skip[:, :].unsqueeze(1).to_broadcast(wide), ALU.mult))
                step(dve.tensor_reduce(skipped[:, :], past[:, :, :], AX.X, ALU.add))
                step(dve.tensor_tensor(rowsf[:, :], rowsf[:, :], skipped[:, :], ALU.add))
                step(dve.tensor_copy(slot_row[:, :, :].rearrange("a j b -> a (j b)"), rowsf[:, :]))
                step(dve.tensor_copy(slot_e[:, :, :].rearrange("a j b -> a (j b)"), slotf[:, :]))

            @block.scalar
            def _(act):
                act.wait_ge(weights_in, 16 * 5)

                def body(at):
                    if g := at(2):
                        act.wait_ge(x_turned, count(g, 1))
                        act.wait_ge(hidden, count(g, 2, back=2))
                        act.wait_ge(logits, count(g, 1, back=2))
                        act.copy(xT[par(g)][:, :], p_x[:, 0:NODES]).then_inc(x_sb, 1)
                    if g := at(3):
                        act.wait_ge(scattered[par(g)], 16 * 4 * pair(g))
                        for k in range(CHOICES):
                            act.copy(pay[k][par(g)][:, :, 0:D], xn[par(g)][:, :, :]).then_inc(payload, 1)
                        act.wait_ge(product, count(g, 1, back=2))
                        for f in range(4):
                            act.wait_ge(hidden, count(g, 2, f // 2 + 1))
                            act.activation(hT[par(g)][:, f, :], p_h[f // 2][:, (f % 2) * NODES:(f % 2 + 1) * NODES], ACT.Gelu, bias=b1[:, f:f + 1]).then_inc(gelu, 1)
                        act.wait_ge(picked, count(g, 8, 3))
                        act.wait_ge(weighed, count(g, 2, back=2))
                        act.activation(th[par(g)][:, :], gap[par(g)][:, :], ACT.Tanh, scale=0.5).then_inc(tanh, 1)

                sweep(act, 3, body)
                pad(act, range(1, EXPERTS, 2))

            @block.tensor
            def _(pe):
                pe.wait_ge(weights_in, 16 * 5)
                pe.wait_ge(consts, 11)

                def body(at):
                    if g := at(4):
                        pe.wait_ge(picked, count(g, 8))
                        pe.wait_ge(placed, count(g, 8, 3, back=1))
                        m = both[par(g)][:, :, :].rearrange("p t e -> p (t e)")
                        nc.tensor.matmul(p_c[:, 0:TILES * EXPERTS], upper[:, :], m, start=True, stop=True)
                        nc.tensor.matmul(p_c[:, 64:64 + TILES * EXPERTS], ones[:, :], m, start=True, stop=True).then_inc(counted, 1)
                    if g := at(2):
                        pe.wait_ge(normed, count(g, 2))
                        pe.wait_ge(x_sb, count(g, 1, back=1))
                        for t in range(TILES):
                            mm = transpose(nc, p_x[:, t * P:(t + 1) * P], xn[par(g)][:, t, :], ident[:, :])
                        mm.then_inc(x_turned, 1)
                    if g := at(3):
                        pe.wait_ge(x_sb, count(g, 1))
                        pe.wait_ge(picked, count(g, 8, 5, back=1))
                        for t in range(TILES):
                            mm = nc.tensor.matmul(p_r[:, t * EXPERTS:(t + 1) * EXPERTS], xT[par(g)][:, t * P:(t + 1) * P], router[:, :], start=True, stop=True)
                        mm.then_inc(logits, 1)
                    if g := at(4):
                        pe.wait_ge(gelu, count(g, 4))
                        pe.wait_ge(added, count(g, 2, 1, back=1))
                        for t in range(TILES):
                            for f in range(4):
                                mm = nc.tensor.matmul(p_y[:, t * D:(t + 1) * D], hT[par(g)][:, f, t * P:(t + 1) * P], W2[:, f, :],
                                                      start=(f == 0), stop=(f == 3))
                        mm.then_inc(product, 1)
                    if g := at(3):
                        for k in range(2):
                            pe.wait_ge(gelu, count(g, 4, 2 * k + 2, back=1))
                            for f in (2 * k, 2 * k + 1):
                                mm = nc.tensor.matmul(p_h[k][:, (f % 2) * NODES:(f % 2 + 1) * NODES], W1[:, f * P:(f + 1) * P], xT[par(g)][:, :],
                                                      start=True, stop=True)
                            mm.then_inc(hidden, 1)

                sweep(pe, 4, body)


def one_of(table, g, n):
    n = n if isinstance(n, slice) else slice(n, n + 1)
    return one(table[:, bass.ds(pair(g), 1), par(g), n])


def experts(nc, outer, ident, slot_e, slot_row, rows_in, rows_out, expert_weights, weights_in):
    with ExitStack() as ctx:
        def sb(name, shape, dt=F32):
            return ctx.enter_context(nc.sbuf_tensor(name, shape, dt))

        def two(name, shape, dt=F32):
            return [sb(name + "0", shape, dt), sb(name + "1", shape, dt)]

        def bank(name):
            return ctx.enter_context(nc.psum_tensor(name, [P, 512], F32))

        def sem(name):
            return outer.enter_context(nc.semaphore(name))

        W1, b1, W2, b2 = expert_weights
        xg = two("e_xg", [P, TILES, ROW])
        xT = two("e_xT", [P, NODES])
        W1_here = two("e_W1_here", [P, FF])
        hT = two("e_hT", [P, 4, NODES])
        y = two("e_y", [P, TILES, D])
        to0 = two("e_to0", [P, TILES], I32)
        to1 = two("e_to1", [P, TILES], I32)
        to2 = two("e_to2", [P, TILES], I32)
        waited = two("e_waited", [P, 1])
        p_x = bank("e_px")
        p_h = [[bank(f"e_ph{q}{k}") for k in range(2)] for q in range(2)]
        p_y = [bank("e_py0"), bank("e_py1")]

        rows_here = [sem("e_rows_here0"), sem("e_rows_here1")]
        scattered = [sem("e_scattered0"), sem("e_scattered1")]
        relay = sem("e_relay")
        x_turned = sem("e_x_turned")
        x_sb = sem("e_x_sb")
        W1_ready = sem("e_W1_ready")
        hidden = sem("e_hidden")
        gelu = sem("e_gelu")
        product = sem("e_product")
        result = sem("e_result")
        kept = sem("e_kept")
        moved = sem("e_moved")
        aimed = sem("e_aimed")

        def expert(eng, s):
            return eng.value_load(one(slot_e[0:1, bass.ds(pair(s), 1), par(s):par(s) + 1]), min_val=0, max_val=EXPERTS - 1)

        with nc.Block() as block:
            @block.sync
            def _(sp):
                def body(at):
                    if s := at(0):
                        sp.wait_ge(kept, count(s, 1, back=2))
                        sp.wait_ge(x_turned, count(s, 1, back=2))
                        r = sp.value_load(one(slot_row[0:1, bass.ds(pair(s), 1), par(s):par(s) + 1]), min_val=0, max_val=ROWS - SLOT)
                        sp.dma_start(xg[par(s)][:, :, :], rows_in[bass.ds(r, SLOT), :].rearrange("(t p) d -> p t d", p=P)).then_inc(rows_here[par(s)], 16)

                sweep(sp, 0, body, SLOTS)

            @block.vector
            def _(dve):
                dve.wait_ge(weights_in, 64)

                def body(at):
                    if s := at(5):
                        dve.wait_ge(scattered[par(s)], 16 * TILES * pair(s))
                        dve.wait_ge(moved, count(s, 1))
                        dve.tensor_copy(to2[par(s)][:, :], to1[par(s)][:, :]).then_inc(aimed, 1)
                        e = expert(dve, s)
                        dve.wait_ge(product, count(s, 1))
                        dve.tensor_tensor(y[par(s)][:, :, :].rearrange("p t d -> p (t d)"), p_y[par(s)][:, 0:TILES * D], one(b2[:, bass.ds(e, 1), :]), ALU.add).then_inc(result, 1)
                    if s := at(1):
                        e = expert(dve, s)
                        dve.wait_ge(hidden, count(s, 2, back=2))
                        dve.tensor_copy(W1_here[par(s)][:, :], one(W1[:, bass.ds(e, 1), :])).then_inc(W1_ready, 1)
                        dve.wait_ge(x_turned, count(s, 1))
                        dve.tensor_copy(xT[par(s)][:, :], p_x[:, 0:NODES]).then_inc(x_sb, 1)
                    if s := at(3):
                        dve.wait_ge(aimed, count(s, 1, back=2))
                        dve.wait_ge(kept, count(s, 1))
                        dve.tensor_copy(to1[par(s)][:, :], to0[par(s)][:, :]).then_inc(moved, 1)
                    if s := at(1):
                        dve.wait_ge(rows_here[par(s)], loads(s))
                        dve.wait_ge(moved, count(s, 1, back=2))
                        dve.tensor_copy(to0[par(s)][:, :], xg[par(s)][:, :, D].bitcast(I32)).then_inc(kept, 1)

                sweep(dve, 5, body, SLOTS)

            @block.gpsimd
            def _(pool):
                def body(at):
                    if s := at(5):
                        pool.wait_ge(aimed, count(s, 1))
                        pool.wait_ge(result, count(s, 1))
                        pool.wait_ge(relay, count(s, 1, back=2))
                        pool.tensor_tensor(waited[par(s)][:, :], ident[:, 0:1], ident[:, 0:1], ALU.mult).then_inc(relay, 1)
                        for t in range(TILES):
                            pool.indirect_dma_start(out=rows_out, out_offset=bass.IndirectOffsetOnAxis(ap=to2[par(s)][:, t:t + 1], axis=0),
                                                                    in_=y[par(s)][:, t, :], in_offset=None).then_inc(scattered[par(s)], 16)

                sweep(pool, 5, body, SLOTS)
                for b in range(2):
                    pool.wait_ge(scattered[b], 16 * TILES * (SLOTS // 2))

            @block.scalar
            def _(act):
                act.wait_ge(weights_in, 64)

                def body(at):
                    if s := at(3):
                        e = expert(act, s)
                        act.wait_ge(product, count(s, 1, back=2))
                        for f in range(4):
                            if f % 2 == 0:
                                act.wait_ge(hidden, count(s, 2, f // 2 + 1))
                            act.activation(hT[par(s)][:, f, :], p_h[par(s)][f // 2][:, (f % 2) * NODES:(f % 2 + 1) * NODES], ACT.Gelu,
                                           bias=b1[:, bass.ds(e, 1), f]).then_inc(gelu, 1)

                sweep(act, 3, body, SLOTS)

            @block.tensor
            def _(pe):
                pe.wait_ge(weights_in, 64)

                def body(at):
                    if s := at(1):
                        pe.wait_ge(rows_here[par(s)], loads(s))
                        pe.wait_ge(x_sb, count(s, 1, back=1))
                        for t in range(TILES):
                            mm = transpose(nc, p_x[:, t * P:(t + 1) * P], xg[par(s)][:, t, 0:D], ident[:, :])
                        mm.then_inc(x_turned, 1)
                    if s := at(4):
                        pe.wait_ge(gelu, count(s, 4))
                        pe.wait_ge(result, count(s, 1, back=2))
                        e = expert(pe, s)
                        for t in range(TILES):
                            for f in range(4):
                                mm = nc.tensor.matmul(p_y[par(s)][:, t * D:(t + 1) * D], hT[par(s)][:, f, t * P:(t + 1) * P],
                                                      one(W2[:, bass.ds(e, 1), f * D:(f + 1) * D]), start=(f == 0), stop=(f == 3))
                        mm.then_inc(product, 1)
                    if s := at(2):
                        pe.wait_ge(x_sb, count(s, 1))
                        pe.wait_ge(W1_ready, count(s, 1))
                        pe.wait_ge(gelu, count(s, 4, back=2))
                        for f in range(4):
                            mm = nc.tensor.matmul(p_h[par(s)][f // 2][:, (f % 2) * NODES:(f % 2 + 1) * NODES], W1_here[par(s)][:, f * P:(f + 1) * P],
                                                  xT[par(s)][:, :], start=True, stop=True)
                            if f % 2:
                                mm.then_inc(hidden, 1)

                sweep(pe, 4, body, SLOTS)


UNIT = 4 * TILES
UNITS = GRAPHS // 4


def combine(nc, outer, X, weights, rows_out, out):
    with ExitStack() as ctx:
        def sb(name, shape, dt=F32):
            return ctx.enter_context(nc.sbuf_tensor(name, shape, dt))

        def sem(name):
            return outer.enter_context(nc.semaphore(name))

        y = [[sb(f"f_y{k}{b}", [P, UNIT, D]) for b in range(2)] for k in range(CHOICES)]
        y_in = [sem("f_y_in0"), sem("f_y_in1")]
        weighted = sem("f_weighted")
        added = sem("f_added")
        stored = sem("f_stored")
        yt = rows_out[0:CHOICES * TOKENS, :].rearrange("(k j v t p) d -> k j v p t d", k=CHOICES, v=2, t=UNIT, p=P)
        ot = out.rearrange("g n d -> (g n) d").rearrange("(j v t p) d -> j v p t d", v=2, t=UNIT, p=P)
        Xu = X[:, :, :, :].rearrange("p (j v w) b (t d) -> p j v (w b t) d", v=2, w=2, t=TILES)
        Wu = weights[:, :, :, :].rearrange("p (j v w) b (k t) -> p j v (w b) k t", v=2, w=2, t=TILES)

        def weight(g, k, t):
            return Wu[:, bass.ds(pair(g), 1), par(g), t // TILES, k, t % TILES:t % TILES + 1].rearrange("p a d -> p (a d)")

        with nc.Block() as block:
            @block.sync
            def _(sp):
                def body(at):
                    if g := at(0):
                        sp.wait_ge(added, count(g, UNIT + 1, back=2))
                        for k in range(CHOICES):
                            sp.dma_start(y[k][par(g)][:, :, :], yt[k, bass.ds(pair(g), 1), par(g)].rearrange("a p t d -> (a p) t d")).then_inc(y_in[par(g)], 16)

                sweep(sp, 0, body, UNITS)

            @block.vector
            def _(dve):
                def body(at):
                    if g := at(0):
                        dve.wait_ge(y_in[par(g)], 32 * pair(g) + 32)
                        for t in range(UNIT):
                            x = Xu[:, bass.ds(pair(g), 1), par(g), t, :].rearrange("p a d -> p (a d)")
                            dve.scalar_tensor_tensor(out=x, in0=y[0][par(g)][:, t, :], scalar=weight(g, 0, t), in1=x,
                                                              op0=ALU.mult, op1=ALU.add).then_inc(added, 1)
                        dve.wait_ge(weighted, count(g, 1))
                        dve.wait_ge(added, count(g, UNIT + 1, UNIT))
                        x = Xu[:, bass.ds(pair(g), 1), par(g)].rearrange("p a t d -> p (a t d)")
                        dve.tensor_tensor(x, x, y[1][par(g)][:, :, :].rearrange("p t d -> p (t d)"), ALU.add).then_inc(added, 1)

                sweep(dve, 0, body, UNITS)

            @block.scalar
            def _(act):
                def body(at):
                    if g := at(0):
                        act.wait_ge(y_in[par(g)], 32 * pair(g) + 32)
                        for t in range(UNIT):
                            mul = act.activation(y[1][par(g)][:, t, :], y[1][par(g)][:, t, :], ACT.Copy, scale=weight(g, 1, t))
                        mul.then_inc(weighted, 1)
                    if g := at(1):
                        act.wait_ge(added, count(g, UNIT + 1))
                        act.dma_start(ot[bass.ds(pair(g), 1), par(g)].rearrange("a p t d -> (a p) t d"),
                                      Xu[:, bass.ds(pair(g), 1), par(g)].rearrange("p a t d -> p (a t) d")).then_inc(stored, 16)

                sweep(act, 1, body, UNITS)
                act.wait_ge(stored, 16 * (UNITS))


def setup(nc, outer, X, x_rest_in, gnn0_weights, gnn0_weights_in, ident, mhalf, lneps, rmseps, epsi, WC, WS, biases, ids, d):
    with ExitStack() as ctx:
        def sb(name, shape, dt=F32):
            return ctx.enter_context(nc.sbuf_tensor(name, shape, dt))

        def sem(name):
            return outer.enter_context(nc.semaphore(name))

        eps = sb("s_eps", [P, 1])
        idi = sb("s_idi", [1, 64], I32)
        idf = sb("s_idf", [1, 64])
        ok = sb("s_ok", [1, 64])
        bs = sb("s_bs", [P, 4])
        x_in, small_in, ident_ready, steps = (sem(n) for n in ("s_x_in", "s_small_in", "s_ident", "s_steps"))

        with nc.Block() as block:
            @block.sync
            def _(sp):
                xt = d["x"].rearrange("g (t p) d -> p (g t) d", p=P)
                xs = X[:, :, :, :].rearrange("p j b (t d) -> p (j b t) d", d=D)
                sp.dma_start(xs[:, 0:8, :], xt[:, 0:8, :]).then_inc(x_in, 16)
                sp.dma_start(WS[:, :, :], d["WsT"]).then_inc(small_in, 16)
                sp.dma_start(eps[:, :], d["a_eps"].partition_broadcast(P)).then_inc(small_in, 16)
                sp.dma_start(idi[:, :], d["route"]).then_inc(small_in, 16)
                sp.dma_start(bs[:, :], d["bsT"]).then_inc(small_in, 16)
                sp.dma_start(biases[:, 0:EXPERTS0, :], d["brT"]).then_inc(small_in, 16)
                for k in range(8, 64, 8):
                    sp.dma_start(xs[:, k:k + 8, :], xt[:, k:k + 8, :]).then_inc(x_rest_in, 16)
                sp.wait_ge(x_in, 16)

            @block.scalar
            def _(act):
                load_gnn0(act, gnn0_weights, gnn0_weights_in, d)

            @block.gpsimd
            def _(pool):
                pool.memset(ident[:, :], 0.0).then_inc(ident_ready, 1)
                pool.wait_ge(ident_ready, 1)
                pool.affine_select(out=ident[:, :], in_=ident[:, :], compare_op=ALU.not_equal, fill=1.0, base=0,
                                   pattern=[[-1, P]], channel_multiplier=1).then_inc(ident_ready, 1)
                pool.memset(mhalf[:, :], -0.5).then_inc(ident_ready, 1)
                pool.memset(lneps[:, :], LN_EPS).then_inc(ident_ready, 1)
                pool.memset(rmseps[:, :], 512 * RMS_EPS).then_inc(ident_ready, 1)

            @block.vector
            def _(dve):
                n = 0

                def step(ins):
                    nonlocal n
                    ins.then_inc(steps, 1)
                    n += 1
                    dve.wait_ge(steps, n)

                dve.wait_ge(small_in, 16 * 5)
                dve.wait_ge(ident_ready, 2)
                step(dve.tensor_scalar(epsi[:, :], ident[:, :], eps[:, 0:1], None, ALU.mult))
                for l in range(2):
                    for k in range(2):
                        w = WS[:, l, k * HID + k * P:k * HID + (k + 1) * P]
                        step(dve.tensor_tensor(w, w, ident[:, :], ALU.add))
                for l in range(2):
                    step(dve.tensor_copy(WC[:, l, EXPERTS0, :], WS[:, l, :]))
                step(dve.tensor_copy(biases[:, EXPERTS0, :], bs[:, :]))
                step(dve.tensor_tensor(biases[:, 0:EXPERTS0, :], biases[:, 0:EXPERTS0, :], bs[:, :].unsqueeze(1).to_broadcast([P, EXPERTS0, 4]), ALU.add))
                step(dve.tensor_copy(idf[:, :], idi[:, :]))
                step(dve.tensor_scalar(ok[:, :], idf[:, :], 0.0, None, ALU.is_ge))
                step(dve.tensor_scalar(idf[:, :], idf[:, :], float(EXPERTS0), -float(EXPERTS0), ALU.min, ALU.add))
                step(dve.tensor_tensor(idf[:, :], idf[:, :], ok[:, :], ALU.mult))
                step(dve.tensor_scalar(idf[:, :], idf[:, :], float(EXPERTS0), None, ALU.add))
                step(dve.tensor_copy(ids[:, :, :].rearrange("a j b -> a (j b)"), idf[:, :]))


def program(nc, d, out):
    with ExitStack() as outer:
        sb = lambda name, shape, dt=F32: outer.enter_context(nc.sbuf_tensor(name, shape, dt))
        X = sb("X", [P, GRAPHS // 2, 2, TILES * D])
        ident = sb("ident", [P, P])
        mhalf = sb("mhalf", [P, 4])
        lneps = sb("lneps", [P, 4])
        rmseps = sb("rmseps", [P, 4])
        ids = sb("ids", [1, GRAPHS // 2, 4], I32)
        sem = lambda name: outer.enter_context(nc.semaphore(name))
        x_rest_in, gnn0_in, ffn0_in, gnn1_in, route_in = (sem(n) for n in ("x_rest_in", "a_weights_in", "b_weights_in", "w_in", "d_in"))
        gnn1_raw = [sb("w_" + name, shape) for name, shape in
                    (("fc_w", [P, HEADS, D]), ("fp_w", [P, HEADS, D]), ("fc_b", [P, HEADS]), ("qk_w", [P, 2]), ("q_b", [1, 1]), ("k_b", [1, 1]),
                     ("fp_b", [P, TILES, D]))]
        route_weights = [sb("d_" + name, shape) for name, shape in
                         (("router", [P, EXPERTS]), ("W1", [P, FF]), ("b1", [P, 4]), ("W2", [P, 4, D]), ("b2", [P, TILES, D]))]
        with ExitStack() as ab:
            sb2 = lambda name, shape: ab.enter_context(nc.sbuf_tensor(name, shape, F32))
            epsi = sb2("epsi", [P, P])
            WC = sb2("WC", [P, 2, EXPERTS0 + 1, 2 * HID])
            WS = sb2("WS", [P, 2, 2 * HID])
            biases = sb2("biases", [P, EXPERTS0 + 1, 4])
            gnn0_weights = [sb2("a_" + name, shape) for name, shape in
                            (("W1", [P, 512]), ("W2", [P, 4, D]), ("b1", [P, 512]), ("rmsw", [P, 512]), ("b2", [P, 2, D]))]
            ffn0_weights = [sb2("b_" + name, shape) for name, shape in
                            (("Wi", [P, HID]), ("bi", [P, 2]), ("Wo", [P, 2, D]), ("bo", [P, 2, D]))]
            setup(nc, outer, X, x_rest_in, gnn0_weights, gnn0_in, ident, mhalf, lneps, rmseps, epsi, WC, WS, biases, ids, d)
            gnn0(nc, outer, X, x_rest_in, ident, mhalf, lneps, rmseps, epsi, WC, WS, gnn0_weights, gnn0_in, ffn0_weights, ffn0_in, d)
            ffn0(nc, outer, X, ident, mhalf, lneps, WC, biases, ids, ffn0_weights, ffn0_in, gnn1_raw, gnn1_in, d)
        gnn1(nc, outer, X, ident, mhalf, lneps, gnn1_raw, gnn1_in, route_weights, route_in, d)
        weights = sb("weights", [P, GRAPHS // 2, 2, CHOICES * TILES])
        slot_e = sb("slot_e", [1, SLOTS // 2, 2], I32)
        slot_row = sb("slot_row", [1, SLOTS // 2, 2], I32)
        rows_in = nc.dram_tensor("rows_in", (ROWS, ROW), F32).ap()
        rows_out = nc.dram_tensor("rows_out", (CHOICES * TOKENS + PAD_TILES * P, D), F32).ap()
        with ExitStack() as de:
            expert_weights = [de.enter_context(nc.sbuf_tensor(name, [P, EXPERTS, width], F32))
                              for name, width in (("e_W1", FF), ("e_b1", 4), ("e_W2", 4 * D), ("e_b2", TILES * D))]
            expert_weights_in = outer.enter_context(nc.semaphore("e_weights_in"))
            route(nc, outer, X, ident, mhalf, lneps, weights, slot_e, slot_row, rows_in, route_weights, route_in, expert_weights, expert_weights_in, d)
            experts(nc, outer, ident, slot_e, slot_row, rows_in, rows_out, expert_weights, expert_weights_in)
        combine(nc, outer, X, weights, rows_out, out)


def kernel(**inputs):
    import numpy as np
    import concourse.bacc as bacc
    from concourse.bass_utils import run_bass_kernel_spmd as run

    v = {k: np.asarray(a) for k, a in inputs.items()}
    c = np.ascontiguousarray
    half = lambda w: w.reshape(*w.shape[:-1], 2, P)
    arrays = {
        "x": v["x"],
        "adj": v["adj"],
        "adjT": c(v["adj"].transpose(0, 2, 1).reshape(GRAPHS, TILES, P, NODES).transpose(0, 2, 1, 3)),
        "a_eps": v["L0_gnn_epsilon"].reshape(1),
        "a_W1": v["L0_gnn_W1"], "a_W2": v["L0_gnn_W2"], "a_b1": v["L0_gnn_b1"], "a_rmsw": v["L0_gnn_rms_weight"],
        "a_b2x2": c(np.stack([v["L0_gnn_b2"]] * 2)),
        "route": v["L0_ffn_route_id"].reshape(1, 64),
        "b_WiT": c(v["L0_ffn_Wi"].T), "b_bi": c(v["L0_ffn_bi"].reshape(2, P).T),
        "WrT": c(half(v["L0_ffn_Wr"]).transpose(4, 0, 1, 3, 2).reshape(P, 2, EXPERTS0, 2 * HID)),
        "WsT": c(half(v["L0_ffn_Ws"][:, 0]).transpose(3, 0, 2, 1).reshape(P, 2, 2 * HID)),
        "brT": c(half(v["L0_ffn_br"]).transpose(3, 1, 0, 2).reshape(P, EXPERTS0, 4)),
        "bsT": c(half(v["L0_ffn_bs"][:, 0]).transpose(2, 0, 1).reshape(P, 4)),
        "b_WoT": c(v["L0_ffn_Wo"].T), "b_box2": c(np.stack([v["L0_ffn_bo"]] * 2)),
        "c_fc_wT": c(v["L1_gnn_fc_w"].reshape(D, HEADS, D).transpose(2, 1, 0)), "c_fp_w": v["L1_gnn_fp_w"],
        "c_fc_bT": c(v["L1_gnn_fc_b"].reshape(HEADS, D).T), "c_qk_w": c(np.concatenate([v["L1_gnn_q_w"], v["L1_gnn_k_w"]], 1)),
        "d_router": v["L1_ffn_Wr"], "d_W1s": v["L1_ffn_W1s"], "d_W2s": v["L1_ffn_W2s"],
        "d_b1sT": c(v["L1_ffn_b1s"].reshape(4, P).T), "d_b2sx2": c(np.stack([v["L1_ffn_b2s"]] * 2)),
        "e_W1": v["L1_ffn_W1p"], "e_W2": v["L1_ffn_W2p"], "e_b1T": c(v["L1_ffn_b1p"].reshape(EXPERTS, 4, P).transpose(2, 0, 1)), "e_b2x2": c(np.stack([v["L1_ffn_b2p"]] * 2, 1).reshape(EXPERTS, TILES * D)),
        "c_q_b": v["L1_gnn_q_b"], "c_k_b": v["L1_gnn_k_b"], "c_fp_bx2": c(np.stack([v["L1_gnn_fp_b"]] * 2)),
    }
    nc = bacc.Bacc("TRN2", target_bir_lowering=False, num_devices=1)
    d = {k: nc.dram_tensor("in_" + k, a.shape, mybir.dt.from_np(a.dtype), kind="ExternalInput").ap() for k, a in arrays.items()}
    out = nc.dram_tensor("out", (GRAPHS, NODES, D), F32, kind="ExternalOutput").ap()
    program(nc, d, out)
    r = run(nc, [{"in_" + k: c(a) for k, a in arrays.items()}], core_ids=[0])
    return r.results[0]["out"]
```
